# Optimizing a Trainium2 kernel written in Bass

```python
import numpy as np
import jax
import jax.numpy as jnp

def _softmax(x, axis=-1):
    return jax.nn.softmax(x, axis=axis)

def _gelu(x):
    return jax.nn.gelu(x, approximate=True)

def _silu(x):
    return jax.nn.silu(x)

def _sigmoid(x):
    return jax.nn.sigmoid(x)

def _layernorm(x, axis=-1, eps=1e-05):
    m = jnp.mean(x, axis=axis, keepdims=True)
    v = jnp.var(x, axis=axis, keepdims=True)
    return (x - m) / jnp.sqrt(v + eps)

def _scatter_add(tgt, idx, src, axis=0):
    return tgt.at[idx].add(src)

def _segment_sum(src, seg, n):
    return jax.ops.segment_sum(src, seg, n)
kernel_name = 'mk_gnn_resnorm_d2_gnn_r64_b9f274'

def setup_inputs(seed: int=0):
    np.random.seed(seed)
    _w = jnp.asarray

    def _rec_inputs():
        import jax
        import jax.numpy as jnp
        _gk = jax.random.key(seed)
        x = -0.0003713 + 1 * jax.random.normal(jax.random.fold_in(_gk, 1), (100000, 128), jnp.float32)
        src = jax.random.randint(jax.random.fold_in(_gk, 2), (25000,), 0, 100000, jnp.int32)
        dst = jax.random.randint(jax.random.fold_in(_gk, 3), (25000,), 0, 100000, jnp.int32)
        _o = jnp.argsort(dst, stable=True)
        src = src[_o]
        dst = dst[_o]
        edge_attr_3 = -3.57403e-05 + 0.999761 * jax.random.normal(jax.random.fold_in(_gk, 12), (25000, 3), jnp.float32)
        return (x, src, dst, edge_attr_3)
    x, src, dst, edge_attr_3 = _rec_inputs()

    def _L0_gnn_setup():
        import jax, jax.numpy as jnp
        import numpy as np
        N_NODES = 100000
        N_EDGES = 25000
        IN_FEAT = 128
        INTER = 128
        OUT_FEAT = 128
        key = jax.random.key(seed)
        k_h, k_w, k_s, k_d, k_w1, k_w2 = jax.random.split(key, 6)
        h = jax.random.normal(k_h, (N_NODES, IN_FEAT), dtype=jnp.float32)
        w = jax.random.normal(k_w, (N_EDGES, 3), dtype=jnp.float32)
        src = jax.random.randint(k_s, (N_EDGES,), 0, N_NODES, dtype=jnp.int32)
        dst = jax.random.randint(k_d, (N_EDGES,), 0, N_NODES, dtype=jnp.int32)
        W1 = jax.random.normal(k_w1, (INTER, IN_FEAT + 3), dtype=jnp.float32) * jnp.sqrt(2.0 / (INTER + IN_FEAT + 3))
        b1 = jnp.zeros((INTER,), dtype=jnp.float32)
        W2 = jax.random.normal(k_w2, (OUT_FEAT, IN_FEAT + INTER), dtype=jnp.float32) * jnp.sqrt(2.0 / (OUT_FEAT + IN_FEAT + INTER))
        return {'h': h, 'w': w, 'src': src, 'dst': dst, 'W1': W1, 'b1': b1, 'W2': W2}
    _L0_gnn_all = _L0_gnn_setup()
    _L0_gnn_in = {k: v for k, v in _L0_gnn_all.items() if k in ('W1', 'b1', 'W2')}
    del _L0_gnn_all

    def _L1_gnn_setup():
        import jax, jax.numpy as jnp
        import numpy as np
        N_NODES = 50000
        N_EDGES = 10000
        D = 128
        L = 3

        def _transformer_conv(x, src, dst, Wq, bq, Wk, bk, Wv, bv, Ws, bs):
            n = x.shape[0]
            d = Wq.shape[1]
            q = x @ Wq + bq
            k = x @ Wk + bk
            v = x @ Wv + bv
            skip = x @ Ws + bs
            logits = jnp.sum(q[dst] * k[src], axis=-1) * (1.0 / jnp.sqrt(jnp.asarray(d, x.dtype)))
            m = jax.ops.segment_max(logits, dst, num_segments=n)
            e = jnp.exp(logits - m[dst])
            z = jax.ops.segment_sum(e, dst, num_segments=n)
            alpha = e / jnp.maximum(z[dst], 1e-16)
            agg = jax.ops.segment_sum(alpha[:, None] * v[src], dst, num_segments=n)
            return agg + skip
        key = jax.random.key(seed)
        ks = jax.random.split(key, 10)
        s = 1.0 / np.sqrt(D)
        inp = {'x': jax.random.normal(ks[0], (N_NODES, D), dtype=jnp.float32), 'edge_index': jax.random.randint(ks[1], (2, N_EDGES), 0, N_NODES, dtype=jnp.int32), 'Wq': jax.random.normal(ks[2], (L, D, D), dtype=jnp.float32) * s, 'bq': jax.random.normal(ks[3], (L, D), dtype=jnp.float32) * 0.02, 'Wk': jax.random.normal(ks[4], (L, D, D), dtype=jnp.float32) * s, 'bk': jax.random.normal(ks[5], (L, D), dtype=jnp.float32) * 0.02, 'Wv': jax.random.normal(ks[6], (L, D, D), dtype=jnp.float32) * s, 'bv': jax.random.normal(ks[7], (L, D), dtype=jnp.float32) * 0.02, 'Ws': jax.random.normal(ks[8], (L, D, D), dtype=jnp.float32) * s, 'bs': jax.random.normal(ks[9], (L, D), dtype=jnp.float32) * 0.02}
        return inp
    _L1_gnn_all = _L1_gnn_setup()
    _L1_gnn_in = {k: v for k, v in _L1_gnn_all.items() if k in ('Wq', 'bq', 'Wk', 'bk', 'Wv', 'bv', 'Ws', 'bs')}
    del _L1_gnn_all
    return {'x': x, 'src': src, 'dst': dst, 'edge_attr_3': edge_attr_3, 'L0_gnn_W1': _L0_gnn_in['W1'], 'L0_gnn_b1': _L0_gnn_in['b1'], 'L0_gnn_W2': _L0_gnn_in['W2'], 'L1_gnn_Wq': _L1_gnn_in['Wq'], 'L1_gnn_bq': _L1_gnn_in['bq'], 'L1_gnn_Wk': _L1_gnn_in['Wk'], 'L1_gnn_bk': _L1_gnn_in['bk'], 'L1_gnn_Wv': _L1_gnn_in['Wv'], 'L1_gnn_bv': _L1_gnn_in['bv'], 'L1_gnn_Ws': _L1_gnn_in['Ws'], 'L1_gnn_bs': _L1_gnn_in['bs']}

def reference(x, src, dst, edge_attr_3, L0_gnn_W1, L0_gnn_b1, L0_gnn_W2, L1_gnn_Wq, L1_gnn_bq, L1_gnn_Wk, L1_gnn_bk, L1_gnn_Wv, L1_gnn_bv, L1_gnn_Ws, L1_gnn_bs):
    import jax
    import jax.numpy as jnp

    def _L0_gnn_ref(h, w, src, dst, W1, b1, W2):
        import jax, jax.numpy as jnp
        import numpy as np
        N_NODES = 100000
        N_EDGES = 25000
        IN_FEAT = 128
        INTER = 128
        OUT_FEAT = 128
        m = jnp.concatenate([h[src], w], axis=1)
        tmp = jax.nn.relu(m @ W1.T + b1)
        h_N = jax.ops.segment_sum(tmp, dst, num_segments=N_NODES)
        h_total = jnp.concatenate([h, h_N], axis=1)
        return jax.nn.relu(h_total @ W2.T)

    def _L1_gnn_ref(x, edge_index, Wq, bq, Wk, bk, Wv, bv, Ws, bs):
        import jax, jax.numpy as jnp
        import numpy as np
        N_NODES = 50000
        N_EDGES = 10000
        D = 128
        L = 3

        def _transformer_conv(x, src, dst, Wq, bq, Wk, bk, Wv, bv, Ws, bs):
            n = x.shape[0]
            d = Wq.shape[1]
            q = x @ Wq + bq
            k = x @ Wk + bk
            v = x @ Wv + bv
            skip = x @ Ws + bs
            logits = jnp.sum(q[dst] * k[src], axis=-1) * (1.0 / jnp.sqrt(jnp.asarray(d, x.dtype)))
            m = jax.ops.segment_max(logits, dst, num_segments=n)
            e = jnp.exp(logits - m[dst])
            z = jax.ops.segment_sum(e, dst, num_segments=n)
            alpha = e / jnp.maximum(z[dst], 1e-16)
            agg = jax.ops.segment_sum(alpha[:, None] * v[src], dst, num_segments=n)
            return agg + skip
        src = edge_index[0]
        dst = edge_index[1]
        n_layers = Wq.shape[0]
        h = x
        for l in range(n_layers):
            h = _transformer_conv(h, src, dst, Wq[l], bq[l], Wk[l], bk[l], Wv[l], bv[l], Ws[l], bs[l])
            if l < n_layers - 1:
                h = jax.nn.relu(h)
        return h
    edge_index = jnp.stack([src, dst])
    x = _layernorm(x + _L0_gnn_ref(x, edge_attr_3, src, dst, L0_gnn_W1, L0_gnn_b1, L0_gnn_W2), axis=-1)
    x = _layernorm(x + _L1_gnn_ref(x, edge_index, L1_gnn_Wq, L1_gnn_bq, L1_gnn_Wk, L1_gnn_bk, L1_gnn_Wv, L1_gnn_bv, L1_gnn_Ws, L1_gnn_bs), axis=-1)
    return x

_drawn_inputs = setup_inputs


def setup_inputs(seed=0):
    import zlib

    import numpy as np

    out = dict(_drawn_inputs(seed))
    spreads = {'L0_gnn_b1': (0.0, 0.571)}
    factors = {'edge_attr_3': 2.867, 'L1_gnn_bq': 64.0, 'L1_gnn_bk': 64.0, 'L1_gnn_bv': 6.316}
    for name, (base, spread) in spreads.items():
        noise = np.random.default_rng([zlib.crc32(name.encode()), seed]).standard_normal(out[name].shape)
        drawn = base * np.exp(spread * noise) if base else spread * noise
        out[name] = jnp.asarray(drawn.astype(out[name].dtype))
    for name, factor in factors.items():
        out[name] = (out[name] * factor).astype(out[name].dtype)
    return out
```

```python
import numpy as np
import concourse.bass as bass
from concourse import mybir
from concourse.alu_op_type import AluOpType as ALU
from contextlib import ExitStack

FP32 = mybir.dt.float32
BF16 = mybir.dt.bfloat16
I32 = mybir.dt.int32
U8 = mybir.dt.uint8
ACT = mybir.ActivationFunctionType

N_NODES, N_EDGES, D = 100000, 25000, 128
P = 128
J = 4
T = P * J
NT = -(-N_EDGES // T)
NC = NT * J
NS = NC * P
HC = NC // 2
LAYERS = 3
DENSE_TILES = -(-N_NODES // T)
UNROLL = 4
SMIN, SMAX = -2, 8
LO = SMAX
HI = LO + UNROLL * ((NT + SMIN - LO) // UNROLL)
BIG = 1.0e30
EPS = 1e-5
SKIP = 1.0e6


def gnn_program(nc, x, xsrc_idx, xdst_idx, slot_ids, dst_pad, wT, w1a, w1b, w2a, w2b,
                wqT, wkT, bq, wv, bv, ws, bs, bs_col, out):
    ctx = ExitStack()
    with ctx:
        def sb(name, shape, dt=FP32):
            return ctx.enter_context(nc.sbuf_tensor(name, shape, dt))

        def pb(name, shape=(P, 512), dt=FP32):
            return ctx.enter_context(nc.psum_tensor(name, list(shape), dt))

        def sem(name):
            return ctx.enter_context(nc.semaphore(name))

        U = [nc.dram_tensor(f"u{l}", (2 * NS, D), FP32).ap() for l in range(LAYERS)]
        msg_d = nc.dram_tensor("msg_d", (NS, D), FP32).ap()
        hs_d = nc.dram_tensor("hs_d", (NS, D), FP32).ap()
        skip_d = nc.dram_tensor("skip_d", (NS, D), FP32).ap()
        map_d = nc.dram_tensor("map_d", (N_NODES, 1), FP32).ap()
        found_d = nc.dram_tensor("found_d", (NT, P, J), FP32).ap()
        srcslot_d = nc.dram_tensor("srcslot_d", (NT, P, J), I32).ap()
        scat_d = nc.dram_tensor("scat_d", (NT, P, J), I32).ap()
        ord_d = nc.dram_tensor("ord_d", (1, NS), U8).ap()

        ident = sb("ident", [P, P])
        one = sb("one", [1, P])
        w1a_s, w2a_s, w2b_s = sb("w1a_s", [P, D]), sb("w2a_s", [P, D]), sb("w2b_s", [P, D])
        w1b_s = sb("w1b_s", [4, D])
        ws_s, wv_s = sb("ws_s", [P, LAYERS, D]), sb("wv_s", [P, LAYERS, D])
        a_s = sb("a_s", [P, LAYERS, D + 1])
        arow_s = sb("arow_s", [1, LAYERS, D + 1])
        bscol_s = sb("bscol_s", [P, LAYERS])
        brow_s = sb("brow_s", [P, LAYERS, J, D])
        b3row_s = sb("b3row_s", [P, J, D])
        ordrow = sb("ordrow", [P, NS], U8)
        firstm = sb("firstm", [P, NS], U8)
        ordcol = sb("ordcol", [P, NC])
        endcol = sb("endcol", [P, NC])
        logit_c = sb("logit_c", [P, NC])
        alpha_c = sb("alpha_c", [P, NC])
        h = [HC, 2, P]
        nb, notstart, last, notlast = sb("nb", h), sb("notstart", h), sb("last", h), sb("notlast", h)
        va, vb, vc, vd = sb("va", h), sb("vb", h), sb("vc", h), sb("vd", h)
        incol = sb("incol", [HC, 2])
        nostart_row, nb_row, nolast_row = sb("nostart_row", [1, NC]), sb("nb_row", [1, NC]), sb("nolast_row", [1, NC])
        crow = sb("crow", [1, NC + 1])
        fixidx = sb("fixidx", [HC, 2], I32)
        fixrow = sb("fixrow", [HC, 2, D])
        ccol = sb("ccol", [HC, 4])
        xr = sb("xr", [P, 4, J, D])
        xT = sb("xT", [P, 2, T])
        yb = sb("yb", [P, J, D])
        x1 = sb("x1", [P, 4, J, D])
        x1T = sb("x1T", [P, 2, T])
        h1T = sb("h1T", [P, 2, T])
        h2T = sb("h2T", [P, 2, T])
        zb = sb("zb", [P, J, D])
        ob = sb("ob", [P, 2, J, D])
        stat = sb("stat", [P, 2, J, 6])
        mv = sb("mv", [P, 2, J, 2])
        rs, ri = sb("rs", [P, 2, J]), sb("ri", [P, 2, J])
        eps_s = sb("eps_s", [P, 1])
        gi = sb("gi", [P, 4, J], I32)
        gm = sb("gm", [P, 4, J], I32)
        slotv = sb("slotv", [P, 4, J])
        x1e = sb("x1e", [P, 2, J, D])
        er = sb("er", [P, 4, J, D + 1])
        eT = sb("eT", [P, 2, T])
        ey = sb("ey", [P, J, D])
        e1 = sb("e1", [P, 2, J, D])
        e1T = sb("e1T", [P, 2, T])
        g1T = sb("g1T", [P, 2, T])
        g2T = sb("g2T", [P, 2, T])
        r1 = sb("r1", [P, 2, J, D])
        r2 = sb("r2", [P, 2, J, D])
        mrow = sb("mrow", [P, 2, J, D])
        sel = sb("sel", [P, 2, J, P])
        wt = sb("wt", [4, 2, T])
        found = sb("found", [P, 2, J])
        zcol = sb("zcol", [P, 1])
        di, dp, dn, slot_i = sb("di", h, I32), sb("dp", h, I32), sb("dn", h, I32), sb("slot_i", h, I32)
        ordb = sb("ordb", h, U8)
        idx_all = sb("idx_all", [P, NC], I32)
        slot_all = sb("slot_all", [P, NC])
        wqT_s, wkT_s = sb("wqT_s", [P, LAYERS, D]), sb("wkT_s", [P, LAYERS, D + 1])
        bq_s = sb("bq_s", [P, LAYERS])
        minus = sb("minus", [P, 800])
        lg = sb("lg", [P, 2, J])
        junk = sb("junk", [P, J, D + 1])
        estat = sb("estat", [P, J, 6])
        emv = sb("emv", [P, J, 2])
        ers, eri = sb("ers", [P, J]), sb("eri", [P, J])

        bank = [pb(f"bank{k}") for k in range(8)]

        s_w, s_b, s_seg, s_mapset, s_id, s_iota = (sem(n) for n in ("s_w", "s_b", "s_seg", "s_mapset", "s_id", "s_iota"))
        x_in = [sem(f"x_in{k}") for k in range(4)]
        o_out = [sem(f"o_out{k}") for k in range(2)]
        dA, dB, dC, dD, dE, dF = (sem(f"pe_d{n}") for n in "ABCDEF")
        xT_r, x1T_r, h1T_r, h2T_r = (sem(n) for n in ("xT_r", "x1T_r", "h1T_r", "h2T_r"))
        sqB, sqF = sem("sqB"), sem("sqF")
        cB, cF = sem("cB"), sem("cF")
        KB, KF, KT = 5, 6, 6

        block = ctx.enter_context(nc.Block())

        def pipeline(eng, step):
            for i in range(SMIN, LO):
                step(i, i % UNROLL, lambda s, i=i: 0 <= i - s < NT)
            with eng.Fori(LO // UNROLL, HI // UNROLL) as r:
                for u in range(UNROLL):
                    step(r * UNROLL + u, u, lambda s: True)
            for i in range(HI, NT + SMAX):
                step(i, i % UNROLL, lambda s, i=i: 0 <= i - s < NT)

        def settle(eng):
            eng.sem_inc(s_passed, 1)

        def after(eng, chain, n):
            if not (isinstance(n, int) and n <= 0):
                eng.wait_ge(chain, n)

        def count(base, t, k=1):
            return t * k + (base + k)

        def slot_count(base, t, u, ring, by=16):
            return (t - u) * (by // ring) + (base + by)

        def in_slot(ring, u, phases, by=16):
            return by * phases * len(range(u, NT, ring))

        NODE_PHASES = DENSE_TILES // NT

        def node_row(ph, t):
            return (ph * NT + t) * T if not isinstance(t, int) else min((ph * NT + t) * T, N_NODES - T)

        def rows_of(a, r0):
            return a[bass.ds(r0, T), :].rearrange("(p j) f -> p j f", p=P)

        def node_load(sp, ph, i, u, on):
            if on(-2):
                t, k = i + 2, (u + 2) % 4
                if not isinstance(t, int) or t >= 4:
                    sp.wait_ge(cB, count(ph * NT * KB, t - 4, KB))
                sp.dma_start(xr[:, k], rows_of(x, node_row(ph, t))).then_inc(x_in[k], 16)

        def node_store(sp, ph, i, u, on):
            if on(6):
                t, k = i - 6, (u - 6) % 2
                sp.wait_ge(cF, count(ph * NT * KF, t, KF))
                if isinstance(t, int) and ph * NT + t == DENSE_TILES - 1:
                    sp.wait_ge(o_out[1 - k], in_slot(2, 1 - k, ph + 1))
                sp.dma_start(rows_of(out, node_row(ph, t)), ob[:, k]).then_inc(o_out[k], 16)

        def node_pe(pe, ph, i, u, on):
            b0 = ph * NT
            if on(0):
                t, k = i, u % 4
                pe.wait_ge(x_in[k], slot_count(in_slot(4, k, ph), t, k, 4))
                if on(4):
                    pe.wait_ge(h1T_r, count(b0, i - 4))
                elif on(1):
                    pe.wait_ge(xT_r, count(b0, i - 1))
                for j in range(J):
                    mm = nc.tensor.transpose(bank[0][:, j * P:(j + 1) * P], xr[:, k, j, :], ident[:, :])
                mm.then_inc(dA, 1)
            if on(1):
                t, k = i - 1, (u - 1) % 2
                pe.wait_ge(xT_r, count(b0, t))
                if on(5):
                    pe.wait_ge(h2T_r, count(b0, i - 5))
                elif on(2):
                    pe.wait_ge(cB, (i - 2) * KB + b0 * KB + 1)
                for j in range(J):
                    mm = nc.tensor.matmul(bank[1][:, j * P:(j + 1) * P], xT[:, k, j * P:(j + 1) * P], w2a_s[:, :],
                                          start=True, stop=True)
                mm.then_inc(dB, 1)
            if on(2):
                t, k = i - 2, (u - 2) % 4
                pe.wait_ge(cB, count(b0 * KB, t, KB))
                if on(6):
                    pe.wait_ge(cF, b0 * KF + (i - 6) * KF + 1)
                elif on(3):
                    pe.wait_ge(x1T_r, count(b0, i - 3))
                for j in range(J):
                    mm = nc.tensor.transpose(bank[2][:, j * P:(j + 1) * P], x1[:, k, j, :], ident[:, :])
                mm.then_inc(dC, 1)
            if on(3):
                t, k = i - 3, (u - 3) % 2
                pe.wait_ge(x1T_r, count(b0, t))
                pe.wait_ge(xT_r, count(b0, min(i, NT - 1) if isinstance(i, int) else i))
                if on(4) and not on(0):
                    pe.wait_ge(h1T_r, count(b0, t - 1))
                nc.tensor.matmul(bank[0][:, :], ws_s[:, 0, :], x1T[:, k, :], start=True, stop=True).then_inc(dD, 1)
            if on(4):
                t, k = i - 4, (u - 4) % 2
                pe.wait_ge(h1T_r, count(b0, t))
                pe.wait_ge(cB, (min(i - 1, NT - 1) if isinstance(i, int) else i - 1) * KB + (b0 * KB + 1))
                if on(5) and not on(1):
                    pe.wait_ge(h2T_r, count(b0, t - 1))
                nc.tensor.matmul(bank[1][:, :], ws_s[:, 1, :], h1T[:, k, :], start=True, stop=True).then_inc(dE, 1)
            if on(5):
                t, k = i - 5, (u - 5) % 2
                pe.wait_ge(h2T_r, count(b0, t))
                pe.wait_ge(x1T_r, count(b0, min(i - 2, NT - 1) if isinstance(i, int) else i - 2))
                if on(6) and not on(2):
                    pe.wait_ge(cF, b0 * KF + (t - 1) * KF + 1)
                for j in range(J):
                    mm = nc.tensor.matmul(bank[2][:, j * P:(j + 1) * P], h2T[:, k, j * P:(j + 1) * P], ws_s[:, 2, :],
                                          start=True, stop=True)
                mm.then_inc(dF, 1)

        def node_act(act, ph, i, u, on):
            b0 = ph * NT
            if on(0):
                t, k = i, u % 2
                act.wait_ge(dA, count(b0, t))
                if on(2):
                    act.wait_ge(dB, count(b0, t - 2))
                nc.scalar.activation(xT[:, k, :], bank[0][:, :], ACT.Copy).then_inc(xT_r, 1)
            if on(2):
                t, k = i - 2, (u - 2) % 2
                act.wait_ge(dC, count(b0, t))
                if on(4):
                    act.wait_ge(dD, count(b0, t - 2))
                nc.scalar.activation(x1T[:, k, :], bank[2][:, :], ACT.Copy).then_inc(x1T_r, 1)
            if on(3):
                t, k = i - 3, (u - 3) % 2
                act.wait_ge(dD, count(b0, t))
                if on(5):
                    act.wait_ge(dE, count(b0, t - 2))
                nc.scalar.activation(h1T[:, k, :], bank[0][:, :], ACT.Relu, bias=bscol_s[:, 0:1]).then_inc(h1T_r, 1)
            if on(4):
                t, k = i - 4, (u - 4) % 2
                act.wait_ge(dE, count(b0, t))
                if on(6):
                    act.wait_ge(dF, count(b0, t - 2))
                nc.scalar.activation(h2T[:, k, :], bank[1][:, :], ACT.Relu, bias=bscol_s[:, 1:2]).then_inc(h2T_r, 1)

        def moments(dve, src, st, m, chain, at):
            dve.wait_ge(chain, at)
            for j in range(J):
                op = nc.vector.bn_stats(st[:, j, :], src[:, j, :])
            op.then_inc(chain, 1)
            dve.wait_ge(chain, at + 1)
            settle(dve)
            for j in range(J):
                op = nc.vector.bn_aggr(m[:, j, :], st[:, j, :])
            op.then_inc(chain, 1)

        def root(m, r, done):
            nc.scalar.activation(r, m[:, :, 1], ACT.Sqrt, bias=eps_s[:, 0:1]).then_inc(done, 1)

        def normalise(dve, src, dst, m, r, inv, chain, at):
            nc.vector.reciprocal(inv, r).then_inc(chain, 1)
            dve.wait_ge(chain, at + 1)
            for j in range(J):
                op = nc.vector.tensor_scalar(dst[:, j, :], src[:, j, :], m[:, j, 0:1], inv[:, j:j + 1],
                                             ALU.subtract, ALU.mult)
            op.then_inc(chain, 1)

        def node_sqrt(act, ph, i, u, on):
            b0 = ph * NT
            if on(1):
                act.wait_ge(cB, (i - 1) * KB + (b0 * KB + 3))
                root(mv[:, 1], rs[:, 1], sqB)
            if on(5):
                act.wait_ge(cF, (i - 5) * KF + (b0 * KF + 4))
                root(mv[:, 0], rs[:, 0], sqF)

        def node_dve1(dve, ph, i, u, on):
            b0 = ph * NT
            if on(1):
                t, k = i - 1, (u - 1) % 4
                at = t * KB + b0 * KB
                after(dve, cB, at)
                dve.wait_ge(dB, count(b0, t))
                nc.vector.scalar_tensor_tensor(yb[:, :, :], bank[1][:, :].rearrange("p (j f) -> p j f", j=J), 0.0,
                                               xr[:, k], ALU.max, ALU.add).then_inc(cB, 1)
                moments(dve, yb, stat[:, 1], mv[:, 1], cB, at + 1)
            if on(5):
                t, k4, k2 = i - 5, (u - 5) % 4, (u - 5) % 2
                at = t * KF + b0 * KF
                after(dve, cF, at)
                dve.wait_ge(dF, count(b0, t))
                nc.vector.tensor_tensor(zb[:, :, :], bank[2][:, :].rearrange("p (j f) -> p j f", j=J),
                                        x1[:, k4], ALU.add).then_inc(cF, 1)
                dve.wait_ge(cF, at + 1)
                nc.vector.tensor_tensor(zb[:, :, :], zb[:, :, :], b3row_s[:, :, :], ALU.add).then_inc(cF, 1)
                moments(dve, zb, stat[:, 0], mv[:, 0], cF, at + 2)

        def node_dve2(dve, ph, i, u, on):
            b0 = ph * NT
            if on(1):
                t, k = i - 1, (u - 1) % 4
                dve.wait_ge(sqB, count(b0, t))
                normalise(dve, yb, x1[:, k], mv[:, 1], rs[:, 1], ri[:, 1], cB, t * KB + (b0 * KB + 3))
            if on(5):
                t, k2 = i - 5, (u - 5) % 2
                dve.wait_ge(sqF, count(b0, t))
                if on(7):
                    dve.wait_ge(o_out[k2], slot_count(in_slot(2, k2, ph), t - 2, k2, 2))
                normalise(dve, zb, ob[:, k2], mv[:, 0], rs[:, 0], ri[:, 0], cF, t * KF + (b0 * KF + 4))

        def edge_rows(a, t, base=0):
            return a[bass.ds(t * T + base, T), :].rearrange("(j p) f -> p j f", p=P)


        i_in = [sem(f"i_in{k}") for k in range(4)]
        m_out = [sem(f"m_out{k}") for k in range(4)]
        g_in = [sem(f"g_in{k}") for k in range(4)]
        f_in = [sem(f"f_in{k}") for k in range(2)]
        f_out = [sem(f"f_out{k}") for k in range(2)]
        w_in = [sem(f"w_in{k}") for k in range(2)]
        S_out = [[sem(f"S_out{n}{k}") for k in range(2)] for n in range(4)]
        s_e, s_a, s_v = ([sem(f"S_{w}{n}") for n in range(m)] for w, m in (("pe", 8), ("act", 7), ("dve", 1)))
        ti_in = [sem(f"ti_in{k}") for k in range(4)]
        tg_in = [sem(f"tg_in{k}") for k in range(4)]
        tl_in = [sem(f"tl_in{k}") for k in range(2)]
        t_out = [sem(f"t_out{k}") for k in range(2)]
        t_e, t_v = ([sem(f"T_{w}{n}") for n in range(3)] for w in ("pe", "dve"))
        t_a = sem("t_a")
        ai_in = [sem(f"ai_in{k}") for k in range(4)]
        ag_in = [sem(f"ag_in{k}") for k in range(4)]
        al_in = [sem(f"al_in{k}") for k in range(2)]
        ah_out = [sem(f"ah_out{k}") for k in range(4)]
        as_out = [sem(f"as_out{k}") for k in range(2)]
        a_e, a_v = ([sem(f"A_{w}{n}") for n in range(3)] for w in ("pe", "dve"))
        a_a = sem("a_a")
        bl_in = [sem(f"bl_in{k}") for k in range(2)]
        b_out = [sem(f"b_out{k}") for k in range(2)]
        b_e, b_v = ([sem(f"B_{w}{n}") for n in range(m)] for w, m in (("pe", 2), ("dve", 3)))
        b_a = sem("b_a")
        bi_in = [sem(f"bi_in{k}") for k in range(4)]
        s_tail, s_row, s_crow, s_col, s_chain = (sem(n) for n in ("s_tail", "s_row", "s_crow", "s_col", "s_chain"))
        s_lt, s_exp, s_al, s_at, s_arg = (sem(n) for n in ("s_lt", "s_exp", "s_al", "s_at", "s_arg"))
        s_p0, s_p1, s_p2, s_ordout, s_ordin, s_scout = (sem(n) for n in ("s_p0", "s_p1", "s_p2", "s_ordout", "s_ordin", "s_scout"))
        s_prep, s_fixi, s_fixg, s_fixw, s_fd, s_fc, s_fo, s_wt = (sem(n) for n in (
            "s_prep", "s_fixi", "s_fixg", "s_fixw", "s_fd", "s_fc", "s_fo", "s_wt"))
        s_fin = [sem(f"s_fin{k}") for k in range(2)]
        s_vl = sem("s_vl")
        s_passed = sem("s_passed")
        S_sq, T_sq, B_sq = sem("S_sq"), sem("T_sq"), sem("B_sq")

        def chunk_rows(v):
            return v.rearrange("p (j f) -> p j f", j=J)

        def wait_all(eng, pairs):
            for s, n in pairs:
                eng.wait_ge(s, n)

        def node_end(ph):
            return [(o_out[k], in_slot(2, k, ph + 1)) for k in range(2)]

        prep_end = [(s_w, 160), (s_p0, 1), (s_prep, 1), (s_ordin, 16), (s_scout, 16), (s_mapset, 16)]
        map_end = [(m_out[k], in_slot(4, k, 1, 64)) for k in range(4)] + node_end(0)
        src_end = [(q[k], in_slot(2, k, 1)) for q in S_out for k in range(2)] + node_end(1)
        dst_end = [(q[k], in_slot(2, k, 1)) for q in (t_out, f_out) for k in range(2)] + node_end(2)

        def a_end(l):
            return ([(ah_out[k], in_slot(4, k, l + 1)) for k in range(4)]
                    + [(as_out[k], in_slot(2, k, l + 1)) for k in range(2)]
                    + [(a_v[0], 5 * NT * (l + 1))] + (node_end(3) if l == 0 else []))

        def b_end(l):
            return ([(b_out[k], in_slot(2, k, l + 1)) for k in range(2)] if l < LAYERS - 1 else [])

        def select(t, k, weight, done):
            for j in range(J):
                cols = bass.ds(t * T + j * P, P)
                c = bass.ds(t * J + j, 1)
                if weight is None:
                    op = nc.vector.tensor_scalar(sel[:, k, j, :], ordrow[:, cols], ordcol[:, c], None, ALU.is_equal)
                else:
                    op = nc.vector.tensor_scalar(sel[:, k, j, :], ordrow[:, cols], ordcol[:, c], weight[:, c],
                                                 ALU.is_equal, ALU.mult)
            op.then_inc(done, 1)

        def carry(dve, t, k, ps, chain, at):
            for j in range(J):
                if j:
                    dve.wait_ge(chain, at + j)
                before = g1T[:, k, j * P - 1:j * P] if j else g1T[:, 1 - k, T - 1:T]
                if isinstance(t, int) and t == 0 and j == 0:
                    before = zcol[:, :]
                nc.vector.scalar_tensor_tensor(g1T[:, k, j * P:(j + 1) * P], firstm[:, bass.ds(t * T + j * P, P)],
                                               before, ps[:, j * P:(j + 1) * P], ALU.mult, ALU.add).then_inc(chain, 1)

        def over_chunks_dve(dve, q, kind, a, b, o):
            rev = kind == "back"
            ops = (ALU.add, ALU.max) if kind == "max" else (ALU.mult, ALU.add)
            first = -BIG if kind == "max" else 0.0
            coef = {"max": nb_row, "add": nostart_row, "back": nolast_row}[kind]

            def within(initial):
                for k in range(2):
                    w = slice(None, None, -1) if rev else slice(None)
                    op = nc.vector.tensor_tensor_scan(o[:, k, w], a[:, k, w], b[:, k, w],
                                                      incol[:, k:k + 1] if initial is None else initial, *ops)
                return op

            within(first).then_inc(s_tail, 1)
            nc.vector.memset(crow[:, NC:NC + 1] if rev else crow[:, 0:1], first).then_inc(s_chain, 1)
            dve.wait_ge(s_row, q + 1)
            ends = bank[6][0:1, 0:NC]
            if rev:
                nc.vector.tensor_tensor_scan(crow[:, NC - 1::-1], coef[:, ::-1], ends[:, ::-1], first, *ops).then_inc(s_crow, 1)
            else:
                nc.vector.tensor_tensor_scan(crow[:, 1:NC + 1], coef[:, :], ends, first, *ops).then_inc(s_crow, 1)
            dve.wait_ge(s_col, q + 1)
            nc.vector.tensor_copy(incol[:, :], bank[7][0:HC, 0:2]).then_inc(s_chain, 1)
            dve.wait_ge(s_chain, 3 * q + 2)
            within(None).then_inc(s_chain, 1)
            dve.wait_ge(s_chain, 3 * q + 3)

        def over_chunks_pe(pe, q, kind, o):
            rev = kind == "back"
            pe.wait_ge(s_tail, q + 1)
            if q:
                pe.wait_ge(s_crow, q)
            e = 0 if rev else P - 1
            for k in range(2):
                mm = nc.tensor.matmul(bank[6][0:1, k * HC:(k + 1) * HC], o[:, k, e:e + 1], ident[0:HC, 0:HC],
                                      start=True, stop=True)
            mm.then_inc(s_row, 1)
            pe.wait_ge(s_crow, q + 1)
            pe.wait_ge(s_chain, 3 * q + 1)
            f = 1 if rev else 0
            for k in range(2):
                mm = nc.tensor.matmul(bank[7][0:HC, k:k + 1], crow[0:1, f + k * HC:f + (k + 1) * HC], one[0:1, 0:1],
                                      start=True, stop=True)
            mm.then_inc(s_col, 1)

        def ends_view(shift):
            return bass.AP(dst_pad.tensor, shift, [[P, HC], [HC * P, 2], [1, P]])

        @block.sync
        def _(sp):
            for a, b in ((w1a_s, w1a), (w1b_s, w1b), (w2a_s, w2a), (w2b_s, w2b)):
                sp.dma_start(a[:, :], b).then_inc(s_w, 16)
            for a, b in ((ws_s, ws), (wv_s, wv), (wqT_s, wqT), (wkT_s, wkT)):
                sp.dma_start(a[:, :, :], b).then_inc(s_w, 16)
            sp.dma_start(bq_s[:, :], bq).then_inc(s_w, 16)
            sp.dma_start(bscol_s[:, :], bs_col).then_inc(s_w, 16)
            for a, shift in ((dp, 0), (di, 1), (dn, 2)):
                sp.dma_start(a[:, :, :], ends_view(shift)).then_inc(s_seg, 16)
            sp.dma_start(slot_all[:, :].rearrange("p (t j) -> p t j", j=J),
                         slot_ids.rearrange("t p j -> p t j")).then_inc(s_seg, 16)
            for l in range(LAYERS):
                for j in range(J):
                    sp.dma_start(brow_s[:, l, j, :],
                                 bass.AP(bs.tensor, l * D, [[0, P], [1, D]])).then_inc(s_b, 16)
                    sp.dma_start(mrow[:, 0, j, :] if l == 0 else mrow[:, 1, j, :] if l == 1 else r1[:, 0, j, :],
                                 bass.AP(bv.tensor, l * D, [[0, P], [1, D]])).then_inc(s_b, 16)
            sp.wait_ge(s_p0, 1)
            sp.dma_start(map_d.rearrange("(p n) o -> p (n o)", p=125), minus[0:125, :]).then_inc(s_mapset, 16)
            sp.wait_ge(s_p1, 1)
            sp.dma_start(bass.AP(ord_d.tensor, 0, [[P, HC], [HC * P, 2], [1, P]]), ordb[:, :, :]).then_inc(s_ordout, 16)
            sp.wait_ge(s_ordout, 16)
            sp.dma_start(ordrow[:, :], bass.AP(ord_d.tensor, 0, [[0, P], [1, NS]])).then_inc(s_ordin, 16)
            sp.wait_ge(s_p2, 1)
            sp.dma_start(scat_d.rearrange("t p j -> p t j"),
                         idx_all[:, :].rearrange("p (t j) -> p t j", j=J)).then_inc(s_scout, 16)
            wait_all(sp, prep_end)

            def map_step(i, u, on):
                node_load(sp, 0, i, u, on)
                if on(-2):
                    t, k = i + 2, (u + 2) % 4
                    if not isinstance(t, int) or t >= 4:
                        sp.wait_ge(m_out[k], slot_count(0, t - 4, k, 4, 64))
                        settle(sp)
                    sp.dma_start(gi[:, k, :], scat_d[bass.ds(t, 1)].rearrange("o p j -> p (o j)")).then_inc(i_in[k], 16)
                    sp.dma_start(slotv[:, k, :], slot_ids[bass.ds(t, 1)].rearrange("o p j -> p (o j)")).then_inc(i_in[k], 16)
                node_store(sp, 0, i, u, on)
            pipeline(sp, map_step)
            wait_all(sp, map_end)

            def src_step(i, u, on):
                node_load(sp, 1, i, u, on)
                if on(-2):
                    t, k = i + 2, (u + 2) % 4
                    if not isinstance(t, int) or t >= 4:
                        sp.wait_ge(g_in[k], slot_count(0, t - 4, k, 4, 64))
                        settle(sp)
                    sp.dma_start(gi[:, k, :], xsrc_idx[bass.ds(t, 1)].rearrange("o p j -> p (o j)")).then_inc(
                        i_in[k], 16)
                if on(0):
                    t, k = i, u % 2
                    if on(2):
                        sp.wait_ge(s_e[1], count(0, t - 2))
                        settle(sp)
                    sp.dma_start(wt[:, k, :], wT[:, bass.ds(t * T, T)]).then_inc(w_in[k], 16)
                if on(2):
                    t, k = i - 2, u % 2
                    sp.wait_ge(s_a[1], count(0, t))
                    settle(sp)
                    sp.dma_start(edge_rows(msg_d, t), mrow[:, k]).then_inc(S_out[0][k], 16)
                    sp.wait_ge(s_v[0], count(0, t, 5))
                    settle(sp)
                    sp.dma_start(edge_rows(U[0], t, NS), e1[:, k]).then_inc(S_out[1][k], 16)
                if on(5):
                    t, k = i - 5, (u - 5) % 2
                    sp.wait_ge(s_a[4], count(0, t))
                    settle(sp)
                    sp.dma_start(edge_rows(U[1], t, NS), r1[:, k]).then_inc(S_out[2][k], 16)
                if on(6):
                    t, k = i - 6, u % 2
                    sp.wait_ge(s_a[6], count(0, t))
                    settle(sp)
                    sp.dma_start(edge_rows(U[2], t, NS), r2[:, k]).then_inc(S_out[3][k], 16)
                node_store(sp, 1, i, u, on)
            pipeline(sp, src_step)
            wait_all(sp, src_end)

            def dst_step(i, u, on):
                node_load(sp, 2, i, u, on)
                if on(-2):
                    t, k = i + 2, (u + 2) % 4
                    if not isinstance(t, int) or t >= 4:
                        sp.wait_ge(tg_in[k], slot_count(0, t - 4, k, 4, 128))
                        settle(sp)
                    sp.dma_start(gi[:, k, :], xdst_idx[bass.ds(t, 1)].rearrange("o p j -> p (o j)")).then_inc(
                        ti_in[k], 16)
                    sp.dma_start(gm[:, k, :], xsrc_idx[bass.ds(t, 1)].rearrange("o p j -> p (o j)")).then_inc(
                        ti_in[k], 16)
                if on(0):
                    t, k = i, u % 2
                    if on(2):
                        sp.wait_ge(t_e[1], count(0, t - 2))
                        settle(sp)
                    sp.dma_start(mrow[:, k], edge_rows(msg_d, t)).then_inc(tl_in[k], 16)
                if on(1):
                    t, k = i - 1, (u - 1) % 2
                    k4 = (u - 1) % 4
                    sp.wait_ge(tg_in[k4], slot_count(0, t, k4, 4, 128))
                    settle(sp)
                    sp.dma_start(found_d[bass.ds(t, 1)].rearrange("o p j -> p (o j)"), found[:, k, :]).then_inc(
                        f_out[k], 16)
                if on(3):
                    t, k = i - 3, (u - 3) % 2
                    sp.wait_ge(t_v[2], count(0, t, 5))
                    settle(sp)
                    sp.dma_start(edge_rows(U[0], t), e1[:, k]).then_inc(t_out[k], 16)
                node_store(sp, 2, i, u, on)
            pipeline(sp, dst_step)
            wait_all(sp, dst_end)
            sp.dma_start(logit_c[:, :].rearrange("p (t j) -> p t j", j=J), found_d.rearrange("t p j -> p t j")).then_inc(s_fd, 16)
            sp.wait_ge(s_fc, 3)
            sp.dma_start(srcslot_d.rearrange("t p j -> p t j"),
                         idx_all[:, :].rearrange("p (t j) -> p t j", j=J)).then_inc(s_fo, 16)
            sp.wait_ge(s_fo, 16)

            def fix(l):
                sp.wait_ge(s_fixg, 32 * (l + 1))
                for k in range(2):
                    sp.dma_start(bass.AP(U[l].tensor, (k * HC * P + P - 1) * D, [[P * D, HC], [1, D]]),
                                 fixrow[:, k, :]).then_inc(s_fixw, 16)
                sp.wait_ge(s_fixw, 32 * (l + 1))

            for l in range(LAYERS):
                fix(l)

                def a_step(i, u, on, l=l):
                    b0 = l * NT
                    if l == 0:
                        node_load(sp, 3, i, u, on)
                    if on(-2):
                        t, k = i + 2, (u + 2) % 4
                        if not isinstance(t, int) or t >= 4:
                            sp.wait_ge(ag_in[k], slot_count(in_slot(4, k, l, 64), t - 4, k, 4, 64))
                            settle(sp)
                        sp.dma_start(gi[:, k, :], srcslot_d[bass.ds(t, 1)].rearrange("o p j -> p (o j)")).then_inc(
                            ai_in[k], 16)
                    if on(0):
                        t, k = i, u % 2
                        if on(2):
                            sp.wait_ge(a_e[0], count(b0, t - 2))
                            settle(sp)
                        sp.dma_start(r1[:, k], edge_rows(U[l], t)).then_inc(al_in[k], 16)
                    if on(1):
                        t, k = i - 1, (u - 1) % 4
                        sp.wait_ge(ag_in[k], slot_count(in_slot(4, k, l, 64), t, k, 4, 64))
                        settle(sp)
                        sp.dma_start(edge_rows(hs_d, t), er[:, k, :, 0:D]).then_inc(ah_out[k], 16)
                    if on(3):
                        t, k = i - 3, (u - 3) % 2
                        sp.wait_ge(a_v[2], count(b0, t))
                        settle(sp)
                        sp.dma_start(edge_rows(skip_d, t), mrow[:, k]).then_inc(as_out[k], 16)
                    if l == 0:
                        node_store(sp, 3, i, u, on)
                pipeline(sp, a_step)
                wait_all(sp, a_end(l))

                def b_step(i, u, on, l=l):
                    b0 = l * NT
                    tail = l == LAYERS - 1
                    if tail and on(-2):
                        t, k = i + 2, (u + 2) % 4
                        if not isinstance(t, int) or t >= 4:
                            sp.wait_ge(s_fin[k % 2], slot_count(0, t - 4, k % 2, 2, 64))
                            settle(sp)
                        sp.dma_start(gi[:, k, :], scat_d[bass.ds(t, 1)].rearrange("o p j -> p (o j)")).then_inc(
                            bi_in[k], 16)
                    if on(0):
                        t, k = i, u % 2
                        if on(2):
                            sp.wait_ge(b_e[0], count(b0, t - 2))
                            if not isinstance(t, int) or t >= 2:
                                sp.wait_ge(b_v[2], (t - 2) * (KT if tail else 1) + (b0 + (KT if tail else 1)))
                                settle(sp)
                        by = 48 if tail else 32
                        sp.dma_start(r1[:, k], edge_rows(hs_d, t)).then_inc(bl_in[k], 16)
                        sp.dma_start(r2[:, k], edge_rows(skip_d, t)).then_inc(bl_in[k], 16)
                        if tail:
                            sp.dma_start(x1e[:, k], edge_rows(U[0], t)).then_inc(bl_in[k], 16)
                    if not tail and on(3):
                        t, k = i - 3, (u - 3) % 2
                        sp.wait_ge(b_a, count(b0, t))
                        settle(sp)
                        sp.dma_start(edge_rows(U[l + 1], t), e1[:, k]).then_inc(b_out[k], 16)
                pipeline(sp, b_step)
                wait_all(sp, b_end(l))
            wait_all(sp, [(s_fin[k], in_slot(2, k, 1, 64)) for k in range(2)])

        @block.gpsimd
        def _(gp):
            gp.memset(ident[:, :], 0.0).then_inc(s_id, 1)
            gp.wait_ge(s_id, 1)
            gp.affine_select(out=ident[:, :], in_=ident[:, :], compare_op=ALU.not_equal, fill=1.0, base=0,
                             pattern=[[-1, P]], channel_multiplier=1).then_inc(s_id, 1)
            gp.memset(one[:, :], 1.0).then_inc(s_id, 1)
            gp.memset(zcol[:, :], 0.0).then_inc(s_id, 1)
            gp.memset(er[:, :, :, :], 1.0).then_inc(s_id, 1)
            gp.iota(slot_i[:, :, :], pattern=[[HC * P, 2], [1, P]], base=0, channel_multiplier=P).then_inc(s_iota, 1)
            gp.wait_ge(s_id, 5)
            wait_all(gp, prep_end)

            def map_step(i, u, on):
                if on(-1):
                    t, k = i + 1, (u + 1) % 4
                    gp.wait_ge(i_in[k], slot_count(0, t, k, 4, 32))
                    settle(gp)
                    for j in range(J):
                        gp.indirect_dma_start(map_d, bass.IndirectOffsetOnAxis(gi[:, k, j:j + 1], 0), slotv[:, k, j:j + 1],
                                              None, bounds_check=N_NODES - 1, oob_is_err=False).then_inc(m_out[k], 16)
            pipeline(gp, map_step)
            wait_all(gp, map_end)

            def src_step(i, u, on):
                if on(-1):
                    t, k = i + 1, (u + 1) % 4
                    gp.wait_ge(i_in[k], slot_count(in_slot(4, k, 1, 32), t, k, 4, 16))
                    if not isinstance(t, int) or t >= 4:
                        gp.wait_ge(s_e[0], count(0, t - 4))
                        gp.wait_ge(s_v[0], count(0, t - 4, 5))
                        settle(gp)
                    for j in range(J):
                        gp.indirect_dma_start(er[:, k, j, 0:D], None, x, bass.IndirectOffsetOnAxis(gi[:, k, j:j + 1], 0)
                                              ).then_inc(g_in[k], 16)
            pipeline(gp, src_step)
            wait_all(gp, src_end)

            def dst_step(i, u, on):
                if on(-1):
                    t, k = i + 1, (u + 1) % 4
                    k2 = (u + 1) % 2
                    gp.wait_ge(ti_in[k], slot_count(0, t, k, 4, 32))
                    if not isinstance(t, int) or t >= 4:
                        gp.wait_ge(t_e[0], count(0, t - 4))
                        gp.wait_ge(t_v[2], count(0, t - 4, 5))
                    if not isinstance(t, int) or t >= 2:
                        gp.wait_ge(f_out[k2], slot_count(0, t - 2, k2, 2))
                        settle(gp)
                    for j in range(J):
                        gp.indirect_dma_start(er[:, k, j, 0:D], None, x, bass.IndirectOffsetOnAxis(gi[:, k, j:j + 1], 0)
                                              ).then_inc(tg_in[k], 16)
                        gp.indirect_dma_start(found[:, k2, j:j + 1], None, map_d,
                                              bass.IndirectOffsetOnAxis(gm[:, k, j:j + 1], 0)).then_inc(tg_in[k], 16)
            pipeline(gp, dst_step)
            wait_all(gp, dst_end)
            gp.wait_ge(s_fo, 16)

            for l in range(LAYERS):
                for k in range(2):
                    gp.indirect_dma_start(fixrow[:, k, :], None, U[l], bass.IndirectOffsetOnAxis(fixidx[:, k:k + 1], 0)
                                          ).then_inc(s_fixg, 16)
                gp.wait_ge(s_fixw, 32 * (l + 1))

                def a_step(i, u, on, l=l):
                    if on(-1):
                        t, k = i + 1, (u + 1) % 4
                        gp.wait_ge(ai_in[k], slot_count(in_slot(4, k, l), t, k, 4))
                        if not isinstance(t, int) or t >= 4:
                            gp.wait_ge(a_v[0], count(l * NT * 5, t - 4, 5))
                            gp.wait_ge(ah_out[k], slot_count(in_slot(4, k, l), t - 4, k, 4))
                            settle(gp)
                        for j in range(J):
                            gp.indirect_dma_start(er[:, k, j, 0:D], None, U[l],
                                                  bass.IndirectOffsetOnAxis(gi[:, k, j:j + 1], 0)).then_inc(ag_in[k], 16)
                pipeline(gp, a_step)
                wait_all(gp, a_end(l))
                if l < LAYERS - 1:
                    wait_all(gp, b_end(l))

            def out_step(i, u, on):
                if on(3):
                    t, k = i - 3, (u - 3) % 4
                    k2 = (u - 3) % 2
                    gp.wait_ge(bi_in[k], slot_count(0, t, k, 4))
                    gp.wait_ge(b_v[2], t * KT + ((LAYERS - 1) * NT + KT))
                    settle(gp)
                    for j in range(J):
                        gp.indirect_dma_start(out, bass.IndirectOffsetOnAxis(gi[:, k, j:j + 1], 0), e1[:, k2, j, :],
                                              None, bounds_check=N_NODES - 1, oob_is_err=False).then_inc(s_fin[k2], 16)
            pipeline(gp, out_step)
            wait_all(gp, [(s_fin[k], in_slot(2, k, 1, 64)) for k in range(2)])

        @block.tensor
        def _(pe):
            pe.wait_ge(s_id, 5)
            pe.wait_ge(s_w, 160)
            for l in range(LAYERS):
                nc.tensor.matmul(bank[l][:, 0:D + 1], wqT_s[:, l, :], wkT_s[:, l, :], start=True, stop=True)
                mm = nc.tensor.matmul(bank[3 + l][0:1, 0:D + 1], bq_s[:, l:l + 1], wkT_s[:, l, :], start=True, stop=True)
            mm.then_inc(s_wt, 1)
            pe.wait_ge(s_p1, 1)
            for n in range(4):
                mm = nc.tensor.matmul(bank[6][0:1, n * HC:(n + 1) * HC], ccol[:, n:n + 1], ident[0:HC, 0:HC],
                                      start=True, stop=True)
            pe.wait_ge(s_wt, 2)
            for k in range(2):
                nc.tensor.transpose(bank[0][:, k * HC:(k + 1) * HC], vb[:, k, :], ident[0:HC, 0:HC])
                nc.tensor.transpose(bank[1][:, k * HC:(k + 1) * HC], vc[:, k, :], ident[0:HC, 0:HC])
                mm = nc.tensor.transpose(bank[2][:, k * HC:(k + 1) * HC], vd[:, k, :], ident[0:HC, 0:HC])
            mm.then_inc(s_wt, 1)
            pe.wait_ge(s_fixi, 1)
            over_chunks_pe(pe, 0, "back", va)
            wait_all(pe, prep_end)

            pipeline(pe, lambda i, u, on: node_pe(pe, 0, i, u, on))
            wait_all(pe, map_end)

            def src_step(i, u, on):
                if on(0):
                    k = u % 4
                    pe.wait_ge(g_in[k], slot_count(0, i, k, 4, 64))
                    if on(5):
                        pe.wait_ge(s_a[4], count(0, i - 5))
                    elif on(1):
                        pe.wait_ge(s_a[0], count(0, i - 1))
                    for j in range(J):
                        mm = nc.tensor.transpose(bank[3][:, j * P:(j + 1) * P], er[:, k, j, 0:D], ident[:, :])
                    mm.then_inc(s_e[0], 1)
                node_pe(pe, 1, i, u, on)
                if on(1):
                    t, k = i - 1, (u - 1) % 2
                    pe.wait_ge(s_a[0], count(0, t))
                    pe.wait_ge(w_in[k], slot_count(0, t, k, 2))
                    if on(5):
                        pe.wait_ge(s_a[5], count(0, i - 5))
                    elif on(2):
                        pe.wait_ge(s_a[1], count(0, i - 2))
                    for j in range(J):
                        c = slice(j * P, (j + 1) * P)
                        nc.tensor.matmul(bank[4][:, c], eT[:, k, c], w1a_s[:, :], start=True, stop=False)
                        mm = nc.tensor.matmul(bank[4][:, c], wt[:, k, c], w1b_s[:, :], start=False, stop=True)
                    mm.then_inc(s_e[1], 1)
                    if on(6):
                        pe.wait_ge(s_a[6], count(0, i - 6))
                    elif on(2):
                        pe.wait_ge(s_v[0], (i - 2) * 5 + 1)
                    for j in range(J):
                        c = slice(j * P, (j + 1) * P)
                        mm = nc.tensor.matmul(bank[5][:, c], eT[:, k, c], w2a_s[:, :], start=True, stop=True)
                    mm.then_inc(s_e[2], 1)
                if on(2):
                    t, k = i - 2, u % 2
                    pe.wait_ge(s_v[0], count(0, t, 5))
                    if on(3):
                        pe.wait_ge(s_a[2], count(0, t - 1))
                    for j in range(J):
                        mm = nc.tensor.transpose(bank[6][:, j * P:(j + 1) * P], e1[:, k, j, :], ident[:, :])
                    mm.then_inc(s_e[3], 1)
                if on(3):
                    t, k = i - 3, (u - 3) % 2
                    pe.wait_ge(s_a[2], count(0, t))
                    if on(4):
                        pe.wait_ge(s_a[3], count(0, t - 1))
                    nc.tensor.matmul(bank[7][:, :], ws_s[:, 0, :], e1T[:, k, :], start=True, stop=True).then_inc(s_e[4], 1)
                if on(4):
                    t, k = i - 4, u % 2
                    pe.wait_ge(s_a[3], count(0, t))
                    pe.wait_ge(s_a[0], count(0, min(i, NT - 1) if isinstance(i, int) else i))
                    if on(5) and not on(0):
                        pe.wait_ge(s_a[4], count(0, t - 1))
                    for j in range(J):
                        mm = nc.tensor.transpose(bank[3][:, j * P:(j + 1) * P], g1T[:, k, j * P:(j + 1) * P], ident[:, :])
                    mm.then_inc(s_e[5], 1)
                    pe.wait_ge(s_a[1], count(0, min(i - 1, NT - 1) if isinstance(i, int) else i - 1))
                    if on(5) and not on(1):
                        pe.wait_ge(s_a[5], count(0, t - 1))
                    nc.tensor.matmul(bank[4][:, :], ws_s[:, 1, :], g1T[:, k, :], start=True, stop=True).then_inc(s_e[6], 1)
                if on(5):
                    t, k = i - 5, (u - 5) % 2
                    pe.wait_ge(s_a[5], count(0, t))
                    pe.wait_ge(s_v[0], (min(i - 1, NT - 1) if isinstance(i, int) else i - 1) * 5 + 1)
                    if on(6) and not on(1):
                        pe.wait_ge(s_a[6], count(0, t - 1))
                    for j in range(J):
                        mm = nc.tensor.transpose(bank[5][:, j * P:(j + 1) * P], g2T[:, k, j * P:(j + 1) * P], ident[:, :])
                    mm.then_inc(s_e[7], 1)
            pipeline(pe, src_step)
            wait_all(pe, src_end)

            def dst_step(i, u, on):
                if on(0):
                    k = u % 4
                    pe.wait_ge(tg_in[k], slot_count(0, i, k, 4, 128))
                    if on(1):
                        pe.wait_ge(t_a, count(0, i - 1))
                    for j in range(J):
                        mm = nc.tensor.transpose(bank[3][:, j * P:(j + 1) * P], er[:, k, j, 0:D], ident[:, :])
                    mm.then_inc(t_e[0], 1)
                node_pe(pe, 2, i, u, on)
                if on(1):
                    t, k = i - 1, (u - 1) % 2
                    pe.wait_ge(tl_in[k], slot_count(0, t, k, 2))
                    pe.wait_ge(t_v[0], count(0, t))
                    if on(2):
                        pe.wait_ge(t_v[1], count(0, t - 1, 4))
                    for j in range(J):
                        mm = nc.tensor.matmul(bank[4][:, j * P:(j + 1) * P], mrow[:, k, j, :], sel[:, k, j, :],
                                              start=True, stop=True)
                    mm.then_inc(t_e[1], 1)
                if on(2):
                    t, k = i - 2, u % 2
                    pe.wait_ge(t_a, count(0, t))
                    pe.wait_ge(t_v[1], count(0, t, 4))
                    if on(3):
                        pe.wait_ge(t_v[2], count(0, t - 1, 5))
                    for j in range(J):
                        c = slice(j * P, (j + 1) * P)
                        nc.tensor.matmul(bank[5][:, c], eT[:, k, c], w2a_s[:, :], start=True, stop=False)
                        mm = nc.tensor.matmul(bank[5][:, c], g1T[:, k, c], w2b_s[:, :], start=False, stop=True)
                    mm.then_inc(t_e[2], 1)
            pipeline(pe, dst_step)
            wait_all(pe, dst_end)

            for l in range(LAYERS):
                b0 = l * NT

                def a_step(i, u, on, l=l, b0=b0):
                    if l == 0:
                        node_pe(pe, 3, i, u, on)
                    if on(1):
                        t, k = i - 1, (u - 1) % 2
                        pe.wait_ge(al_in[k], slot_count(in_slot(2, k, l), t, k, 2))
                        pe.wait_ge(a_v[1], count(b0, t))
                        if on(2):
                            pe.wait_ge(a_a, count(b0, t - 1))
                        for j in range(J):
                            mm = nc.tensor.matmul(bank[3][:, j * P:(j + 1) * P], r1[:, k, j, :], sel[:, k, j, :],
                                                  start=True, stop=True)
                        mm.then_inc(a_e[0], 1)
                    if on(2):
                        t, k = i - 2, u % 2
                        pe.wait_ge(a_a, count(b0, t))
                        if on(3):
                            pe.wait_ge(a_v[0], count(b0 * 5, t - 1, 5) - 1)
                        for j in range(J):
                            ps = bank[4 + j // 2][:, (j % 2) * (D + 1):(j % 2 + 1) * (D + 1)]
                            nc.tensor.matmul(ps, eT[:, k, j * P:(j + 1) * P], a_s[:, l, :], start=True, stop=False)
                            mm = nc.tensor.matmul(ps, one[0:1, :], arow_s[0:1, l, :], start=False, stop=True)
                        mm.then_inc(a_e[1], 1)
                        if on(3):
                            pe.wait_ge(a_v[2], count(b0, t - 1))
                        for j in range(J):
                            mm = nc.tensor.matmul(bank[6][:, j * P:(j + 1) * P], eT[:, k, j * P:(j + 1) * P],
                                                  ws_s[:, l, :], start=True, stop=True)
                        mm.then_inc(a_e[2], 1)
                pipeline(pe, a_step)
                wait_all(pe, a_end(l))
                for k in range(2):
                    mm = nc.tensor.transpose(bank[0][0:HC, k * P:(k + 1) * P], logit_c[:, k * HC:(k + 1) * HC], ident[:, :])
                mm.then_inc(s_lt, 1)
                for n, (kind, o) in enumerate((("max", vb), ("back", vd), ("add", vb), ("back", vd))):
                    over_chunks_pe(pe, 1 + 4 * l + n, kind, o)
                pe.wait_ge(s_al, l + 1)
                for k in range(2):
                    mm = nc.tensor.transpose(bank[0][:, k * HC:(k + 1) * HC], va[:, k, :], ident[0:HC, 0:HC])
                mm.then_inc(s_at, 1)

                def b_step(i, u, on, l=l, b0=b0):
                    if on(1):
                        t, k = i - 1, (u - 1) % 2
                        by = 48 if l == LAYERS - 1 else 32
                        pe.wait_ge(bl_in[k], slot_count(in_slot(2, k, l, 32), t, k, 2, by))
                        pe.wait_ge(b_v[0], count(b0, t))
                        if on(2):
                            pe.wait_ge(b_v[1], count(b0 * 4, t - 1, 4))
                        for j in range(J):
                            mm = nc.tensor.matmul(bank[3][:, j * P:(j + 1) * P], r1[:, k, j, :], sel[:, k, j, :],
                                                  start=True, stop=True)
                        mm.then_inc(b_e[0], 1)
                    if on(2):
                        t, k = i - 2, u % 2
                        kb = KT if l == LAYERS - 1 else 1
                        pe.wait_ge(b_v[1], count(b0 * 4, t, 4))
                        if on(3):
                            pe.wait_ge(b_v[2], (t - 1) * kb + (b0 + 1))
                        for j in range(J):
                            mm = nc.tensor.matmul(bank[4][:, j * P:(j + 1) * P], g1T[:, k, j * P:(j + 1) * P],
                                                  wv_s[:, l, :], start=True, stop=True)
                        mm.then_inc(b_e[1], 1)
                pipeline(pe, b_step)
                wait_all(pe, b_end(l))

        @block.scalar
        def _(act):
            wait_all(act, prep_end)
            def map_step(i, u, on):
                node_act(act, 0, i, u, on)
                node_sqrt(act, 0, i, u, on)
            pipeline(act, map_step)
            wait_all(act, map_end)

            def src_step(i, u, on):
                if on(0):
                    act.wait_ge(s_e[0], count(0, i))
                    if on(2):
                        act.wait_ge(s_e[2], count(0, i - 2))
                    nc.scalar.activation(eT[:, u % 2, :], bank[3][:, :], ACT.Copy).then_inc(s_a[0], 1)
                node_act(act, 1, i, u, on)
                node_sqrt(act, 1, i, u, on)
                if on(1):
                    act.wait_ge(s_v[0], (i - 1) * 5 + 3)
                    root(emv, ers[:, :], S_sq)
                if on(1):
                    t, k = i - 1, (u - 1) % 2
                    act.wait_ge(s_e[1], count(0, t))
                    if on(3):
                        act.wait_ge(S_out[0][k], slot_count(0, t - 2, k, 2))
                    nc.scalar.activation(mrow[:, k], chunk_rows(bank[4][:, :]), ACT.Relu).then_inc(s_a[1], 1)
                if on(2):
                    t, k = i - 2, u % 2
                    act.wait_ge(s_e[3], count(0, t))
                    if on(4):
                        act.wait_ge(s_e[4], count(0, t - 2))
                    nc.scalar.activation(e1T[:, k, :], bank[6][:, :], ACT.Copy).then_inc(s_a[2], 1)
                if on(3):
                    t, k = i - 3, (u - 3) % 2
                    act.wait_ge(s_e[4], count(0, t))
                    if on(5):
                        act.wait_ge(s_e[6], count(0, t - 2))
                    nc.scalar.activation(g1T[:, k, :], bank[7][:, :], ACT.Relu, bias=bscol_s[:, 0:1]).then_inc(s_a[3], 1)
                if on(4):
                    t, k = i - 4, u % 2
                    act.wait_ge(s_e[5], count(0, t))
                    if on(6):
                        act.wait_ge(S_out[2][k], slot_count(0, t - 2, k, 2))
                    nc.scalar.activation(r1[:, k], chunk_rows(bank[3][:, :]), ACT.Copy).then_inc(s_a[4], 1)
                    act.wait_ge(s_e[6], count(0, t))
                    if on(6):
                        act.wait_ge(s_e[7], count(0, t - 2))
                    nc.scalar.activation(g2T[:, k, :], bank[4][:, :], ACT.Relu, bias=bscol_s[:, 1:2]).then_inc(s_a[5], 1)
                if on(5):
                    t, k = i - 5, (u - 5) % 2
                    act.wait_ge(s_e[7], count(0, t))
                    if on(7):
                        act.wait_ge(S_out[3][k], slot_count(0, t - 2, k, 2))
                    nc.scalar.activation(r2[:, k], chunk_rows(bank[5][:, :]), ACT.Copy).then_inc(s_a[6], 1)
            pipeline(act, src_step)
            wait_all(act, src_end)

            def dst_step(i, u, on):
                node_act(act, 2, i, u, on)
                if on(0):
                    act.wait_ge(t_e[0], count(0, i))
                    if on(2):
                        act.wait_ge(t_e[2], count(0, i - 2))
                    nc.scalar.activation(eT[:, u % 2, :], bank[3][:, :], ACT.Copy).then_inc(t_a, 1)
                node_sqrt(act, 2, i, u, on)
                if on(2):
                    act.wait_ge(t_v[2], (i - 2) * 5 + 3)
                    root(emv, ers[:, :], T_sq)
            pipeline(act, dst_step)
            wait_all(act, dst_end)

            for l in range(LAYERS):
                b0 = l * NT

                def a_step(i, u, on, l=l, b0=b0):
                    if l == 0:
                        node_act(act, 3, i, u, on)
                        node_sqrt(act, 3, i, u, on)
                    if on(1):
                        t, k = i - 1, (u - 1) % 2
                        act.wait_ge(a_e[0], count(b0, t))
                        if on(3):
                            act.wait_ge(a_e[2], count(b0, t - 2))
                        nc.scalar.activation(eT[:, k, :], bank[3][:, :], ACT.Copy).then_inc(a_a, 1)
                pipeline(act, a_step)
                wait_all(act, a_end(l))
                act.wait_ge(s_arg, l + 1)
                nc.scalar.activation(va[:, :, :], va[:, :, :], ACT.Exp).then_inc(s_exp, 1)

                def b_step(i, u, on, l=l, b0=b0):
                    if on(2):
                        t, k = i - 2, u % 2
                        act.wait_ge(b_v[2], count(b0, t))
                        if on(4):
                            act.wait_ge(b_out[k], slot_count(in_slot(2, k, l), t - 2, k, 2))
                        nc.scalar.activation(e1[:, k], mrow[:, k], ACT.Relu).then_inc(b_a, 1)
                if l < LAYERS - 1:
                    pipeline(act, b_step)
                    wait_all(act, b_end(l))

            def out_step(i, u, on):
                if on(2):
                    act.wait_ge(b_v[2], (i - 2) * KT + ((LAYERS - 1) * NT + 4))
                    root(emv, ers[:, :], B_sq)
            pipeline(act, out_step)

        @block.vector
        def _(dve):
            steps = [0]

            def link(op):
                steps[0] += 1
                op.then_inc(s_vl, 1)
                dve.wait_ge(s_vl, steps[0])

            nc.vector.memset(eps_s[:, :], EPS)
            nc.vector.memset(minus[:, :], -1.0).then_inc(s_p0, 1)
            dve.wait_ge(s_seg, 64)
            link(nc.vector.tensor_tensor(va[:, :, :], di[:, :, :], dp[:, :, :], ALU.not_equal))
            link(nc.vector.tensor_tensor(last[:, :, :], di[:, :, :], dn[:, :, :], ALU.not_equal))
            link(nc.vector.tensor_scalar(notstart[:, :, :], va[:, :, :], -1.0, 1.0, ALU.mult, ALU.add))
            link(nc.vector.tensor_scalar(notlast[:, :, :], last[:, :, :], -1.0, 1.0, ALU.mult, ALU.add))
            link(nc.vector.tensor_scalar(nb[:, :, :], va[:, :, :], -BIG, None, ALU.mult))
            for k in range(2):
                link(nc.vector.tensor_tensor_scan(vb[:, k, :], va[:, k, :], va[:, k, :], 0.0, ALU.add, ALU.max))
            link(nc.vector.tensor_copy(ordb[:, :, :], vb[:, :, :]))
            link(nc.vector.tensor_copy(vc[:, :, :], last[:, :, :]))
            link(nc.vector.memset(vc[:, :, P - 1:P], 1.0))
            link(nc.vector.scalar_tensor_tensor(vd[:, :, :], notlast[:, :, :], SKIP, di[:, :, :], ALU.mult, ALU.add))
            link(nc.vector.tensor_scalar(ccol[:, 0:2], vb[:, :, P - 1], 0.0, None, ALU.is_equal))
            link(nc.vector.reduce_max(ccol[:, 2:4], last[:, :, :], mybir.AxisListType.X))
            link(nc.vector.tensor_scalar(ccol[:, 2:4], ccol[:, 2:4], 0.0, None, ALU.is_equal))
            nc.vector.tensor_copy(va[:, :, :], last[:, :, :]).then_inc(s_p1, 1)
            dve.wait_ge(s_wt, 1)
            for l in range(LAYERS):
                nc.vector.tensor_copy(a_s[:, l, :], bank[l][:, 0:D + 1])
                op = nc.vector.tensor_copy(arow_s[0:1, l, :], bank[3 + l][0:1, 0:D + 1])
            op.then_inc(s_wt, 1)
            dve.wait_ge(s_b, 16 * 2 * LAYERS * J)
            link(nc.vector.tensor_copy(b3row_s[:, :, :], brow_s[:, LAYERS - 1]))
            for l, b in enumerate((mrow[:, 0], mrow[:, 1], r1[:, 0])):
                link(nc.vector.tensor_tensor(brow_s[:, l], brow_s[:, l], b, ALU.add))
            dve.wait_ge(s_wt, 3)
            link(nc.vector.tensor_copy(ordcol[:, :], bank[0][:, 0:NC]))
            link(nc.vector.tensor_copy(endcol[:, :], bank[1][:, 0:NC]))
            nc.vector.tensor_copy(idx_all[:, :], bank[2][:, 0:NC]).then_inc(s_p2, 1)
            link(nc.vector.tensor_copy(nostart_row[:, :], bank[6][0:1, 0:NC]))
            link(nc.vector.tensor_copy(nolast_row[:, :], bank[6][0:1, NC:2 * NC]))
            link(nc.vector.tensor_scalar(nb_row[:, :], nostart_row[:, :], -1.0, BIG, ALU.add, ALU.mult))
            dve.wait_ge(s_iota, 1)
            link(nc.vector.tensor_copy(vd[:, :, :], slot_i[:, :, :]))
            nc.vector.tensor_tensor(vc[:, :, :], vd[:, :, :], last[:, :, :], ALU.mult).then_inc(s_fixi, 1)
            dve.wait_ge(s_fixi, 1)
            over_chunks_dve(dve, 0, "back", notlast, vc, va)
            link(nc.vector.tensor_copy(fixidx[:, :], va[:, :, P - 1]))
            dve.wait_ge(s_ordin, 16)
            nc.vector.tensor_scalar(firstm[:, :], ordrow[:, :], 0.0, None, ALU.is_equal).then_inc(s_prep, 1)
            wait_all(dve, prep_end)

            def map_step(i, u, on):
                node_dve1(dve, 0, i, u, on)
                node_dve2(dve, 0, i, u, on)
            pipeline(dve, map_step)
            wait_all(dve, map_end)

            def src_step(i, u, on):
                node_dve1(dve, 1, i, u, on)
                if on(1):
                    t = i - 1
                    after(dve, s_v[0], t * 5)
                    dve.wait_ge(s_e[2], count(0, t))
                    nc.vector.scalar_tensor_tensor(ey[:, :, :], chunk_rows(bank[5][:, :]), 0.0, er[:, (u - 1) % 4, :, 0:D],
                                                   ALU.max, ALU.add).then_inc(s_v[0], 1)
                    moments(dve, ey, estat, emv, s_v[0], t * 5 + 1)
                node_dve2(dve, 1, i, u, on)
                if on(1):
                    t, k = i - 1, (u - 1) % 2
                    dve.wait_ge(S_sq, count(0, t))
                    if on(3):
                        dve.wait_ge(S_out[1][k], slot_count(0, t - 2, k, 2))
                        dve.wait_ge(s_e[3], count(0, t - 2))
                    normalise(dve, ey, e1[:, k], emv, ers[:, :], eri[:, :], s_v[0], t * 5 + 3)
            pipeline(dve, src_step)
            wait_all(dve, src_end)

            def dst_step(i, u, on):
                if on(0):
                    if on(2):
                        dve.wait_ge(t_e[1], count(0, i - 2))
                    select(i, u % 2, None, t_v[0])
                node_dve1(dve, 2, i, u, on)
                if on(1):
                    t, k = i - 1, (u - 1) % 2
                    dve.wait_ge(t_e[1], count(0, t))
                    if on(2):
                        dve.wait_ge(t_v[1], t * 4)
                    if on(3):
                        dve.wait_ge(t_e[2], count(0, t - 2))
                    carry(dve, t, k, bank[4], t_v[1], t * 4)
                if on(2):
                    t, k = i - 2, u % 2
                    after(dve, t_v[2], t * 5)
                    dve.wait_ge(t_e[2], count(0, t))
                    nc.vector.scalar_tensor_tensor(ey[:, :, :], chunk_rows(bank[5][:, :]), 0.0, er[:, (u - 2) % 4, :, 0:D],
                                                   ALU.max, ALU.add).then_inc(t_v[2], 1)
                    moments(dve, ey, estat, emv, t_v[2], t * 5 + 1)
                if on(2):
                    t, k = i - 2, u % 2
                    dve.wait_ge(T_sq, count(0, t))
                    if on(4):
                        dve.wait_ge(t_out[k], slot_count(0, t - 2, k, 2))
                    normalise(dve, ey, e1[:, k], emv, ers[:, :], eri[:, :], t_v[2], t * 5 + 3)
                node_dve2(dve, 2, i, u, on)
            pipeline(dve, dst_step)
            wait_all(dve, dst_end)
            dve.wait_ge(s_fd, 16)
            nc.vector.tensor_scalar(alpha_c[:, :], slot_all[:, :], float(NS + 1), None, ALU.add).then_inc(s_fc, 1)
            dve.wait_ge(s_fc, 1)
            nc.vector.scalar_tensor_tensor(alpha_c[:, :], logit_c[:, :], 0.0, alpha_c[:, :], ALU.is_lt, ALU.mult).then_inc(s_fc, 1)
            dve.wait_ge(s_fc, 2)
            nc.vector.tensor_tensor(idx_all[:, :], alpha_c[:, :], logit_c[:, :], ALU.add).then_inc(s_fc, 1)
            dve.wait_ge(s_fc, 3)

            for l in range(LAYERS):
                b0 = l * NT

                def a_step(i, u, on, l=l, b0=b0):
                    if on(0):
                        if on(2):
                            dve.wait_ge(a_e[0], count(b0, i - 2))
                        select(i, u % 2, endcol, a_v[1])
                    if l == 0:
                        node_dve1(dve, 3, i, u, on)
                    if on(2):
                        t, k = i - 2, u % 2
                        k4 = (u - 2) % 4
                        at = t * 5 + b0 * 5
                        dve.wait_ge(ag_in[k4], slot_count(in_slot(4, k4, l, 64), t, k4, 4, 64))
                        dve.wait_ge(a_e[1], count(b0, t))
                        after(dve, a_v[0], at)
                        for j in range(J):
                            nc.vector.tensor_tensor_reduce(
                                out=junk[:, j, :], in0=bank[4 + j // 2][:, (j % 2) * (D + 1):(j % 2 + 1) * (D + 1)],
                                in1=er[:, k4, j, :], scale=float(D) ** -0.5, scalar=0.0, op0=ALU.mult, op1=ALU.add,
                                accum_out=lg[:, k, j:j + 1]).then_inc(a_v[0], 1)
                        dve.wait_ge(a_v[0], at + 4)
                        nc.vector.tensor_copy(logit_c[:, bass.ds(t * J, J)], lg[:, k, :]).then_inc(a_v[0], 1)
                        dve.wait_ge(a_e[2], count(b0, t))
                        if on(4):
                            dve.wait_ge(as_out[k], slot_count(in_slot(2, k, l), t - 2, k, 2))
                        nc.vector.tensor_tensor(mrow[:, k], chunk_rows(bank[6][:, :]), brow_s[:, l], ALU.add).then_inc(
                            a_v[2], 1)
                    if l == 0:
                        node_dve2(dve, 3, i, u, on)
                pipeline(dve, a_step)
                wait_all(dve, a_end(l))
                dve.wait_ge(s_lt, l + 1)
                q = 1 + 4 * l
                link(nc.vector.tensor_copy(va[:, :, :], bank[0][0:HC, 0:2 * P].rearrange("c (k e) -> c k e", k=2)))
                over_chunks_dve(dve, q, "max", nb, va, vb)
                link(nc.vector.tensor_tensor(vc[:, :, :], vb[:, :, :], last[:, :, :], ALU.mult))
                over_chunks_dve(dve, q + 1, "back", notlast, vc, vd)
                nc.vector.tensor_tensor(va[:, :, :], va[:, :, :], vd[:, :, :], ALU.subtract).then_inc(s_arg, 1)
                dve.wait_ge(s_exp, l + 1)
                over_chunks_dve(dve, q + 2, "add", notstart, va, vb)
                link(nc.vector.tensor_tensor(vc[:, :, :], vb[:, :, :], last[:, :, :], ALU.mult))
                over_chunks_dve(dve, q + 3, "back", notlast, vc, vd)
                link(nc.vector.tensor_scalar(vd[:, :, :], vd[:, :, :], 1e-16, None, ALU.max))
                link(nc.vector.reciprocal(vc[:, :, :], vd[:, :, :]))
                nc.vector.tensor_tensor(va[:, :, :], va[:, :, :], vc[:, :, :], ALU.mult).then_inc(s_al, 1)
                dve.wait_ge(s_at, l + 1)
                link(nc.vector.tensor_copy(alpha_c[:, :], bank[0][:, 0:NC]))

                def b_step(i, u, on, l=l, b0=b0):
                    tail = l == LAYERS - 1
                    if on(0):
                        if on(2):
                            dve.wait_ge(b_e[0], count(b0, i - 2))
                        select(i, u % 2, alpha_c, b_v[0])
                    if on(1):
                        t, k = i - 1, (u - 1) % 2
                        dve.wait_ge(b_e[0], count(b0, t))
                        if on(2):
                            dve.wait_ge(b_v[1], t * 4 + b0 * 4)
                        if on(3):
                            dve.wait_ge(b_e[1], count(b0, t - 2))
                        carry(dve, t, k, bank[3], b_v[1], t * 4 + b0 * 4)
                    if on(2):
                        t, k = i - 2, u % 2
                        dve.wait_ge(b_e[1], count(b0, t))
                        if not tail:
                            if on(4):
                                dve.wait_ge(b_a, count(b0, t - 2))
                            dve.wait_ge(bl_in[k], slot_count(in_slot(2, k, l, 32), t, k, 2, 32))
                            nc.vector.tensor_tensor(mrow[:, k], chunk_rows(bank[4][:, :]), r2[:, k], ALU.add).then_inc(
                                b_v[2], 1)
                        else:
                            at = t * KT + b0
                            after(dve, b_v[2], at)
                            dve.wait_ge(bl_in[k], slot_count(in_slot(2, k, l, 32), t, k, 2, 48))
                            nc.vector.tensor_tensor(mrow[:, 0], chunk_rows(bank[4][:, :]), r2[:, k], ALU.add).then_inc(
                                b_v[2], 1)
                            dve.wait_ge(b_v[2], at + 1)
                            nc.vector.tensor_tensor(ey[:, :, :], mrow[:, 0], x1e[:, k], ALU.add).then_inc(b_v[2], 1)
                            if on(4):
                                dve.wait_ge(s_fin[k], slot_count(0, t - 2, k, 2, 64))
                            dve.wait_ge(b_v[2], at + 2)
                            moments(dve, ey, estat, emv, b_v[2], at + 2)
                            dve.wait_ge(B_sq, count(0, t))
                            normalise(dve, ey, e1[:, k], emv, ers[:, :], eri[:, :], b_v[2], at + 4)
                pipeline(dve, b_step)
                wait_all(dve, b_end(l))


def kernel(**inputs):
    import numpy as _np
    import concourse.bacc as _bacc
    from concourse import mybir as _mybir
    from concourse.bass_utils import run_bass_kernel_spmd as _run

    get = {k: _np.ascontiguousarray(v) for k, v in inputs.items()}
    pad = NS - N_EDGES

    def tiles(v):
        return _np.ascontiguousarray(v.reshape(NT, J, P).transpose(0, 2, 1))

    src, dst = get["src"], get["dst"]
    fill = _np.zeros(pad, _np.int32)
    arrays = {
        "x": get["x"],
        "xsrc_idx": tiles(_np.concatenate([src, fill])),
        "xdst_idx": tiles(_np.concatenate([dst, fill])),
        "slot_ids": tiles(_np.arange(NS, dtype=_np.float32)),
        "dst_pad": _np.concatenate([_np.full(1, -1, _np.int32), dst, _np.full(pad, N_NODES, _np.int32),
                                    _np.full(1, -2, _np.int32)]),
        "wT": _np.concatenate([_np.concatenate([get["edge_attr_3"].T, _np.ones((1, N_EDGES), _np.float32)]),
                               _np.zeros((4, pad), _np.float32)], axis=1),
        "w1a": get["L0_gnn_W1"][:, :D].T,
        "w1b": _np.concatenate([get["L0_gnn_W1"][:, D:].T, get["L0_gnn_b1"][None, :]]),
        "w2a": get["L0_gnn_W2"][:, :D].T,
        "w2b": get["L0_gnn_W2"][:, D:].T,
        "wqT": get["L1_gnn_Wq"].transpose(2, 0, 1),
        "wkT": _np.concatenate([get["L1_gnn_Wk"].transpose(2, 0, 1), get["L1_gnn_bk"].T[:, :, None]], axis=2),
        "bq": get["L1_gnn_bq"].T,
        "wv": get["L1_gnn_Wv"].transpose(1, 0, 2),
        "bv": get["L1_gnn_bv"],
        "ws": get["L1_gnn_Ws"].transpose(1, 0, 2),
        "bs": get["L1_gnn_bs"],
        "bs_col": get["L1_gnn_bs"].T,
    }
    nc = _bacc.Bacc("TRN2", target_bir_lowering=False, num_devices=1)
    given, args = {}, {}
    for name, a in arrays.items():
        a = _np.ascontiguousarray(a)
        given[f"in_{name}"] = a
        args[name] = nc.dram_tensor(f"in_{name}", a.shape, _mybir.dt.from_np(a.dtype), kind="ExternalInput").ap()
    args["out"] = nc.dram_tensor("out_rows", (N_NODES, D), _mybir.dt.float32, kind="ExternalOutput").ap()
    gnn_program(nc, **args)
    return _run(nc, [given], core_ids=[0]).results[0]["out_rows"]
```

```python
import numpy as np
import concourse.bass as bass
from concourse import mybir
from concourse.alu_op_type import AluOpType as ALU
from contextlib import ExitStack

FP32 = mybir.dt.float32
BF16 = mybir.dt.bfloat16
I32 = mybir.dt.int32
U8 = mybir.dt.uint8
ACT = mybir.ActivationFunctionType

N_NODES, N_EDGES, D = 100000, 25000, 128
P = 128
J = 4
T = P * J
NT = -(-N_EDGES // T)
NC = NT * J
NS = NC * P
HC = NC // 2
LAYERS = 3
DENSE_TILES = -(-N_NODES // T)
UNROLL = 4
SMIN, SMAX = -2, 8
LO = SMAX
HI = LO + UNROLL * ((NT + SMIN - LO) // UNROLL)
SPLIT = 96
SKIP_AT = LAYERS * (D + 1)
LAST_AT = SKIP_AT + LAYERS * D
NBIAS = LAST_AT + D
BIG = 1.0e30
EPS = 1e-5
SKIP = 1.0e6


def gnn_program(nc, x, xsrc_idx, xdst_idx, slot_ids, dst_pad, wT, w1a, w1b, w2a, w2b,
                wqT, wkT, bq, wv, bv, ws, bs, bs_col, out):
    ctx = ExitStack()
    with ctx:
        def sb(name, shape, dt=FP32):
            return ctx.enter_context(nc.sbuf_tensor(name, shape, dt))

        def pb(name, shape=(P, 512), dt=FP32):
            return ctx.enter_context(nc.psum_tensor(name, list(shape), dt))

        def sem(name):
            return ctx.enter_context(nc.semaphore(name))

        U = [nc.dram_tensor(f"u{l}", (2 * NS, D), FP32).ap() for l in range(LAYERS)]
        msg_d = nc.dram_tensor("msg_d", (NS, D), FP32).ap()
        hs_d = nc.dram_tensor("hs_d", (NS, D), FP32).ap()
        skip_d = nc.dram_tensor("skip_d", (NS, D), FP32).ap()
        map_d = nc.dram_tensor("map_d", (N_NODES, 1), FP32).ap()
        found_d = nc.dram_tensor("found_d", (NT, P, J), FP32).ap()
        srcslot_d = nc.dram_tensor("srcslot_d", (NT, P, J), I32).ap()
        scat_d = nc.dram_tensor("scat_d", (NT, P, J), I32).ap()
        ord_d = nc.dram_tensor("ord_d", (1, NS), U8).ap()

        ident = sb("ident", [P, P])
        one = sb("one", [1, P])
        w1a_s, w2a_s, w2b_s = sb("w1a_s", [P, D]), sb("w2a_s", [P, D]), sb("w2b_s", [P, D])
        w1b_s = sb("w1b_s", [4, D])
        ws_s, wv_s = sb("ws_s", [P, LAYERS, D]), sb("wv_s", [P, LAYERS, D])
        a_s = sb("a_s", [P, LAYERS, D + 1])
        bscol_s = sb("bscol_s", [P, LAYERS])
        biases = sb("biases", [SPLIT, NBIAS], BF16)
        parts = sb("parts", [SPLIT, P], BF16)
        ordrow = sb("ordrow", [P, NS], U8)
        firstm = sb("firstm", [P, NS], U8)
        ordcol = sb("ordcol", [P, NC])
        endcol = sb("endcol", [P, NC])
        logit_c = sb("logit_c", [P, NC])
        alpha_c = sb("alpha_c", [P, NC])
        h = [HC, 2, P]
        nb, notstart, last, notlast = sb("nb", h), sb("notstart", h), sb("last", h), sb("notlast", h)
        va, vb, vc, vd = sb("va", h), sb("vb", h), sb("vc", h), sb("vd", h)
        incol = sb("incol", [HC, 2])
        nostart_row, nb_row, nolast_row = sb("nostart_row", [1, NC]), sb("nb_row", [1, NC]), sb("nolast_row", [1, NC])
        crow = sb("crow", [1, NC + 1])
        fixidx = sb("fixidx", [HC, 2], I32)
        fixrow = sb("fixrow", [HC, 2, D])
        ccol = sb("ccol", [HC, 4])
        xr = sb("xr", [P, 4, J, D])
        xT = sb("xT", [P, 2, T])
        yb = sb("yb", [P, J, D])
        x1 = sb("x1", [P, 4, J, D])
        x1T = sb("x1T", [P, 2, T])
        h1T = sb("h1T", [P, 2, T])
        h2T = sb("h2T", [P, 2, T])
        zb = sb("zb", [P, 2, J, D])
        ob = sb("ob", [P, 2, J, D])
        stat = sb("stat", [P, 2, J, 6])
        mv = sb("mv", [P, 2, J, 2])
        rs, ri = sb("rs", [P, 2, J]), sb("ri", [P, 2, 2, J])
        fbias = sb("fbias", [P, 2, J])
        eps_s = sb("eps_s", [P, 1])
        gi = sb("gi", [P, 4, J], I32)
        gm = sb("gm", [P, 4, J], I32)
        slotv = sb("slotv", [P, 4, J])
        er = sb("er", [P, 4, J, D + 1])
        eT = sb("eT", [P, 2, T])
        ey = sb("ey", [P, 2, J, D])
        e1 = sb("e1", [P, 2, J, D])
        e1T = sb("e1T", [P, 2, T])
        g1T = sb("g1T", [P, 2, T])
        g2T = sb("g2T", [P, 2, T])
        rr = sb("rr", [P, 4, J, D])
        r1, r2 = rr[:, 0:2], rr[:, 2:4]
        mrow = sb("mrow", [P, 2, J, D])
        sel = sb("sel", [P, 2, J, P])
        wt = sb("wt", [4, 2, T])
        found = sb("found", [P, 2, J])
        zcol = sb("zcol", [P, 1])
        di, dp, dn, slot_i = sb("di", h, I32), sb("dp", h, I32), sb("dn", h, I32), sb("slot_i", h, I32)
        ordb = sb("ordb", h, U8)
        idx_all = sb("idx_all", [P, NC], I32)
        slot_all = sb("slot_all", [P, NC])
        wqT_s, wkT_s = sb("wqT_s", [P, LAYERS, D]), sb("wkT_s", [P, LAYERS, D + 1])
        bq_s = sb("bq_s", [P, LAYERS])
        minus = sb("minus", [P, 800])
        lg = sb("lg", [P, 2, J])
        junk = sb("junk", [P, J, D + 1])
        estat = sb("estat", [P, J, 6])
        emv = sb("emv", [P, J, 2])
        ers, eri, ebias = sb("ers", [P, J]), sb("eri", [P, 2, J]), sb("ebias", [P, 2, J])

        bank = [pb(f"bank{k}") for k in range(8)]

        s_w, s_b, s_seg, s_mapset, s_id, s_iota = (sem(n) for n in ("s_w", "s_b", "s_seg", "s_mapset", "s_id", "s_iota"))
        x_in = [sem(f"x_in{k}") for k in range(4)]
        o_out = [sem(f"o_out{k}") for k in range(2)]
        dA, dB, dC, dD, dE, dF = (sem(f"pe_d{n}") for n in "ABCDEF")
        xT_r, x1T_r, h1T_r, h2T_r = (sem(n) for n in ("xT_r", "x1T_r", "h1T_r", "h2T_r"))
        cN = sem("cN")
        sqN, oN = sem("sqN"), sem("oN")
        KN, KT = 6, 6
        Z, Y, X1 = 1, 2, 6

        block = ctx.enter_context(nc.Block())

        def pipeline(eng, step):
            for i in range(SMIN, LO):
                step(i, i % UNROLL, lambda s, i=i: 0 <= i - s < NT)
            with eng.Fori(LO // UNROLL, HI // UNROLL) as r:
                for u in range(UNROLL):
                    step(r * UNROLL + u, u, lambda s: True)
            for i in range(HI, NT + SMAX):
                step(i, i % UNROLL, lambda s, i=i: 0 <= i - s < NT)

        def settle(eng):
            eng.sem_inc(s_passed, 1)

        def after(eng, chain, n):
            if not (isinstance(n, int) and n <= 0):
                eng.wait_ge(chain, n)

        def count(base, t, k=1):
            return t * k + (base + k)

        def slot_count(base, t, u, ring, by=16):
            return (t - u) * (by // ring) + (base + by)

        def in_slot(ring, u, phases, by=16):
            return by * phases * len(range(u, NT, ring))

        def bias_rows(at, n, copies):
            return biases[:, at:at + n].unsqueeze(1).broadcast_to([SPLIT, copies, n])

        NODE_PHASES = DENSE_TILES // NT

        def node_row(ph, t):
            return (ph * NT + t) * T if not isinstance(t, int) else min((ph * NT + t) * T, N_NODES - T)

        def rows_of(a, r0):
            return a[bass.ds(r0, T), :].rearrange("(p j) f -> p j f", p=P)

        def first_part(ph, t, step):
            return t * KN + (ph * (NT + 4) * KN + step)

        def last_part(ph, t, step):
            return t * KN + ((ph * (NT + 4) + 4) * KN + step)

        def node_load(sp, ph, i, u, on):
            if on(-2):
                t, k = i + 2, (u + 2) % 4
                if not isinstance(t, int) or t >= 4:
                    sp.wait_ge(cN, first_part(ph, t - 4, Y))
                sp.dma_start(xr[:, k], rows_of(x, node_row(ph, t))).then_inc(x_in[k], 16)

        def node_store(sp, ph, i, u, on):
            if on(7):
                t, k = i - 7, (u - 7) % 2
                sp.wait_ge(oN, count(ph * NT, t))
                if isinstance(t, int) and ph * NT + t == DENSE_TILES - 1:
                    sp.wait_ge(o_out[1 - k], in_slot(2, 1 - k, ph + 1))
                sp.dma_start(rows_of(out, node_row(ph, t)), ob[:, k]).then_inc(o_out[k], 16)

        def node_pe(pe, ph, i, u, on):
            b0 = ph * NT
            if on(5):
                t, k = i - 5, (u - 5) % 2
                pe.wait_ge(h2T_r, count(b0, t))
                pe.wait_ge(x1T_r, count(b0, min(i - 3, NT - 1) if isinstance(i, int) else i - 3))
                if on(6) and not on(3):
                    pe.wait_ge(cN, last_part(ph, t - 1, Z))
                nc.tensor.matmul(bank[2][:, :].rearrange("p (j f) -> p j f", j=J), parts[:, :],
                                 bias_rows(LAST_AT, D, J), start=True, stop=False)
                for j in range(J):
                    mm = nc.tensor.matmul(bank[2][:, j * P:(j + 1) * P], h2T[:, k, j * P:(j + 1) * P], ws_s[:, 2, :],
                                          start=False, stop=j == J - 1)
                mm.then_inc(dF, 1)
            if on(0):
                t, k = i, u % 4
                pe.wait_ge(x_in[k], slot_count(in_slot(4, k, ph), t, k, 4))
                if on(4):
                    pe.wait_ge(h1T_r, count(b0, i - 4))
                elif on(1):
                    pe.wait_ge(xT_r, count(b0, i - 1))
                for j in range(J):
                    mm = nc.tensor.transpose(bank[0][:, j * P:(j + 1) * P], xr[:, k, j, :], ident[:, :])
                mm.then_inc(dA, 1)
            if on(1):
                t, k = i - 1, (u - 1) % 2
                pe.wait_ge(xT_r, count(b0, t))
                if on(5):
                    pe.wait_ge(h2T_r, count(b0, i - 5))
                elif on(2):
                    pe.wait_ge(cN, first_part(ph, i - 2, Y))
                for j in range(J):
                    mm = nc.tensor.matmul(bank[1][:, j * P:(j + 1) * P], xT[:, k, j * P:(j + 1) * P], w2a_s[:, :],
                                          start=True, stop=True)
                mm.then_inc(dB, 1)
            if on(2):
                t, k = i - 2, (u - 2) % 4
                pe.wait_ge(cN, first_part(ph, t, X1))
                if on(5):
                    pe.wait_ge(cN, last_part(ph, i - 5, Z))
                elif on(3):
                    pe.wait_ge(x1T_r, count(b0, i - 3))
                for j in range(J):
                    mm = nc.tensor.transpose(bank[2][:, j * P:(j + 1) * P], x1[:, k, j, :], ident[:, :])
                mm.then_inc(dC, 1)
            if on(3):
                t, k = i - 3, (u - 3) % 2
                pe.wait_ge(x1T_r, count(b0, t))
                pe.wait_ge(xT_r, count(b0, min(i, NT - 1) if isinstance(i, int) else i))
                if on(4) and not on(0):
                    pe.wait_ge(h1T_r, count(b0, t - 1))
                nc.tensor.matmul(bank[0][:, :], ws_s[:, 0, :], x1T[:, k, :], start=True, stop=True).then_inc(dD, 1)
            if on(4):
                t, k = i - 4, (u - 4) % 2
                pe.wait_ge(h1T_r, count(b0, t))
                pe.wait_ge(cN, first_part(ph, min(i - 1, NT - 1) if isinstance(i, int) else i - 1, Y))
                if on(5) and not on(1):
                    pe.wait_ge(h2T_r, count(b0, t - 1))
                nc.tensor.matmul(bank[1][:, :], ws_s[:, 1, :], h1T[:, k, :], start=True, stop=True).then_inc(dE, 1)

        def node_act(act, ph, i, u, on):
            b0 = ph * NT
            if on(0):
                t, k = i, u % 2
                act.wait_ge(dA, count(b0, t))
                if on(2):
                    act.wait_ge(dB, count(b0, t - 2))
                nc.scalar.activation(xT[:, k, :], bank[0][:, :], ACT.Copy).then_inc(xT_r, 1)
            if on(2):
                t, k = i - 2, (u - 2) % 2
                act.wait_ge(dC, count(b0, t))
                if on(4):
                    act.wait_ge(dD, count(b0, t - 2))
                nc.scalar.activation(x1T[:, k, :], bank[2][:, :], ACT.Copy).then_inc(x1T_r, 1)
            if on(3):
                t, k = i - 3, (u - 3) % 2
                act.wait_ge(dD, count(b0, t))
                if on(5):
                    act.wait_ge(dE, count(b0, t - 2))
                nc.scalar.activation(h1T[:, k, :], bank[0][:, :], ACT.Relu, bias=bscol_s[:, 0:1]).then_inc(h1T_r, 1)
            if on(4):
                t, k = i - 4, (u - 4) % 2
                act.wait_ge(dE, count(b0, t))
                if on(6):
                    act.wait_ge(dF, count(b0, t - 2))
                nc.scalar.activation(h2T[:, k, :], bank[1][:, :], ACT.Relu, bias=bscol_s[:, 1:2]).then_inc(h2T_r, 1)

        def node_out(act, ph, i, u, on):
            if on(6):
                t, k = i - 6, (u - 6) % 2
                act.wait_ge(cN, last_part(ph, t, KN))
                if on(8):
                    act.wait_ge(o_out[k], slot_count(in_slot(2, k, ph), t - 2, k, 2))
                for j in range(J):
                    op = nc.scalar.activation(ob[:, k, j, :], zb[:, k, j, :], ACT.Identity,
                                              scale=ri[:, (u - 1) % 2, 0, j:j + 1], bias=fbias[:, k, j:j + 1])
                op.then_inc(oN, 1)

        def moments(dve, rows, chain, at):
            dve.wait_ge(chain, at)
            for src, st, m in rows:
                for j in range(J):
                    op = nc.vector.bn_stats(st[:, j, :], src[:, j, :])
            op.then_inc(chain, 1)
            dve.wait_ge(chain, at + 1)
            settle(dve)
            for src, st, m in rows:
                for j in range(J):
                    op = nc.vector.bn_aggr(m[:, j, :], st[:, j, :])
            op.then_inc(chain, 1)

        def root(variance, r, done):
            nc.scalar.activation(r, variance, ACT.Sqrt, bias=eps_s[:, 0:1]).then_inc(done, 1)

        def minus_mean(out, m, inv):
            return nc.vector.scalar_tensor_tensor(out, m[:, :, 0], -1.0, inv, ALU.mult, ALU.mult)

        def halves(on):
            return slice(0 if on(5) else 1, 2 if on(1) else 1)

        def node_sqrt(act, ph, i, u, on):
            if on(1) or on(5):
                act.wait_ge(cN, first_part(ph, i - 1, 4))
                root(mv[:, halves(on), :, 1], rs[:, halves(on)], sqN)

        def node_dve1(dve, ph, i, u, on):
            b0 = ph * NT
            if not (on(1) or on(5)):
                return
            at = first_part(ph, i - 1, 0)
            after(dve, cN, at)
            rows = []
            if on(5):
                t, k4, k2 = i - 5, (u - 5) % 4, (u - 5) % 2
                dve.wait_ge(dF, count(b0, t))
                if on(7):
                    dve.wait_ge(oN, count(b0, t - 2))
                nc.vector.tensor_tensor(zb[:, k2], bank[2][:, :].rearrange("p (j f) -> p j f", j=J),
                                        x1[:, k4], ALU.add).then_inc(cN, 1)
                rows.append((zb[:, k2], stat[:, 0], mv[:, 0]))
            else:
                dve.sem_inc(cN, 1)
            if on(1):
                dve.wait_ge(dB, count(b0, i - 1))
                nc.vector.scalar_tensor_tensor(yb[:, :, :], bank[1][:, :].rearrange("p (j f) -> p j f", j=J), 0.0,
                                               xr[:, (u - 1) % 4], ALU.max, ALU.add).then_inc(cN, 1)
                rows.append((yb, stat[:, 1], mv[:, 1]))
            else:
                dve.wait_ge(cN, at + 1)
                dve.sem_inc(cN, 1)
            moments(dve, rows, cN, at + 2)

        def node_dve2(dve, ph, i, u, on):
            if not (on(1) or on(5)):
                return
            at, r = first_part(ph, i - 1, 0), u % 2
            dve.wait_ge(sqN, count(ph * (NT + 4), i - 1))
            nc.vector.reciprocal(ri[:, r, halves(on)], rs[:, halves(on)]).then_inc(cN, 1)
            dve.wait_ge(cN, at + 5)
            if on(5):
                op = minus_mean(fbias[:, (u - 5) % 2], mv[:, 0], ri[:, r, 0])
            if on(1):
                for j in range(J):
                    op = nc.vector.tensor_scalar(x1[:, (u - 1) % 4, j, :], yb[:, j, :], mv[:, 1, j, 0:1],
                                                 ri[:, r, 1, j:j + 1], ALU.subtract, ALU.mult)
            op.then_inc(cN, 1)

        def edge_rows(a, t, base=0):
            return a[bass.ds(t * T + base, T), :].rearrange("(j p) f -> p j f", p=P)


        i_in = [sem(f"i_in{k}") for k in range(4)]
        m_out = [sem(f"m_out{k}") for k in range(4)]
        g_in = [sem(f"g_in{k}") for k in range(4)]
        f_in = [sem(f"f_in{k}") for k in range(2)]
        f_out = [sem(f"f_out{k}") for k in range(2)]
        w_in = [sem(f"w_in{k}") for k in range(2)]
        S_out = [[sem(f"S_out{n}{k}") for k in range(2)] for n in range(4)]
        s_e, s_a, s_v = ([sem(f"S_{w}{n}") for n in range(m)] for w, m in (("pe", 8), ("act", 7), ("dve", 1)))
        ti_in = [sem(f"ti_in{k}") for k in range(4)]
        tg_in = [sem(f"tg_in{k}") for k in range(4)]
        rows_in = [sem(f"rows_in{k}") for k in range(4)]
        t_out = [sem(f"t_out{k}") for k in range(2)]
        t_e, t_v = ([sem(f"T_{w}{n}") for n in range(3)] for w in ("pe", "dve"))
        t_a = sem("t_a")
        ai_in = [sem(f"ai_in{k}") for k in range(4)]
        ag_in = [sem(f"ag_in{k}") for k in range(4)]
        ah_out = [sem(f"ah_out{k}") for k in range(4)]
        as_out = [sem(f"as_out{k}") for k in range(2)]
        a_e, a_v = ([sem(f"A_{w}{n}") for n in range(m)] for w, m in (("pe", 3), ("dve", 2)))
        a_a = sem("a_a")
        b_out = [sem(f"b_out{k}") for k in range(2)]
        b_e, b_v = ([sem(f"B_{w}{n}") for n in range(m)] for w, m in (("pe", 2), ("dve", 3)))
        b_a = sem("b_a")
        bi_in = [sem(f"bi_in{k}") for k in range(4)]
        s_tail, s_row, s_crow, s_col, s_chain = (sem(n) for n in ("s_tail", "s_row", "s_crow", "s_col", "s_chain"))
        s_lt, s_exp, s_al, s_at, s_arg = (sem(n) for n in ("s_lt", "s_exp", "s_al", "s_at", "s_arg"))
        s_p0, s_p1, s_p2, s_ordout, s_ordin, s_scout = (sem(n) for n in ("s_p0", "s_p1", "s_p2", "s_ordout", "s_ordin", "s_scout"))
        s_prep, s_fixi, s_fixg, s_fixw, s_fd, s_fc, s_fo, s_wt = (sem(n) for n in (
            "s_prep", "s_fixi", "s_fixg", "s_fixw", "s_fd", "s_fc", "s_fo", "s_wt"))
        s_fin = [sem(f"s_fin{k}") for k in range(2)]
        s_vl = sem("s_vl")
        s_passed = sem("s_passed")
        e_sq = sem("e_sq")
        e_o = sem("e_o")
        a_k = sem("a_k")

        def chunk_rows(v):
            return v.rearrange("p (j f) -> p j f", j=J)

        def wait_all(eng, pairs):
            for s, n in pairs:
                eng.wait_ge(s, n)

        def node_end(ph):
            return [(o_out[k], in_slot(2, k, ph + 1)) for k in range(2)]

        prep_end = [(s_w, 160), (s_p0, 2), (s_prep, 1), (s_ordin, 16), (s_scout, 16), (s_mapset, 16)]
        map_end = [(m_out[k], in_slot(4, k, 1, 64)) for k in range(4)] + node_end(0)
        src_end = [(q[k], in_slot(2, k, 1)) for q in S_out for k in range(2)] + node_end(1)
        dst_end = [(q[k], in_slot(2, k, 1)) for q in (t_out, f_out) for k in range(2)] + node_end(2)

        def a_end(l):
            return ([(ah_out[k], in_slot(4, k, l + 1)) for k in range(4)]
                    + [(as_out[k], in_slot(2, k, l + 1)) for k in range(2)]
                    + [(a_v[0], 5 * NT * (l + 1))] + (node_end(3) if l == 0 else []))

        def b_end(l):
            return ([(b_out[k], in_slot(2, k, l + 1)) for k in range(2)] if l < LAYERS - 1 else [])

        def select(t, k, weight, done):
            for j in range(J):
                cols = bass.ds(t * T + j * P, P)
                c = bass.ds(t * J + j, 1)
                if weight is None:
                    op = nc.vector.tensor_scalar(sel[:, k, j, :], ordrow[:, cols], ordcol[:, c], None, ALU.is_equal)
                else:
                    op = nc.vector.tensor_scalar(sel[:, k, j, :], ordrow[:, cols], ordcol[:, c], weight[:, c],
                                                 ALU.is_equal, ALU.mult)
            op.then_inc(done, 1)

        def carry(dve, t, k, ps, chain, at):
            for j in range(J):
                if j:
                    dve.wait_ge(chain, at + j)
                before = g1T[:, k, j * P - 1:j * P] if j else g1T[:, 1 - k, T - 1:T]
                if isinstance(t, int) and t == 0 and j == 0:
                    before = zcol[:, :]
                nc.vector.scalar_tensor_tensor(g1T[:, k, j * P:(j + 1) * P], firstm[:, bass.ds(t * T + j * P, P)],
                                               before, ps[:, j * P:(j + 1) * P], ALU.mult, ALU.add).then_inc(chain, 1)

        def over_chunks_dve(dve, q, kind, a, b, o):
            rev = kind == "back"
            ops = (ALU.add, ALU.max) if kind == "max" else (ALU.mult, ALU.add)
            first = -BIG if kind == "max" else 0.0
            coef = {"max": nb_row, "add": nostart_row, "back": nolast_row}[kind]

            def within(initial):
                for k in range(2):
                    w = slice(None, None, -1) if rev else slice(None)
                    op = nc.vector.tensor_tensor_scan(o[:, k, w], a[:, k, w], b[:, k, w],
                                                      incol[:, k:k + 1] if initial is None else initial, *ops)
                return op

            within(first).then_inc(s_tail, 1)
            nc.vector.memset(crow[:, NC:NC + 1] if rev else crow[:, 0:1], first).then_inc(s_chain, 1)
            dve.wait_ge(s_row, q + 1)
            ends = bank[6][0:1, 0:NC]
            if rev:
                nc.vector.tensor_tensor_scan(crow[:, NC - 1::-1], coef[:, ::-1], ends[:, ::-1], first, *ops).then_inc(s_crow, 1)
            else:
                nc.vector.tensor_tensor_scan(crow[:, 1:NC + 1], coef[:, :], ends, first, *ops).then_inc(s_crow, 1)
            dve.wait_ge(s_col, q + 1)
            nc.vector.tensor_copy(incol[:, :], bank[7][0:HC, 0:2]).then_inc(s_chain, 1)
            dve.wait_ge(s_chain, 3 * q + 2)
            within(None).then_inc(s_chain, 1)
            dve.wait_ge(s_chain, 3 * q + 3)

        def over_chunks_pe(pe, q, kind, o):
            rev = kind == "back"
            pe.wait_ge(s_tail, q + 1)
            if q:
                pe.wait_ge(s_crow, q)
            e = 0 if rev else P - 1
            for k in range(2):
                mm = nc.tensor.matmul(bank[6][0:1, k * HC:(k + 1) * HC], o[:, k, e:e + 1], ident[0:HC, 0:HC],
                                      start=True, stop=True)
            mm.then_inc(s_row, 1)
            pe.wait_ge(s_crow, q + 1)
            pe.wait_ge(s_chain, 3 * q + 1)
            f = 1 if rev else 0
            for k in range(2):
                mm = nc.tensor.matmul(bank[7][0:HC, k:k + 1], crow[0:1, f + k * HC:f + (k + 1) * HC], one[0:1, 0:1],
                                      start=True, stop=True)
            mm.then_inc(s_col, 1)

        def ends_view(shift):
            return bass.AP(dst_pad.tensor, shift, [[P, HC], [HC * P, 2], [1, P]])

        bias_raw = sel.rearrange("p a j e -> p (a j e)")[0:SPLIT, 0:NBIAS]
        bias_rest = rr.rearrange("p a j e -> p (a j e)")[0:SPLIT, 0:NBIAS]
        bq_wide = x1[:, 0].rearrange("p j f -> p (j f)")[:, 0:LAYERS * SPLIT]

        @block.sync
        def _(sp):
            for a, b in ((w1a_s, w1a), (w1b_s, w1b), (w2a_s, w2a), (w2b_s, w2b)):
                sp.dma_start(a[:, :], b).then_inc(s_w, 16)
            for a, b in ((ws_s, ws), (wv_s, wv), (wqT_s, wqT), (wkT_s, wkT)):
                sp.dma_start(a[:, :, :], b).then_inc(s_w, 16)
            sp.dma_start(bq_s[:, :], bq).then_inc(s_w, 16)
            sp.dma_start(bscol_s[:, :], bs_col).then_inc(s_w, 16)
            for a, shift in ((dp, 0), (di, 1), (dn, 2)):
                sp.dma_start(a[:, :, :], ends_view(shift)).then_inc(s_seg, 16)
            sp.dma_start(slot_all[:, :].rearrange("p (t j) -> p t j", j=J),
                         slot_ids.rearrange("t p j -> p t j")).then_inc(s_seg, 16)
            sp.dma_start(bias_raw[:, SKIP_AT:LAST_AT], bass.AP(bs.tensor, 0, [[0, SPLIT], [1, LAYERS * D]])).then_inc(s_b, 16)
            sp.dma_start(bias_rest[:, 0:LAYERS * D], bass.AP(bv.tensor, 0, [[0, SPLIT], [1, LAYERS * D]])).then_inc(s_b, 16)
            sp.wait_ge(s_p0, 1)
            sp.dma_start(map_d.rearrange("(p n) o -> p (n o)", p=125), minus[0:125, :]).then_inc(s_mapset, 16)
            sp.wait_ge(s_p1, 1)
            sp.dma_start(bass.AP(ord_d.tensor, 0, [[P, HC], [HC * P, 2], [1, P]]), ordb[:, :, :]).then_inc(s_ordout, 16)
            sp.wait_ge(s_ordout, 16)
            sp.dma_start(ordrow[:, :], bass.AP(ord_d.tensor, 0, [[0, P], [1, NS]])).then_inc(s_ordin, 16)
            sp.wait_ge(s_p2, 1)
            sp.dma_start(scat_d.rearrange("t p j -> p t j"),
                         idx_all[:, :].rearrange("p (t j) -> p t j", j=J)).then_inc(s_scout, 16)
            wait_all(sp, prep_end)

            def map_step(i, u, on):
                node_load(sp, 0, i, u, on)
                if on(-2):
                    t, k = i + 2, (u + 2) % 4
                    if not isinstance(t, int) or t >= 4:
                        sp.wait_ge(m_out[k], slot_count(0, t - 4, k, 4, 64))
                        settle(sp)
                    sp.dma_start(gi[:, k, :], scat_d[bass.ds(t, 1)].rearrange("o p j -> p (o j)")).then_inc(i_in[k], 16)
                    sp.dma_start(slotv[:, k, :], slot_ids[bass.ds(t, 1)].rearrange("o p j -> p (o j)")).then_inc(i_in[k], 16)
                node_store(sp, 0, i, u, on)
            pipeline(sp, map_step)
            wait_all(sp, map_end)

            def src_step(i, u, on):
                node_load(sp, 1, i, u, on)
                if on(-2):
                    t, k = i + 2, (u + 2) % 4
                    if not isinstance(t, int) or t >= 4:
                        sp.wait_ge(g_in[k], slot_count(0, t - 4, k, 4, 64))
                        settle(sp)
                    sp.dma_start(gi[:, k, :], xsrc_idx[bass.ds(t, 1)].rearrange("o p j -> p (o j)")).then_inc(
                        i_in[k], 16)
                if on(0):
                    t, k = i, u % 2
                    if on(2):
                        sp.wait_ge(s_e[1], count(0, t - 2))
                        settle(sp)
                    sp.dma_start(wt[:, k, :], wT[:, bass.ds(t * T, T)]).then_inc(w_in[k], 16)
                if on(2):
                    t, k = i - 2, u % 2
                    sp.wait_ge(s_a[1], count(0, t))
                    settle(sp)
                    sp.dma_start(edge_rows(msg_d, t), mrow[:, k]).then_inc(S_out[0][k], 16)
                    sp.wait_ge(s_v[0], count(0, t, 5))
                    settle(sp)
                    sp.dma_start(edge_rows(U[0], t, NS), e1[:, k]).then_inc(S_out[1][k], 16)
                if on(5):
                    t, k = i - 5, (u - 5) % 2
                    sp.wait_ge(s_a[4], count(0, t))
                    settle(sp)
                    sp.dma_start(edge_rows(U[1], t, NS), r1[:, k]).then_inc(S_out[2][k], 16)
                if on(6):
                    t, k = i - 6, u % 2
                    sp.wait_ge(s_a[6], count(0, t))
                    settle(sp)
                    sp.dma_start(edge_rows(U[2], t, NS), r2[:, k]).then_inc(S_out[3][k], 16)
                node_store(sp, 1, i, u, on)
            pipeline(sp, src_step)
            wait_all(sp, src_end)

            def dst_step(i, u, on):
                node_load(sp, 2, i, u, on)
                if on(-2):
                    t, k = i + 2, (u + 2) % 4
                    if not isinstance(t, int) or t >= 4:
                        sp.wait_ge(tg_in[k], slot_count(0, t - 4, k, 4, 128))
                        settle(sp)
                    sp.dma_start(gi[:, k, :], xdst_idx[bass.ds(t, 1)].rearrange("o p j -> p (o j)")).then_inc(
                        ti_in[k], 16)
                    sp.dma_start(gm[:, k, :], xsrc_idx[bass.ds(t, 1)].rearrange("o p j -> p (o j)")).then_inc(
                        ti_in[k], 16)
                    if not isinstance(t, int) or t >= 4:
                        sp.wait_ge(t_e[1], count(0, t - 4))
                        settle(sp)
                    sp.dma_start(rr[:, k], edge_rows(msg_d, t)).then_inc(rows_in[k], 16)
                if on(1):
                    t, k = i - 1, (u - 1) % 2
                    k4 = (u - 1) % 4
                    sp.wait_ge(tg_in[k4], slot_count(0, t, k4, 4, 128))
                    settle(sp)
                    sp.dma_start(found_d[bass.ds(t, 1)].rearrange("o p j -> p (o j)"), found[:, k, :]).then_inc(
                        f_out[k], 16)
                if on(4):
                    t, k = i - 4, u % 2
                    sp.wait_ge(e_o, count(0, t))
                    settle(sp)
                    sp.dma_start(edge_rows(U[0], t), e1[:, k]).then_inc(t_out[k], 16)
                node_store(sp, 2, i, u, on)
            pipeline(sp, dst_step)
            wait_all(sp, dst_end)
            sp.dma_start(logit_c[:, :].rearrange("p (t j) -> p t j", j=J), found_d.rearrange("t p j -> p t j")).then_inc(s_fd, 16)
            sp.wait_ge(s_fc, 3)
            sp.dma_start(srcslot_d.rearrange("t p j -> p t j"),
                         idx_all[:, :].rearrange("p (t j) -> p t j", j=J)).then_inc(s_fo, 16)
            sp.wait_ge(s_fo, 16)

            def fix(l):
                sp.wait_ge(s_fixg, 32 * (l + 1))
                for k in range(2):
                    sp.dma_start(bass.AP(U[l].tensor, (k * HC * P + P - 1) * D, [[P * D, HC], [1, D]]),
                                 fixrow[:, k, :]).then_inc(s_fixw, 16)
                sp.wait_ge(s_fixw, 32 * (l + 1))

            for l in range(LAYERS):
                fix(l)

                def a_step(i, u, on, l=l):
                    b0 = l * NT
                    if l == 0:
                        node_load(sp, 3, i, u, on)
                    if on(-2):
                        t, k = i + 2, (u + 2) % 4
                        if not isinstance(t, int) or t >= 4:
                            sp.wait_ge(ag_in[k], slot_count(in_slot(4, k, l, 64), t - 4, k, 4, 64))
                            settle(sp)
                        sp.dma_start(gi[:, k, :], srcslot_d[bass.ds(t, 1)].rearrange("o p j -> p (o j)")).then_inc(
                            ai_in[k], 16)
                        if not isinstance(t, int) or t >= 4:
                            sp.wait_ge(a_e[0], count(b0, t - 4))
                            settle(sp)
                        sp.dma_start(rr[:, k], edge_rows(U[l], t)).then_inc(rows_in[k], 16)
                    if on(1):
                        t, k = i - 1, (u - 1) % 4
                        sp.wait_ge(ag_in[k], slot_count(in_slot(4, k, l, 64), t, k, 4, 64))
                        settle(sp)
                        sp.dma_start(edge_rows(hs_d, t), er[:, k, :, 0:D]).then_inc(ah_out[k], 16)
                    if on(3):
                        t, k = i - 3, (u - 3) % 2
                        sp.wait_ge(a_k, count(b0, t))
                        settle(sp)
                        sp.dma_start(edge_rows(skip_d, t), mrow[:, k]).then_inc(as_out[k], 16)
                    if l == 0:
                        node_store(sp, 3, i, u, on)
                pipeline(sp, a_step)
                wait_all(sp, a_end(l))

                def b_step(i, u, on, l=l):
                    b0 = l * NT
                    tail = l == LAYERS - 1
                    if on(-2):
                        t, k = i + 2, (u + 2) % 4
                        if not isinstance(t, int) or t >= 4:
                            sp.wait_ge(b_e[0], count(b0, t - 4))
                            if tail:
                                sp.wait_ge(b_v[2], (t - 4) * KT + (b0 + 2))
                            else:
                                sp.wait_ge(b_v[2], count(b0, t - 4))
                            settle(sp)
                        sp.dma_start(er[:, k, :, 0:D], edge_rows(hs_d, t)).then_inc(rows_in[k], 16)
                        sp.dma_start(xr[:, k], edge_rows(skip_d, t)).then_inc(rows_in[k], 16)
                        if tail:
                            sp.dma_start(x1[:, k], edge_rows(U[0], t)).then_inc(rows_in[k], 16)
                    if not tail and on(3):
                        t, k = i - 3, (u - 3) % 2
                        sp.wait_ge(b_a, count(b0, t))
                        settle(sp)
                        sp.dma_start(edge_rows(U[l + 1], t), e1[:, k]).then_inc(b_out[k], 16)
                pipeline(sp, b_step)
                wait_all(sp, b_end(l))
            wait_all(sp, [(s_fin[k], in_slot(2, k, 1, 64)) for k in range(2)])

        @block.gpsimd
        def _(gp):
            gp.memset(ident[:, :], 0.0).then_inc(s_id, 1)
            gp.wait_ge(s_id, 1)
            gp.affine_select(out=ident[:, :], in_=ident[:, :], compare_op=ALU.not_equal, fill=1.0, base=0,
                             pattern=[[-1, P]], channel_multiplier=1).then_inc(s_id, 1)
            gp.memset(one[:, :], 1.0).then_inc(s_id, 1)
            gp.memset(zcol[:, :], 0.0).then_inc(s_id, 1)
            gp.memset(er[:, :, :, :], 1.0).then_inc(s_id, 1)
            gp.iota(slot_i[:, :, :], pattern=[[HC * P, 2], [1, P]], base=0, channel_multiplier=P).then_inc(s_iota, 1)
            gp.wait_ge(s_id, 5)
            wait_all(gp, prep_end)

            def map_step(i, u, on):
                if on(-1):
                    t, k = i + 1, (u + 1) % 4
                    gp.wait_ge(i_in[k], slot_count(0, t, k, 4, 32))
                    settle(gp)
                    for j in range(J):
                        gp.indirect_dma_start(map_d, bass.IndirectOffsetOnAxis(gi[:, k, j:j + 1], 0), slotv[:, k, j:j + 1],
                                              None, bounds_check=N_NODES - 1, oob_is_err=False).then_inc(m_out[k], 16)
            pipeline(gp, map_step)
            wait_all(gp, map_end)

            def src_step(i, u, on):
                if on(-1):
                    t, k = i + 1, (u + 1) % 4
                    gp.wait_ge(i_in[k], slot_count(in_slot(4, k, 1, 32), t, k, 4, 16))
                    if not isinstance(t, int) or t >= 4:
                        gp.wait_ge(s_e[0], count(0, t - 4))
                        gp.wait_ge(s_v[0], count(0, t - 4, 5))
                        settle(gp)
                    for j in range(J):
                        gp.indirect_dma_start(er[:, k, j, 0:D], None, x, bass.IndirectOffsetOnAxis(gi[:, k, j:j + 1], 0)
                                              ).then_inc(g_in[k], 16)
            pipeline(gp, src_step)
            wait_all(gp, src_end)

            def dst_step(i, u, on):
                if on(-1):
                    t, k = i + 1, (u + 1) % 4
                    k2 = (u + 1) % 2
                    gp.wait_ge(ti_in[k], slot_count(0, t, k, 4, 32))
                    if not isinstance(t, int) or t >= 4:
                        gp.wait_ge(t_e[0], count(0, t - 4))
                        gp.wait_ge(t_v[2], count(0, t - 4, 5))
                    if not isinstance(t, int) or t >= 2:
                        gp.wait_ge(f_out[k2], slot_count(0, t - 2, k2, 2))
                        settle(gp)
                    for j in range(J):
                        gp.indirect_dma_start(er[:, k, j, 0:D], None, x, bass.IndirectOffsetOnAxis(gi[:, k, j:j + 1], 0)
                                              ).then_inc(tg_in[k], 16)
                        gp.indirect_dma_start(found[:, k2, j:j + 1], None, map_d,
                                              bass.IndirectOffsetOnAxis(gm[:, k, j:j + 1], 0)).then_inc(tg_in[k], 16)
            pipeline(gp, dst_step)
            wait_all(gp, dst_end)
            gp.wait_ge(s_fo, 16)

            for l in range(LAYERS):
                for k in range(2):
                    gp.indirect_dma_start(fixrow[:, k, :], None, U[l], bass.IndirectOffsetOnAxis(fixidx[:, k:k + 1], 0)
                                          ).then_inc(s_fixg, 16)
                gp.wait_ge(s_fixw, 32 * (l + 1))

                def a_step(i, u, on, l=l):
                    if on(-1):
                        t, k = i + 1, (u + 1) % 4
                        gp.wait_ge(ai_in[k], slot_count(in_slot(4, k, l), t, k, 4))
                        if not isinstance(t, int) or t >= 4:
                            gp.wait_ge(a_v[0], count(l * NT * 5, t - 4, 5))
                            gp.wait_ge(ah_out[k], slot_count(in_slot(4, k, l), t - 4, k, 4))
                            settle(gp)
                        for j in range(J):
                            gp.indirect_dma_start(er[:, k, j, 0:D], None, U[l],
                                                  bass.IndirectOffsetOnAxis(gi[:, k, j:j + 1], 0)).then_inc(ag_in[k], 16)
                pipeline(gp, a_step)
                wait_all(gp, a_end(l))
                if l < LAYERS - 1:
                    wait_all(gp, b_end(l))

            def out_step(i, u, on):
                if on(4):
                    t, k = i - 4, u % 4
                    k2 = u % 2
                    gp.wait_ge(bi_in[k], slot_count(0, t, k, 4))
                    gp.wait_ge(e_o, count(NT, t))
                    settle(gp)
                    for j in range(J):
                        gp.indirect_dma_start(out, bass.IndirectOffsetOnAxis(gi[:, k, j:j + 1], 0), e1[:, k2, j, :],
                                              None, bounds_check=N_NODES - 1, oob_is_err=False).then_inc(s_fin[k2], 16)
            pipeline(gp, out_step)
            wait_all(gp, [(s_fin[k], in_slot(2, k, 1, 64)) for k in range(2)])

        @block.tensor
        def _(pe):
            pe.wait_ge(s_id, 5)
            pe.wait_ge(s_w, 160)
            pe.wait_ge(s_p0, 2)
            for l in range(LAYERS):
                nc.tensor.matmul(bank[l][:, 0:D + 1], wqT_s[:, l, :], wkT_s[:, l, :], start=True, stop=True)
                mm = nc.tensor.matmul(bank[3 + l][0:SPLIT, 0:D + 1], bq_wide[:, l * SPLIT:(l + 1) * SPLIT], wkT_s[:, l, :],
                                      start=True, stop=True)
            mm.then_inc(s_wt, 1)
            pe.wait_ge(s_p1, 1)
            for n in range(4):
                mm = nc.tensor.matmul(bank[6][0:1, n * HC:(n + 1) * HC], ccol[:, n:n + 1], ident[0:HC, 0:HC],
                                      start=True, stop=True)
            pe.wait_ge(s_wt, 2)
            for k in range(2):
                nc.tensor.transpose(bank[0][:, k * HC:(k + 1) * HC], vb[:, k, :], ident[0:HC, 0:HC])
                nc.tensor.transpose(bank[1][:, k * HC:(k + 1) * HC], vc[:, k, :], ident[0:HC, 0:HC])
                mm = nc.tensor.transpose(bank[2][:, k * HC:(k + 1) * HC], vd[:, k, :], ident[0:HC, 0:HC])
            mm.then_inc(s_wt, 1)
            pe.wait_ge(s_fixi, 1)
            over_chunks_pe(pe, 0, "back", va)
            wait_all(pe, prep_end)

            pipeline(pe, lambda i, u, on: node_pe(pe, 0, i, u, on))
            wait_all(pe, map_end)

            def src_step(i, u, on):
                if on(0):
                    k = u % 4
                    pe.wait_ge(g_in[k], slot_count(0, i, k, 4, 64))
                    if on(5):
                        pe.wait_ge(s_a[4], count(0, i - 5))
                    elif on(1):
                        pe.wait_ge(s_a[0], count(0, i - 1))
                    for j in range(J):
                        mm = nc.tensor.transpose(bank[3][:, j * P:(j + 1) * P], er[:, k, j, 0:D], ident[:, :])
                    mm.then_inc(s_e[0], 1)
                node_pe(pe, 1, i, u, on)
                if on(1):
                    t, k = i - 1, (u - 1) % 2
                    pe.wait_ge(s_a[0], count(0, t))
                    pe.wait_ge(w_in[k], slot_count(0, t, k, 2))
                    if on(5):
                        pe.wait_ge(s_a[5], count(0, i - 5))
                    elif on(2):
                        pe.wait_ge(s_a[1], count(0, i - 2))
                    for j in range(J):
                        c = slice(j * P, (j + 1) * P)
                        nc.tensor.matmul(bank[4][:, c], eT[:, k, c], w1a_s[:, :], start=True, stop=False)
                        mm = nc.tensor.matmul(bank[4][:, c], wt[:, k, c], w1b_s[:, :], start=False, stop=True)
                    mm.then_inc(s_e[1], 1)
                    if on(6):
                        pe.wait_ge(s_a[6], count(0, i - 6))
                    elif on(2):
                        pe.wait_ge(s_v[0], (i - 2) * 5 + 1)
                    for j in range(J):
                        c = slice(j * P, (j + 1) * P)
                        mm = nc.tensor.matmul(bank[5][:, c], eT[:, k, c], w2a_s[:, :], start=True, stop=True)
                    mm.then_inc(s_e[2], 1)
                if on(2):
                    t, k = i - 2, u % 2
                    pe.wait_ge(s_v[0], count(0, t, 5))
                    if on(3):
                        pe.wait_ge(s_a[2], count(0, t - 1))
                    for j in range(J):
                        mm = nc.tensor.transpose(bank[6][:, j * P:(j + 1) * P], e1[:, k, j, :], ident[:, :])
                    mm.then_inc(s_e[3], 1)
                if on(3):
                    t, k = i - 3, (u - 3) % 2
                    pe.wait_ge(s_a[2], count(0, t))
                    if on(4):
                        pe.wait_ge(s_a[3], count(0, t - 1))
                    nc.tensor.matmul(bank[7][:, :], ws_s[:, 0, :], e1T[:, k, :], start=True, stop=True).then_inc(s_e[4], 1)
                if on(4):
                    t, k = i - 4, u % 2
                    pe.wait_ge(s_a[3], count(0, t))
                    pe.wait_ge(s_a[0], count(0, min(i, NT - 1) if isinstance(i, int) else i))
                    if on(5) and not on(0):
                        pe.wait_ge(s_a[4], count(0, t - 1))
                    for j in range(J):
                        mm = nc.tensor.transpose(bank[3][:, j * P:(j + 1) * P], g1T[:, k, j * P:(j + 1) * P], ident[:, :])
                    mm.then_inc(s_e[5], 1)
                    pe.wait_ge(s_a[1], count(0, min(i - 1, NT - 1) if isinstance(i, int) else i - 1))
                    if on(5) and not on(1):
                        pe.wait_ge(s_a[5], count(0, t - 1))
                    nc.tensor.matmul(bank[4][:, :], ws_s[:, 1, :], g1T[:, k, :], start=True, stop=True).then_inc(s_e[6], 1)
                if on(5):
                    t, k = i - 5, (u - 5) % 2
                    pe.wait_ge(s_a[5], count(0, t))
                    pe.wait_ge(s_v[0], (min(i - 1, NT - 1) if isinstance(i, int) else i - 1) * 5 + 1)
                    if on(6) and not on(1):
                        pe.wait_ge(s_a[6], count(0, t - 1))
                    for j in range(J):
                        mm = nc.tensor.transpose(bank[5][:, j * P:(j + 1) * P], g2T[:, k, j * P:(j + 1) * P], ident[:, :])
                    mm.then_inc(s_e[7], 1)
            pipeline(pe, src_step)
            wait_all(pe, src_end)

            def dst_step(i, u, on):
                if on(0):
                    k = u % 4
                    pe.wait_ge(tg_in[k], slot_count(0, i, k, 4, 128))
                    if on(1):
                        pe.wait_ge(t_a, count(0, i - 1))
                    for j in range(J):
                        mm = nc.tensor.transpose(bank[3][:, j * P:(j + 1) * P], er[:, k, j, 0:D], ident[:, :])
                    mm.then_inc(t_e[0], 1)
                node_pe(pe, 2, i, u, on)
                if on(1):
                    t, k, k4 = i - 1, (u - 1) % 2, (u - 1) % 4
                    pe.wait_ge(rows_in[k4], slot_count(0, t, k4, 4))
                    pe.wait_ge(t_v[0], count(0, t))
                    if on(2):
                        pe.wait_ge(t_v[1], count(0, t - 1, 4))
                    for j in range(J):
                        mm = nc.tensor.matmul(bank[4][:, j * P:(j + 1) * P], rr[:, k4, j, :], sel[:, k, j, :],
                                              start=True, stop=True)
                    mm.then_inc(t_e[1], 1)
                if on(2):
                    t, k = i - 2, u % 2
                    pe.wait_ge(t_a, count(0, t))
                    pe.wait_ge(t_v[1], count(0, t, 4))
                    if on(3):
                        pe.wait_ge(t_v[2], (t - 1) * 5 + 1)
                    for j in range(J):
                        c = slice(j * P, (j + 1) * P)
                        nc.tensor.matmul(bank[5][:, c], eT[:, k, c], w2a_s[:, :], start=True, stop=False)
                        mm = nc.tensor.matmul(bank[5][:, c], g1T[:, k, c], w2b_s[:, :], start=False, stop=True)
                    mm.then_inc(t_e[2], 1)
            pipeline(pe, dst_step)
            wait_all(pe, dst_end)

            for l in range(LAYERS):
                b0 = l * NT

                def a_step(i, u, on, l=l, b0=b0):
                    if l == 0:
                        node_pe(pe, 3, i, u, on)
                    if on(1):
                        t, k, k4 = i - 1, (u - 1) % 2, (u - 1) % 4
                        pe.wait_ge(rows_in[k4], slot_count(in_slot(4, k4, 1 + 3 * l), t, k4, 4))
                        pe.wait_ge(a_v[1], count(b0, t))
                        if on(2):
                            pe.wait_ge(a_a, count(b0, t - 1))
                        for j in range(J):
                            mm = nc.tensor.matmul(bank[3][:, j * P:(j + 1) * P], rr[:, k4, j, :], sel[:, k, j, :],
                                                  start=True, stop=True)
                        mm.then_inc(a_e[0], 1)
                    if on(2):
                        t, k = i - 2, u % 2
                        pe.wait_ge(a_a, count(b0, t))
                        if on(3):
                            pe.wait_ge(a_v[0], count(b0 * 5, t - 1, 5) - 1)
                        for j in range(J):
                            ps = bank[4 + j // 2][:, 0:2 * (D + 1)].rearrange("p (j f) -> p j f", j=2)
                            if j % 2 == 0:
                                nc.tensor.matmul(ps, parts[:, :], bias_rows(l * (D + 1), D + 1, 2),
                                                 start=True, stop=False)
                            mm = nc.tensor.matmul(ps[:, j % 2, :], eT[:, k, j * P:(j + 1) * P], a_s[:, l, :],
                                                  start=False, stop=j % 2 == 1)
                        mm.then_inc(a_e[1], 1)
                        if on(3):
                            pe.wait_ge(a_k, count(b0, t - 1))
                        nc.tensor.matmul(chunk_rows(bank[6][:, :]), parts[:, :], bias_rows(SKIP_AT + l * D, D, J),
                                         start=True, stop=False)
                        for j in range(J):
                            mm = nc.tensor.matmul(bank[6][:, j * P:(j + 1) * P], eT[:, k, j * P:(j + 1) * P],
                                                  ws_s[:, l, :], start=False, stop=j == J - 1)
                        mm.then_inc(a_e[2], 1)
                pipeline(pe, a_step)
                wait_all(pe, a_end(l))
                for k in range(2):
                    mm = nc.tensor.transpose(bank[0][0:HC, k * P:(k + 1) * P], logit_c[:, k * HC:(k + 1) * HC], ident[:, :])
                mm.then_inc(s_lt, 1)
                for n, (kind, o) in enumerate((("max", vb), ("back", vd), ("add", vb), ("back", vd))):
                    over_chunks_pe(pe, 1 + 4 * l + n, kind, o)
                pe.wait_ge(s_al, l + 1)
                for k in range(2):
                    mm = nc.tensor.transpose(bank[0][:, k * HC:(k + 1) * HC], va[:, k, :], ident[0:HC, 0:HC])
                mm.then_inc(s_at, 1)

                def b_step(i, u, on, l=l, b0=b0):
                    if on(1):
                        t, k, k4 = i - 1, (u - 1) % 2, (u - 1) % 4
                        by = 48 if l == LAYERS - 1 else 32
                        pe.wait_ge(rows_in[k4], slot_count(in_slot(4, k4, 2 + 3 * l), t, k4, 4, by))
                        pe.wait_ge(b_v[0], count(b0, t))
                        if on(2):
                            pe.wait_ge(b_v[1], count(b0 * 4, t - 1, 4))
                        for j in range(J):
                            mm = nc.tensor.matmul(bank[3][:, j * P:(j + 1) * P], er[:, k4, j, 0:D], sel[:, k, j, :],
                                                  start=True, stop=True)
                        mm.then_inc(b_e[0], 1)
                    if on(2):
                        t, k = i - 2, u % 2
                        kb = KT if l == LAYERS - 1 else 1
                        pe.wait_ge(b_v[1], count(b0 * 4, t, 4))
                        if on(3):
                            pe.wait_ge(b_v[2], (t - 1) * kb + (b0 + 1))
                        for j in range(J):
                            mm = nc.tensor.matmul(bank[4][:, j * P:(j + 1) * P], g1T[:, k, j * P:(j + 1) * P],
                                                  wv_s[:, l, :], start=True, stop=True)
                        mm.then_inc(b_e[1], 1)
                pipeline(pe, b_step)
                wait_all(pe, b_end(l))

        @block.scalar
        def _(act):
            def edge_out(k):
                for j in range(J):
                    op = nc.scalar.activation(e1[:, k, j, :], ey[:, k, j, :], ACT.Identity,
                                              scale=eri[:, k, j:j + 1], bias=ebias[:, k, j:j + 1])
                op.then_inc(e_o, 1)

            wait_all(act, prep_end)
            def map_step(i, u, on):
                node_out(act, 0, i, u, on)
                node_act(act, 0, i, u, on)
                node_sqrt(act, 0, i, u, on)
            pipeline(act, map_step)
            wait_all(act, map_end)

            def src_step(i, u, on):
                node_out(act, 1, i, u, on)
                if on(0):
                    act.wait_ge(s_e[0], count(0, i))
                    if on(2):
                        act.wait_ge(s_e[2], count(0, i - 2))
                    nc.scalar.activation(eT[:, u % 2, :], bank[3][:, :], ACT.Copy).then_inc(s_a[0], 1)
                node_act(act, 1, i, u, on)
                node_sqrt(act, 1, i, u, on)
                if on(1):
                    act.wait_ge(s_v[0], (i - 1) * 5 + 3)
                    root(emv[:, :, 1], ers[:, :], e_sq)
                if on(1):
                    t, k = i - 1, (u - 1) % 2
                    act.wait_ge(s_e[1], count(0, t))
                    if on(3):
                        act.wait_ge(S_out[0][k], slot_count(0, t - 2, k, 2))
                    nc.scalar.activation(mrow[:, k], chunk_rows(bank[4][:, :]), ACT.Relu).then_inc(s_a[1], 1)
                if on(2):
                    t, k = i - 2, u % 2
                    act.wait_ge(s_e[3], count(0, t))
                    if on(4):
                        act.wait_ge(s_e[4], count(0, t - 2))
                    nc.scalar.activation(e1T[:, k, :], bank[6][:, :], ACT.Copy).then_inc(s_a[2], 1)
                if on(3):
                    t, k = i - 3, (u - 3) % 2
                    act.wait_ge(s_e[4], count(0, t))
                    if on(5):
                        act.wait_ge(s_e[6], count(0, t - 2))
                    nc.scalar.activation(g1T[:, k, :], bank[7][:, :], ACT.Relu, bias=bscol_s[:, 0:1]).then_inc(s_a[3], 1)
                if on(4):
                    t, k = i - 4, u % 2
                    act.wait_ge(s_e[5], count(0, t))
                    if on(6):
                        act.wait_ge(S_out[2][k], slot_count(0, t - 2, k, 2))
                    nc.scalar.activation(r1[:, k], chunk_rows(bank[3][:, :]), ACT.Copy).then_inc(s_a[4], 1)
                    act.wait_ge(s_e[6], count(0, t))
                    if on(6):
                        act.wait_ge(s_e[7], count(0, t - 2))
                    nc.scalar.activation(g2T[:, k, :], bank[4][:, :], ACT.Relu, bias=bscol_s[:, 1:2]).then_inc(s_a[5], 1)
                if on(5):
                    t, k = i - 5, (u - 5) % 2
                    act.wait_ge(s_e[7], count(0, t))
                    if on(7):
                        act.wait_ge(S_out[3][k], slot_count(0, t - 2, k, 2))
                    nc.scalar.activation(r2[:, k], chunk_rows(bank[5][:, :]), ACT.Copy).then_inc(s_a[6], 1)
            pipeline(act, src_step)
            wait_all(act, src_end)

            def dst_step(i, u, on):
                if on(3):
                    t, k = i - 3, (u - 3) % 2
                    act.wait_ge(t_v[2], count(0, t, 5))
                    if on(5):
                        act.wait_ge(t_out[k], slot_count(0, t - 2, k, 2))
                    edge_out(k)
                node_out(act, 2, i, u, on)
                node_act(act, 2, i, u, on)
                if on(0):
                    act.wait_ge(t_e[0], count(0, i))
                    if on(2):
                        act.wait_ge(t_e[2], count(0, i - 2))
                    nc.scalar.activation(eT[:, u % 2, :], bank[3][:, :], ACT.Copy).then_inc(t_a, 1)
                node_sqrt(act, 2, i, u, on)
                if on(2):
                    act.wait_ge(t_v[2], (i - 2) * 5 + 3)
                    root(emv[:, :, 1], ers[:, :], e_sq)
            pipeline(act, dst_step)
            wait_all(act, dst_end)

            for l in range(LAYERS):
                b0 = l * NT

                def a_step(i, u, on, l=l, b0=b0):
                    if l == 0:
                        node_out(act, 3, i, u, on)
                        node_act(act, 3, i, u, on)
                    if on(1):
                        t, k = i - 1, (u - 1) % 2
                        act.wait_ge(a_e[0], count(b0, t))
                        if on(3):
                            act.wait_ge(a_e[2], count(b0, t - 2))
                        nc.scalar.activation(eT[:, k, :], bank[3][:, :], ACT.Copy).then_inc(a_a, 1)
                    if l == 0:
                        node_sqrt(act, 3, i, u, on)
                    if on(2):
                        t, k = i - 2, u % 2
                        act.wait_ge(a_e[2], count(b0, t))
                        if on(4):
                            act.wait_ge(as_out[k], slot_count(in_slot(2, k, l), t - 2, k, 2))
                        nc.scalar.activation(mrow[:, k], chunk_rows(bank[6][:, :]), ACT.Copy).then_inc(a_k, 1)
                pipeline(act, a_step)
                wait_all(act, a_end(l))
                act.wait_ge(s_arg, l + 1)
                nc.scalar.activation(va[:, :, :], va[:, :, :], ACT.Exp).then_inc(s_exp, 1)

                def b_step(i, u, on, l=l, b0=b0):
                    if on(2):
                        t, k = i - 2, u % 2
                        act.wait_ge(b_v[2], count(b0, t))
                        if on(4):
                            act.wait_ge(b_out[k], slot_count(in_slot(2, k, l), t - 2, k, 2))
                        nc.scalar.activation(e1[:, k], mrow[:, k], ACT.Relu).then_inc(b_a, 1)
                if l < LAYERS - 1:
                    pipeline(act, b_step)
                    wait_all(act, b_end(l))

            def out_step(i, u, on):
                if on(1):
                    t, k = i - 1, (u - 1) % 4
                    if not isinstance(t, int) or t >= 4:
                        act.wait_ge(s_fin[k % 2], slot_count(0, t - 4, k % 2, 2, 64))
                        settle(act)
                    act.dma_start(gi[:, k, :], scat_d[bass.ds(t, 1)].rearrange("o p j -> p (o j)")).then_inc(bi_in[k], 16)
                if on(3):
                    t, k = i - 3, (u - 3) % 2
                    act.wait_ge(b_v[2], t * KT + ((LAYERS - 1) * NT + KT))
                    if on(5):
                        act.wait_ge(s_fin[k], slot_count(0, t - 2, k, 2, 64))
                    edge_out(k)
                if on(2):
                    act.wait_ge(b_v[2], (i - 2) * KT + ((LAYERS - 1) * NT + 4))
                    root(emv[:, :, 1], ers[:, :], e_sq)
            pipeline(act, out_step)

        @block.vector
        def _(dve):
            steps = [1]

            def link(op):
                steps[0] += 1
                op.then_inc(s_vl, 1)
                dve.wait_ge(s_vl, steps[0])

            nc.vector.memset(eps_s[:, :], EPS)
            nc.vector.memset(minus[:, :], -1.0).then_inc(s_p0, 1)
            nc.vector.memset(parts[:, :], 0.0).then_inc(s_vl, 1)
            dve.wait_ge(s_vl, 1)
            for k in range(0, SPLIT, 32):
                nc.vector.memset(parts[k:k + 1, :], 1.0)
            dve.wait_ge(s_w, 160)
            dve.wait_ge(s_p0, 1)
            for l in range(LAYERS):
                op = nc.vector.tensor_scalar(bq_wide[:, l * SPLIT:(l + 1) * SPLIT], minus[:, 0:SPLIT], 0.0, bq_s[:, l:l + 1],
                                             ALU.mult, ALU.add)
            op.then_inc(s_p0, 1)
            dve.wait_ge(s_seg, 64)
            link(nc.vector.tensor_tensor(va[:, :, :], di[:, :, :], dp[:, :, :], ALU.not_equal))
            link(nc.vector.tensor_tensor(last[:, :, :], di[:, :, :], dn[:, :, :], ALU.not_equal))
            link(nc.vector.tensor_scalar(notstart[:, :, :], va[:, :, :], -1.0, 1.0, ALU.mult, ALU.add))
            link(nc.vector.tensor_scalar(notlast[:, :, :], last[:, :, :], -1.0, 1.0, ALU.mult, ALU.add))
            link(nc.vector.tensor_scalar(nb[:, :, :], va[:, :, :], -BIG, None, ALU.mult))
            for k in range(2):
                link(nc.vector.tensor_tensor_scan(vb[:, k, :], va[:, k, :], va[:, k, :], 0.0, ALU.add, ALU.max))
            link(nc.vector.tensor_copy(ordb[:, :, :], vb[:, :, :]))
            link(nc.vector.tensor_copy(vc[:, :, :], last[:, :, :]))
            link(nc.vector.memset(vc[:, :, P - 1:P], 1.0))
            link(nc.vector.scalar_tensor_tensor(vd[:, :, :], notlast[:, :, :], SKIP, di[:, :, :], ALU.mult, ALU.add))
            link(nc.vector.tensor_scalar(ccol[:, 0:2], vb[:, :, P - 1], 0.0, None, ALU.is_equal))
            link(nc.vector.reduce_max(ccol[:, 2:4], last[:, :, :], mybir.AxisListType.X))
            link(nc.vector.tensor_scalar(ccol[:, 2:4], ccol[:, 2:4], 0.0, None, ALU.is_equal))
            nc.vector.tensor_copy(va[:, :, :], last[:, :, :]).then_inc(s_p1, 1)
            dve.wait_ge(s_wt, 1)
            for l in range(LAYERS):
                nc.vector.tensor_copy(a_s[:, l, :], bank[l][:, 0:D + 1])
                op = nc.vector.tensor_copy(bias_raw[:, l * (D + 1):(l + 1) * (D + 1)], bank[3 + l][0:SPLIT, 0:D + 1])
            op.then_inc(s_wt, 1)
            dve.wait_ge(s_b, 32)
            link(nc.vector.tensor_copy(bias_raw[:, LAST_AT:], bias_raw[:, LAST_AT - D:LAST_AT]))
            link(nc.vector.tensor_tensor(bias_raw[:, SKIP_AT:LAST_AT], bias_raw[:, SKIP_AT:LAST_AT],
                                         bias_rest[:, 0:LAYERS * D], ALU.add))
            link(nc.vector.tensor_copy(biases[:, :], bias_raw))
            link(nc.vector.tensor_tensor(bias_rest, bias_raw, biases[:, :], ALU.subtract))
            nc.vector.tensor_copy(biases[32:64, :], bias_rest[32:64, :])
            link(nc.vector.tensor_copy(biases[64:96, :], bias_rest[64:96, :]))
            link(nc.vector.tensor_tensor(bias_raw[64:96, :], bias_rest[64:96, :], biases[64:96, :], ALU.subtract))
            link(nc.vector.tensor_copy(biases[64:96, :], bias_raw[64:96, :]))
            dve.wait_ge(s_wt, 3)
            link(nc.vector.tensor_copy(ordcol[:, :], bank[0][:, 0:NC]))
            link(nc.vector.tensor_copy(endcol[:, :], bank[1][:, 0:NC]))
            nc.vector.tensor_copy(idx_all[:, :], bank[2][:, 0:NC]).then_inc(s_p2, 1)
            link(nc.vector.tensor_copy(nostart_row[:, :], bank[6][0:1, 0:NC]))
            link(nc.vector.tensor_copy(nolast_row[:, :], bank[6][0:1, NC:2 * NC]))
            link(nc.vector.tensor_scalar(nb_row[:, :], nostart_row[:, :], -1.0, BIG, ALU.add, ALU.mult))
            dve.wait_ge(s_iota, 1)
            link(nc.vector.tensor_copy(vd[:, :, :], slot_i[:, :, :]))
            nc.vector.tensor_tensor(vc[:, :, :], vd[:, :, :], last[:, :, :], ALU.mult).then_inc(s_fixi, 1)
            dve.wait_ge(s_fixi, 1)
            over_chunks_dve(dve, 0, "back", notlast, vc, va)
            link(nc.vector.tensor_copy(fixidx[:, :], va[:, :, P - 1]))
            dve.wait_ge(s_ordin, 16)
            nc.vector.tensor_scalar(firstm[:, :], ordrow[:, :], 0.0, None, ALU.is_equal).then_inc(s_prep, 1)
            wait_all(dve, prep_end)

            def map_step(i, u, on):
                node_dve1(dve, 0, i, u, on)
                node_dve2(dve, 0, i, u, on)
            pipeline(dve, map_step)
            wait_all(dve, map_end)

            def src_step(i, u, on):
                node_dve1(dve, 1, i, u, on)
                if on(1):
                    t = i - 1
                    after(dve, s_v[0], t * 5)
                    dve.wait_ge(s_e[2], count(0, t))
                    nc.vector.scalar_tensor_tensor(ey[:, 0], chunk_rows(bank[5][:, :]), 0.0, er[:, (u - 1) % 4, :, 0:D],
                                                   ALU.max, ALU.add).then_inc(s_v[0], 1)
                    moments(dve, [(ey[:, 0], estat, emv)], s_v[0], t * 5 + 1)
                node_dve2(dve, 1, i, u, on)
                if on(1):
                    t, k = i - 1, (u - 1) % 2
                    dve.wait_ge(e_sq, count(0, t))
                    if on(3):
                        dve.wait_ge(S_out[1][k], slot_count(0, t - 2, k, 2))
                        dve.wait_ge(s_e[3], count(0, t - 2))
                    nc.vector.reciprocal(eri[:, 0], ers[:, :]).then_inc(s_v[0], 1)
                    dve.wait_ge(s_v[0], t * 5 + 4)
                    for j in range(J):
                        op = nc.vector.tensor_scalar(e1[:, k, j, :], ey[:, 0, j, :], emv[:, j, 0:1], eri[:, 0, j:j + 1],
                                                     ALU.subtract, ALU.mult)
                    op.then_inc(s_v[0], 1)
            pipeline(dve, src_step)
            wait_all(dve, src_end)

            def dst_step(i, u, on):
                if on(0):
                    if on(2):
                        dve.wait_ge(t_e[1], count(0, i - 2))
                    select(i, u % 2, None, t_v[0])
                node_dve1(dve, 2, i, u, on)
                if on(1):
                    t, k = i - 1, (u - 1) % 2
                    dve.wait_ge(t_e[1], count(0, t))
                    if on(2):
                        dve.wait_ge(t_v[1], t * 4)
                    if on(3):
                        dve.wait_ge(t_e[2], count(0, t - 2))
                    carry(dve, t, k, bank[4], t_v[1], t * 4)
                if on(2):
                    t, k = i - 2, u % 2
                    after(dve, t_v[2], t * 5)
                    dve.wait_ge(t_e[2], count(0, t))
                    if on(4):
                        dve.wait_ge(e_o, count(0, t - 2))
                    nc.vector.scalar_tensor_tensor(ey[:, k], chunk_rows(bank[5][:, :]), 0.0, er[:, (u - 2) % 4, :, 0:D],
                                                   ALU.max, ALU.add).then_inc(t_v[2], 1)
                    moments(dve, [(ey[:, k], estat, emv)], t_v[2], t * 5 + 1)
                    dve.wait_ge(e_sq, count(NT, t))
                    nc.vector.reciprocal(eri[:, k], ers[:, :]).then_inc(t_v[2], 1)
                    dve.wait_ge(t_v[2], t * 5 + 4)
                    minus_mean(ebias[:, k], emv, eri[:, k]).then_inc(t_v[2], 1)
                node_dve2(dve, 2, i, u, on)
            pipeline(dve, dst_step)
            wait_all(dve, dst_end)
            dve.wait_ge(s_fd, 16)
            nc.vector.tensor_scalar(alpha_c[:, :], slot_all[:, :], float(NS + 1), None, ALU.add).then_inc(s_fc, 1)
            dve.wait_ge(s_fc, 1)
            nc.vector.scalar_tensor_tensor(alpha_c[:, :], logit_c[:, :], 0.0, alpha_c[:, :], ALU.is_lt, ALU.mult).then_inc(s_fc, 1)
            dve.wait_ge(s_fc, 2)
            nc.vector.tensor_tensor(idx_all[:, :], alpha_c[:, :], logit_c[:, :], ALU.add).then_inc(s_fc, 1)
            dve.wait_ge(s_fc, 3)

            for l in range(LAYERS):
                b0 = l * NT

                def a_step(i, u, on, l=l, b0=b0):
                    if on(0):
                        if on(2):
                            dve.wait_ge(a_e[0], count(b0, i - 2))
                        select(i, u % 2, endcol, a_v[1])
                    if l == 0:
                        node_dve1(dve, 3, i, u, on)
                    if on(2):
                        t, k = i - 2, u % 2
                        k4 = (u - 2) % 4
                        at = t * 5 + b0 * 5
                        dve.wait_ge(ag_in[k4], slot_count(in_slot(4, k4, l, 64), t, k4, 4, 64))
                        dve.wait_ge(a_e[1], count(b0, t))
                        after(dve, a_v[0], at)
                        for j in range(J):
                            nc.vector.tensor_tensor_reduce(
                                out=junk[:, j, :], in0=bank[4 + j // 2][:, (j % 2) * (D + 1):(j % 2 + 1) * (D + 1)],
                                in1=er[:, k4, j, :], scale=float(D) ** -0.5, scalar=0.0, op0=ALU.mult, op1=ALU.add,
                                accum_out=lg[:, k, j:j + 1]).then_inc(a_v[0], 1)
                        dve.wait_ge(a_v[0], at + 4)
                        nc.vector.tensor_copy(logit_c[:, bass.ds(t * J, J)], lg[:, k, :]).then_inc(a_v[0], 1)
                    if l == 0:
                        node_dve2(dve, 3, i, u, on)
                pipeline(dve, a_step)
                wait_all(dve, a_end(l))
                dve.wait_ge(s_lt, l + 1)
                q = 1 + 4 * l
                link(nc.vector.tensor_copy(va[:, :, :], bank[0][0:HC, 0:2 * P].rearrange("c (k e) -> c k e", k=2)))
                over_chunks_dve(dve, q, "max", nb, va, vb)
                link(nc.vector.tensor_tensor(vc[:, :, :], vb[:, :, :], last[:, :, :], ALU.mult))
                over_chunks_dve(dve, q + 1, "back", notlast, vc, vd)
                nc.vector.tensor_tensor(va[:, :, :], va[:, :, :], vd[:, :, :], ALU.subtract).then_inc(s_arg, 1)
                dve.wait_ge(s_exp, l + 1)
                over_chunks_dve(dve, q + 2, "add", notstart, va, vb)
                link(nc.vector.tensor_tensor(vc[:, :, :], vb[:, :, :], last[:, :, :], ALU.mult))
                over_chunks_dve(dve, q + 3, "back", notlast, vc, vd)
                link(nc.vector.tensor_scalar(vd[:, :, :], vd[:, :, :], 1e-16, None, ALU.max))
                link(nc.vector.reciprocal(vc[:, :, :], vd[:, :, :]))
                nc.vector.tensor_tensor(va[:, :, :], va[:, :, :], vc[:, :, :], ALU.mult).then_inc(s_al, 1)
                dve.wait_ge(s_at, l + 1)
                link(nc.vector.tensor_copy(alpha_c[:, :], bank[0][:, 0:NC]))

                def b_step(i, u, on, l=l, b0=b0):
                    tail = l == LAYERS - 1
                    if on(0):
                        if on(2):
                            dve.wait_ge(b_e[0], count(b0, i - 2))
                        select(i, u % 2, alpha_c, b_v[0])
                    if on(1):
                        t, k = i - 1, (u - 1) % 2
                        dve.wait_ge(b_e[0], count(b0, t))
                        if on(2):
                            dve.wait_ge(b_v[1], t * 4 + b0 * 4)
                        if on(3):
                            dve.wait_ge(b_e[1], count(b0, t - 2))
                        carry(dve, t, k, bank[3], b_v[1], t * 4 + b0 * 4)
                    if on(2):
                        t, k, k4 = i - 2, u % 2, (u - 2) % 4
                        dve.wait_ge(b_e[1], count(b0, t))
                        if not tail:
                            if on(4):
                                dve.wait_ge(b_a, count(b0, t - 2))
                            dve.wait_ge(rows_in[k4], slot_count(in_slot(4, k4, 2 + 3 * l), t, k4, 4, 32))
                            nc.vector.tensor_tensor(mrow[:, k], chunk_rows(bank[4][:, :]), xr[:, k4], ALU.add).then_inc(
                                b_v[2], 1)
                        else:
                            at = t * KT + b0
                            after(dve, b_v[2], at)
                            dve.wait_ge(rows_in[k4], slot_count(in_slot(4, k4, 2 + 3 * l), t, k4, 4, 48))
                            nc.vector.tensor_tensor(mrow[:, 0], chunk_rows(bank[4][:, :]), xr[:, k4], ALU.add).then_inc(
                                b_v[2], 1)
                            dve.wait_ge(b_v[2], at + 1)
                            if on(4):
                                dve.wait_ge(e_o, count(NT, t - 2))
                            nc.vector.tensor_tensor(ey[:, k], mrow[:, 0], x1[:, k4], ALU.add).then_inc(b_v[2], 1)
                            moments(dve, [(ey[:, k], estat, emv)], b_v[2], at + 2)
                            dve.wait_ge(e_sq, count(2 * NT, t))
                            nc.vector.reciprocal(eri[:, k], ers[:, :]).then_inc(b_v[2], 1)
                            dve.wait_ge(b_v[2], at + 5)
                            minus_mean(ebias[:, k], emv, eri[:, k]).then_inc(b_v[2], 1)
                pipeline(dve, b_step)
                wait_all(dve, b_end(l))


def kernel(**inputs):
    import numpy as _np
    import concourse.bacc as _bacc
    from concourse import mybir as _mybir
    from concourse.bass_utils import run_bass_kernel_spmd as _run

    get = {k: _np.ascontiguousarray(v) for k, v in inputs.items()}
    pad = NS - N_EDGES

    def tiles(v):
        return _np.ascontiguousarray(v.reshape(NT, J, P).transpose(0, 2, 1))

    src, dst = get["src"], get["dst"]
    fill = _np.zeros(pad, _np.int32)
    arrays = {
        "x": get["x"],
        "xsrc_idx": tiles(_np.concatenate([src, fill])),
        "xdst_idx": tiles(_np.concatenate([dst, fill])),
        "slot_ids": tiles(_np.arange(NS, dtype=_np.float32)),
        "dst_pad": _np.concatenate([_np.full(1, -1, _np.int32), dst, _np.full(pad, N_NODES, _np.int32),
                                    _np.full(1, -2, _np.int32)]),
        "wT": _np.concatenate([_np.concatenate([get["edge_attr_3"].T, _np.ones((1, N_EDGES), _np.float32)]),
                               _np.zeros((4, pad), _np.float32)], axis=1),
        "w1a": get["L0_gnn_W1"][:, :D].T,
        "w1b": _np.concatenate([get["L0_gnn_W1"][:, D:].T, get["L0_gnn_b1"][None, :]]),
        "w2a": get["L0_gnn_W2"][:, :D].T,
        "w2b": get["L0_gnn_W2"][:, D:].T,
        "wqT": get["L1_gnn_Wq"].transpose(2, 0, 1),
        "wkT": _np.concatenate([get["L1_gnn_Wk"].transpose(2, 0, 1), get["L1_gnn_bk"].T[:, :, None]], axis=2),
        "bq": get["L1_gnn_bq"].T,
        "wv": get["L1_gnn_Wv"].transpose(1, 0, 2),
        "bv": get["L1_gnn_bv"],
        "ws": get["L1_gnn_Ws"].transpose(1, 0, 2),
        "bs": get["L1_gnn_bs"],
        "bs_col": get["L1_gnn_bs"].T,
    }
    nc = _bacc.Bacc("TRN2", target_bir_lowering=False, num_devices=1)
    given, args = {}, {}
    for name, a in arrays.items():
        a = _np.ascontiguousarray(a)
        given[f"in_{name}"] = a
        args[name] = nc.dram_tensor(f"in_{name}", a.shape, _mybir.dt.from_np(a.dtype), kind="ExternalInput").ap()
    args["out"] = nc.dram_tensor("out_rows", (N_NODES, D), _mybir.dt.float32, kind="ExternalOutput").ap()
    gnn_program(nc, **args)
    return _run(nc, [given], core_ids=[0]).results[0]["out_rows"]
```

```python
import numpy as np
import concourse.bass as bass
from concourse import mybir
from concourse.alu_op_type import AluOpType as ALU
from contextlib import ExitStack

FP32 = mybir.dt.float32
BF16 = mybir.dt.bfloat16
I32 = mybir.dt.int32
U8 = mybir.dt.uint8
ACT = mybir.ActivationFunctionType

N_NODES, N_EDGES, D = 100000, 25000, 128
P = 128
J = 4
T = P * J
NT = -(-N_EDGES // T)
NC = NT * J
NS = NC * P
HC = NC // 2
LAYERS = 3
DENSE_TILES = -(-N_NODES // T)
UNROLL = 4
FIRST = -UNROLL
SPLIT = 96
SKIP_AT = LAYERS * (D + 1)
LAST_AT = SKIP_AT + LAYERS * D
NBIAS = LAST_AT + D
ATTRS = 4
TERMS = 9 * ATTRS
BIG = 1.0e30
EPS = 1e-5
SKIP = 1.0e6


def iterations_end(last):
    return UNROLL * -(-(NT + last + 1) // UNROLL)


MAP_LAST, SRC_LAST, DST_LAST, A_LAST, B_LAST = 0, 7, 7, 4, 7
A_EVERY = 4
FIRSTM_AT = (1, 3, 5, 7, NT, NT + 1, NT + 3, NT + 5)
DST_NODES_UNTIL = 48
MAP_NODES = FIRST
SRC_NODES = MAP_NODES + iterations_end(MAP_LAST) - FIRST
DST_NODES = SRC_NODES + iterations_end(SRC_LAST) - FIRST
A_NODES = [DST_NODES + DST_NODES_UNTIL - FIRST + l * (iterations_end(A_LAST) - FIRST) // A_EVERY for l in range(LAYERS)]


def gnn_program(nc, x, xsrc_idx, xdst_idx, slot_ids, dst_pad, wT, w1a, w1b, w2a, w2b,
                wqT, wkT, bq, wv, bv, ws, bs, bs_col, which_part, out):
    ctx = ExitStack()
    with ctx:
        def sb(name, shape, dt=FP32):
            return ctx.enter_context(nc.sbuf_tensor(name, shape, dt))

        def pb(name, shape=(P, 512), dt=FP32):
            return ctx.enter_context(nc.psum_tensor(name, list(shape), dt))

        def sem(name):
            return ctx.enter_context(nc.semaphore(name))

        U = [nc.dram_tensor(f"u{l}", (2 * NS, D), FP32).ap() for l in range(LAYERS)]
        msg_d = nc.dram_tensor("msg_d", (NS, D), FP32).ap()
        hs_d = nc.dram_tensor("hs_d", (NS, D), FP32).ap()
        skip_d = nc.dram_tensor("skip_d", (NS, D), FP32).ap()
        map_d = nc.dram_tensor("map_d", (N_NODES, 1), FP32).ap()
        found_d = nc.dram_tensor("found_d", (NT, P, J), FP32).ap()
        srcslot_d = nc.dram_tensor("srcslot_d", (NT, P, J), I32).ap()
        scat_d = nc.dram_tensor("scat_d", (NT, P, J), I32).ap()
        attr_d = nc.dram_tensor("attr_d", (3 * ATTRS, NS), BF16).ap()
        ord_d = nc.dram_tensor("ord_d", (1, NS), U8).ap()

        ident = sb("ident", [P, P])
        one = sb("one", [1, P])
        which = sb("which", [TERMS, 3])
        w1a_s, w2a_s, w2b_s = sb("w1a_s", [P, D]), sb("w2a_s", [P, D]), sb("w2b_s", [P, D])
        w1b_s = sb("w1b_s", [TERMS, D], BF16)
        ws_s, wv_s = sb("ws_s", [P, LAYERS, D]), sb("wv_s", [P, LAYERS, D])
        a_s = sb("a_s", [P, LAYERS, D + 1])
        bscol_s = sb("bscol_s", [P, LAYERS])
        biases = sb("biases", [SPLIT, NBIAS], BF16)
        parts = sb("parts", [SPLIT, P], BF16)
        ordrow = sb("ordrow", [P, NS], U8)
        firstm = sb("firstm", [P, NS], U8)
        ordcol = sb("ordcol", [P, NC])
        endcol = sb("endcol", [P, NC])
        logit_c = sb("logit_c", [P, NC])
        alpha_c = sb("alpha_c", [P, NC])
        h = [HC, 2, P]
        nb, notstart, last, notlast = sb("nb", h), sb("notstart", h), sb("last", h), sb("notlast", h)
        va, vb, vc, vd = sb("va", h), sb("vb", h), sb("vc", h), sb("vd", h)
        incol = sb("incol", [HC, 2])
        nostart_row, nb_row, nolast_row = sb("nostart_row", [1, NC]), sb("nb_row", [1, NC]), sb("nolast_row", [1, NC])
        crow = sb("crow", [1, NC + 1])
        fixidx = sb("fixidx", [HC, 2], I32)
        fixrow = sb("fixrow", [HC, 2, D])
        ccol = sb("ccol", [HC, 4])
        xr = sb("xr", [P, 4, J, D])
        xT = sb("xT", [P, 2, T])
        yb = sb("yb", [P, 2, J, D])
        x1 = sb("x1", [P, 4, J, D])
        x1T = sb("x1T", [P, 2, T])
        h1T = sb("h1T", [P, 2, T])
        h2T = sb("h2T", [P, 2, T])
        zb = sb("zb", [P, 4, J, D])
        ob = sb("ob", [P, 2, J, D])
        stat = sb("stat", [P, 2, J, 6])
        mv = sb("mv", [P, 2, 2, J, 2])
        rs, ri = sb("rs", [P, 2, J]), sb("ri", [P, 4, 2, J])
        fbias = sb("fbias", [P, 4, J])
        eps_s = sb("eps_s", [P, 1])
        gi = sb("gi", [P, 4, J], I32)
        gm = sb("gm", [P, 4, J], I32)
        slotv = sb("slotv", [P, 4, J])
        er = sb("er", [P, 4, J, D + 1])
        eT = sb("eT", [P, 2, T])
        ey = sb("ey", [P, 4, J, D])
        e1 = sb("e1", [P, 2, J, D])
        e1T = sb("e1T", [P, 2, T])
        g1T = sb("g1T", [P, 2, T])
        g2T = sb("g2T", [P, 2, T])
        rr = sb("rr", [P, 4, J, D])
        r1, r2 = rr[:, 0:2], rr[:, 2:4]
        mrow = sb("mrow", [P, 2, J, D])
        sel = sb("sel", [P, 2, J, P])
        wt = sb("wt", [TERMS, 2, T], BF16)
        attr_parts = sb("attr_parts", [P, 3, ATTRS * NS // P], BF16)
        found = sb("found", [P, 2, J])
        zcol = sb("zcol", [P, 1])
        di, dp, dn, slot_i = sb("di", h, I32), sb("dp", h, I32), sb("dn", h, I32), sb("slot_i", h, I32)
        ordb = sb("ordb", h, U8)
        idx_all = sb("idx_all", [P, NC], I32)
        slot_all = sb("slot_all", [P, NC])
        wqT_s, wkT_s = sb("wqT_s", [P, LAYERS, D]), sb("wkT_s", [P, LAYERS, D + 1])
        bq_s = sb("bq_s", [P, LAYERS])
        minus = ob.rearrange("p a j f -> p (a j f)")[:, 0:800]
        lg = sb("lg", [P, 2, J])
        junk = sb("junk", [P, J, D + 1])
        estat = sb("estat", [P, J, 6])
        emv = sb("emv", [P, 2, J, 2])
        ers, eri, ebias = sb("ers", [P, J]), sb("eri", [P, 2, J]), sb("ebias", [P, 2, J])

        bank = [pb(f"bank{k}") for k in range(8)]

        s_w, s_b, s_seg, s_mapset, s_id, s_iota = (sem(n) for n in ("s_w", "s_b", "s_seg", "s_mapset", "s_id", "s_iota"))
        skip_in = [sem(f"skip_in{k}") for k in range(4)]
        x_in = [sem(f"x_in{k}") for k in range(4)]
        o_out = [sem(f"o_out{k}") for k in range(2)]
        dA, dB, dC, dD, dE, dF = (sem(f"pe_d{n}") for n in "ABCDEF")
        xT_r, x1T_r, h1T_r, h2T_r = (sem(n) for n in ("xT_r", "x1T_r", "h1T_r", "h2T_r"))
        cN = sem("cN")
        sqN, oN = sem("sqN"), sem("oN")
        KN, KT = 6, 4
        Z, Y, X1 = 1, 2, 5

        block = ctx.enter_context(nc.Block())

        def pipeline(eng, step, last, nodes_from=None, every=1, nodes_until=None, back=10):
            end, block = iterations_end(last), UNROLL * every

            def node_at(i):
                if nodes_from is None or i % every or (nodes_until is not None and i >= nodes_until):
                    return None
                return nodes_from + (i - FIRST) // every

            def stages(i):
                edge = [0 <= i - s < NT for s in range(-2, back + 1)]
                n = node_at(i - i % every)
                return edge + [n is not None and 0 <= n - s < DENSE_TILES for s in range(-3, 11)]

            def run(i, known, turn=0):
                n = node_at(known)
                if n is None:
                    node = (0, 0, lambda s: False)
                else:
                    node = (turn * UNROLL + n if known is not i else n, n % UNROLL, lambda s: 0 <= n - s < DENSE_TILES)
                step(i, known % UNROLL, lambda s: 0 <= known - s < NT, node)

            i = FIRST
            while i < end:
                blocks = 0
                while i + block * (blocks + 1) <= end and all(
                        stages(k) == stages(i) for k in range(i + block * blocks, i + block * (blocks + 1))):
                    blocks += 1
                if blocks > 1:
                    with eng.Fori(0, blocks) as r:
                        for k in range(i, i + block):
                            run(r * block + k, k, r)
                    i += block * blocks
                else:
                    for k in range(i, i + UNROLL):
                        run(k, k)
                    i += UNROLL

        def settle(eng):
            eng.sem_inc(s_passed, 1)

        def after(eng, chain, n):
            if not (isinstance(n, int) and n <= 0):
                eng.wait_ge(chain, n)

        def count(base, t, k=1):
            return t * k + (base + k)

        def slot_count(base, t, u, ring, by=16):
            return (t - u) * (by // ring) + (base + by)

        def node_slots(ring, u):
            return 16 * len(range(u, DENSE_TILES, ring))

        def in_slot(ring, u, phases, by=16):
            return by * phases * len(range(u, NT, ring))

        def bias_rows(at, n, copies):
            return biases[:, at:at + n].unsqueeze(1).broadcast_to([SPLIT, copies, n])

        def node_row(t):
            return t * T if not isinstance(t, int) else min(t * T, N_NODES - T)

        def rows_of(a, r0):
            return a[bass.ds(r0, T), :].rearrange("(p j) f -> p j f", p=P)

        def step_at(i, step):
            return i * KN + (step - KN)

        def node_load(sp, i, u, on):
            if on(-2):
                t, k = i + 2, (u + 2) % 4
                if not isinstance(t, int) or t >= 4:
                    sp.wait_ge(cN, step_at(t - 3, Y))
                sp.dma_start(xr[:, k], rows_of(x, node_row(t))).then_inc(x_in[k], 16)

        def node_store(sp, i, u, on):
            if on(9):
                t, k = i - 9, (u - 9) % 2
                sp.wait_ge(oN, count(0, t))
                if isinstance(t, int) and t == DENSE_TILES - 1:
                    sp.wait_ge(o_out[1 - k], node_slots(2, 1 - k))
                sp.dma_start(rows_of(out, node_row(t)), ob[:, k]).then_inc(o_out[k], 16)

        def node_pe(pe, i, u, on, y_bank=1):
            if on(0):
                t, k = i, u % 4
                pe.wait_ge(x_in[k], slot_count(0, t, k, 4))
                if on(5):
                    pe.wait_ge(h1T_r, count(0, i - 5))
                elif on(1):
                    pe.wait_ge(xT_r, count(0, i - 1))
                for j in range(J):
                    mm = nc.tensor.transpose(bank[0][:, j * P:(j + 1) * P], xr[:, k, j, :], ident[:, :])
                mm.then_inc(dA, 1)
            def h3():
                if on(6):
                    t, k = i - 6, (u - 6) % 2
                    pe.wait_ge(h2T_r, count(0, t))
                    pe.wait_ge(x1T_r, count(0, min(i - 4, DENSE_TILES - 1) if isinstance(i, int) else i - 4))
                    if on(7) and not on(4):
                        pe.wait_ge(cN, step_at(i - 1, Z if y_bank == 1 else 2))
                    nc.tensor.matmul(bank[2][:, :].rearrange("p (j f) -> p j f", j=J), parts[:, :],
                                     bias_rows(LAST_AT, D, J), start=True, stop=False)
                    for j in range(J):
                        mm = nc.tensor.matmul(bank[2][:, j * P:(j + 1) * P], h2T[:, k, j * P:(j + 1) * P], ws_s[:, 2, :],
                                              start=False, stop=j == J - 1)
                    mm.then_inc(dF, 1)

            def y():
                if on(1):
                    t, k = i - 1, (u - 1) % 2
                    pe.wait_ge(xT_r, count(0, t))
                    if on(6) and y_bank == 1:
                        pe.wait_ge(h2T_r, count(0, i - 6))
                    elif on(2):
                        pe.wait_ge(cN, step_at(i - 1, Y))
                    for j in range(J):
                        mm = nc.tensor.matmul(bank[y_bank][:, j * P:(j + 1) * P], xT[:, k, j * P:(j + 1) * P], w2a_s[:, :],
                                              start=True, stop=True)
                    mm.then_inc(dB, 1)

            for part in (h3, y) if y_bank == 1 else (y, h3):
                part()
            if on(4):
                t, k = i - 4, u % 2
                pe.wait_ge(x1T_r, count(0, t))
                pe.wait_ge(xT_r, count(0, min(i, DENSE_TILES - 1) if isinstance(i, int) else i))
                if on(5) and not on(0):
                    pe.wait_ge(h1T_r, count(0, t - 1))
                nc.tensor.matmul(bank[0][:, :], ws_s[:, 0, :], x1T[:, k, :], start=True, stop=True).then_inc(dD, 1)
            if on(3):
                t, k = i - 3, (u - 3) % 4
                pe.wait_ge(cN, step_at(t + 2, X1))
                if on(6):
                    pe.wait_ge(cN, step_at(i, Z if y_bank == 1 else 2))
                elif on(4):
                    pe.wait_ge(x1T_r, count(0, i - 4))
                for j in range(J):
                    mm = nc.tensor.transpose(bank[2][:, j * P:(j + 1) * P], x1[:, k, j, :], ident[:, :])
                mm.then_inc(dC, 1)
            if on(5):
                t, k = i - 5, (u - 5) % 2
                pe.wait_ge(h1T_r, count(0, t))
                pe.wait_ge(cN, step_at(min(i, DENSE_TILES) if isinstance(i, int) else i, Y))
                if on(6) and (y_bank != 1 or not on(1)):
                    pe.wait_ge(h2T_r, count(0, t - 1))
                nc.tensor.matmul(bank[1][:, :], ws_s[:, 1, :], h1T[:, k, :], start=True, stop=True).then_inc(dE, 1)

        def node_x(act, i, u, on):
            if on(0):
                t, k = i, u % 2
                act.wait_ge(dA, count(0, t))
                if on(2):
                    act.wait_ge(dB, count(0, t - 2))
                nc.scalar.activation(xT[:, k, :], bank[0][:, :], ACT.Copy).then_inc(xT_r, 1)

        def node_act(act, i, u, on):
            if on(2) or on(7):
                act.wait_ge(cN, step_at(i, 0))
                root(mv[:, (u - 1) % 2, before(on), :, 1], rs[:, before(on)], sqN)
            node_out(act, i, u, on)
            if on(4):
                t, k = i - 4, u % 2
                act.wait_ge(dD, count(0, t))
                if on(6):
                    act.wait_ge(dE, count(0, t - 2))
                nc.scalar.activation(h1T[:, k, :], bank[0][:, :], ACT.Relu, bias=bscol_s[:, 0:1]).then_inc(h1T_r, 1)
            if on(3):
                t, k = i - 3, (u - 3) % 2
                act.wait_ge(dC, count(0, t))
                if on(5):
                    act.wait_ge(dD, count(0, t - 2))
                nc.scalar.activation(x1T[:, k, :], bank[2][:, :], ACT.Copy).then_inc(x1T_r, 1)
            if on(5):
                t, k = i - 5, (u - 5) % 2
                act.wait_ge(dE, count(0, t))
                if on(7):
                    act.wait_ge(dF, count(0, t - 2))
                nc.scalar.activation(h2T[:, k, :], bank[1][:, :], ACT.Relu, bias=bscol_s[:, 1:2]).then_inc(h2T_r, 1)

        def node_out(act, i, u, on):
            if on(8):
                t, k = i - 8, u % 2
                act.wait_ge(cN, step_at(i - 1, 5))
                if on(10):
                    act.wait_ge(o_out[k], slot_count(0, t - 2, k, 2))
                for j in range(J):
                    op = nc.scalar.activation(ob[:, k, j, :], zb[:, u % 4, j, :], ACT.Identity,
                                              scale=ri[:, u % 4, 0, j:j + 1], bias=fbias[:, u % 4, j:j + 1])
                op.then_inc(oN, 1)

        def passed(dve, chain, at):
            after(dve, chain, at)
            dve.sem_inc(chain, 1)

        def sums(dve, rows, chain, at):
            after(dve, chain, at)
            for src, st in rows:
                for j in range(J):
                    op = nc.vector.bn_stats(st[:, j, :], src[:, j, :])
            op.then_inc(chain, 1)

        def means(dve, rows, chain, at):
            dve.wait_ge(chain, at)
            settle(dve)
            for st, m in rows:
                for j in range(J):
                    op = nc.vector.bn_aggr(m[:, j, :], st[:, j, :])
            op.then_inc(chain, 1)

        def root(variance, r, done):
            nc.scalar.activation(r, variance, ACT.Sqrt, bias=eps_s[:, 0:1]).then_inc(done, 1)

        def minus_mean(out, m, inv):
            return nc.vector.scalar_tensor_tensor(out, m[:, :, 0], -1.0, inv, ALU.mult, ALU.mult)

        def before(on):
            return slice(0 if on(7) else 1, 2 if on(2) else 1)

        def has_sums(on):
            return on(1) or on(6)

        def had_sums(on):
            return on(2) or on(7)

        def node_zy(dve, i, u, on, y_bank=1):
            if not (has_sums(on) or had_sums(on)):
                return
            at = step_at(i, 0)
            after(dve, cN, at - 1)
            def z(n):
                if on(6):
                    dve.wait_ge(dF, count(0, i - 6))
                    if on(10):
                        dve.wait_ge(oN, count(0, i - 10))
                    nc.vector.tensor_tensor(zb[:, (u - 6) % 4], bank[2][:, :].rearrange("p (j f) -> p j f", j=J),
                                            x1[:, (u - 6) % 4], ALU.add).then_inc(cN, 1)
                else:
                    passed(dve, cN, n)

            def y(n):
                if on(1):
                    dve.wait_ge(dB, count(0, i - 1))
                    nc.vector.scalar_tensor_tensor(yb[:, (u - 1) % 2], bank[y_bank][:, :].rearrange("p (j f) -> p j f", j=J), 0.0,
                                                   xr[:, (u - 1) % 4], ALU.max, ALU.add).then_inc(cN, 1)
                else:
                    passed(dve, cN, n)

            for n, part in enumerate((z, y) if y_bank == 1 else (y, z)):
                part(at + n)

        def node_inv(dve, i, u, on):
            at = step_at(i, 0)
            if had_sums(on):
                dve.wait_ge(sqN, count(0, i - 2))
                nc.vector.reciprocal(ri[:, (u - 7) % 4, before(on)], rs[:, before(on)]).then_inc(cN, 1)
            elif has_sums(on):
                passed(dve, cN, at + 2)

        def node_sums(dve, i, u, on):
            at = step_at(i, 0)
            if has_sums(on):
                sums(dve, [(zb[:, (u - 6) % 4], stat[:, 0])] * on(6) + [(yb[:, (u - 1) % 2], stat[:, 1])] * on(1), cN, at + 2)
            elif had_sums(on):
                passed(dve, cN, at + 3)

        def node_norm(dve, i, u, on):
            at, r = step_at(i, 0), (u - 1) % 2
            if had_sums(on):
                dve.wait_ge(cN, at + 3)
                if on(7):
                    op = minus_mean(fbias[:, (u - 7) % 4], mv[:, r, 0], ri[:, (u - 7) % 4, 0])
                if on(2):
                    for j in range(J):
                        op = nc.vector.tensor_scalar(x1[:, (u - 2) % 4, j, :], yb[:, u % 2, j, :], mv[:, r, 1, j, 0:1],
                                                     ri[:, (u - 7) % 4, 1, j:j + 1], ALU.subtract, ALU.mult)
                op.then_inc(cN, 1)
            elif has_sums(on):
                passed(dve, cN, at + 4)

        def node_means(dve, i, u, on):
            at, r = step_at(i, 0), u % 2
            if has_sums(on):
                means(dve, [(stat[:, 0], mv[:, r, 0])] * on(6) + [(stat[:, 1], mv[:, r, 1])] * on(1), cN, at + 4)
            elif had_sums(on):
                passed(dve, cN, at + 5)

        def edge_inv(dve, s, k, i, u, on, chain, at, roots):
            if on(s + 1):
                dve.wait_ge(e_sq, count(roots, i - s - 1))
                nc.vector.reciprocal(eri[:, (u - s - 1) % 2], ers[:, :]).then_inc(chain, 1)
            elif on(s):
                passed(dve, chain, at + k)

        def edge_sums(dve, s, k, i, u, on, chain, at, src):
            if on(s):
                sums(dve, [(src, estat)], chain, at + k)
            elif on(s + 1):
                passed(dve, chain, at + k + 1)

        def edge_means(dve, s, k, i, u, on, chain, at):
            if on(s):
                means(dve, [(estat, emv[:, (u - s) % 2])], chain, at + k + 2)
            elif on(s + 1):
                passed(dve, chain, at + k + 3)

        def edge_minus_mean(dve, s, k, i, u, on, chain, at):
            r = (u - s - 1) % 2
            if on(s + 1):
                dve.wait_ge(chain, at + k + 1)
                minus_mean(ebias[:, r], emv[:, r], eri[:, r]).then_inc(chain, 1)
            elif on(s):
                passed(dve, chain, at + k + 2)

        def edge_rows(a, t, base=0):
            return a[bass.ds(t * T + base, T), :].rearrange("(j p) f -> p j f", p=P)


        i_in = [sem(f"i_in{k}") for k in range(4)]
        m_out = [sem(f"m_out{k}") for k in range(4)]
        g_in = [sem(f"g_in{k}") for k in range(4)]
        f_in = [sem(f"f_in{k}") for k in range(2)]
        f_out = [sem(f"f_out{k}") for k in range(2)]
        w_in = [sem(f"w_in{k}") for k in range(2)]
        S_out = [[sem(f"S_out{n}{k}") for k in range(2)] for n in range(4)]
        s_e, s_a, s_v = ([sem(f"S_{w}{n}") for n in range(m)] for w, m in (("pe", 8), ("act", 7), ("dve", 1)))
        ti_in = [sem(f"ti_in{k}") for k in range(4)]
        tg_in = [sem(f"tg_in{k}") for k in range(4)]
        rows_in = [sem(f"rows_in{k}") for k in range(4)]
        t_out = [sem(f"t_out{k}") for k in range(2)]
        t_e, t_v = ([sem(f"T_{w}{n}") for n in range(3)] for w in ("pe", "dve"))
        t_a = sem("t_a")
        ai_in = [sem(f"ai_in{k}") for k in range(4)]
        ag_in = [sem(f"ag_in{k}") for k in range(4)]
        ah_out = [sem(f"ah_out{k}") for k in range(4)]
        as_out = [sem(f"as_out{k}") for k in range(2)]
        a_e, a_v = ([sem(f"A_{w}{n}") for n in range(m)] for w, m in (("pe", 3), ("dve", 2)))
        a_a = sem("a_a")
        b_out = [sem(f"b_out{k}") for k in range(2)]
        b_e, b_v = ([sem(f"B_{w}{n}") for n in range(m)] for w, m in (("pe", 2), ("dve", 3)))
        b_a = sem("b_a")
        bi_in = [sem(f"bi_in{k}") for k in range(4)]
        s_tail, s_row, s_crow, s_col, s_chain = (sem(n) for n in ("s_tail", "s_row", "s_crow", "s_col", "s_chain"))
        s_lt, s_exp, s_al, s_at, s_arg = (sem(n) for n in ("s_lt", "s_exp", "s_al", "s_at", "s_arg"))
        s_p0, s_p1, s_p2, s_ordout, s_ordin, s_scout = (sem(n) for n in ("s_p0", "s_p1", "s_p2", "s_ordout", "s_ordin", "s_scout"))
        s_prep, s_fixi, s_fixg, s_fixw, s_fd, s_fc, s_fo, s_wt = (sem(n) for n in (
            "s_prep", "s_fixi", "s_fixg", "s_fixw", "s_fd", "s_fc", "s_fo", "s_wt"))
        s_fin = [sem(f"s_fin{k}") for k in range(2)]
        s_vl = sem("s_vl")
        s_passed = sem("s_passed")
        s_attr, s_parts = sem("s_attr"), sem("s_parts")
        e_sq = sem("e_sq")
        e_o = sem("e_o")
        a_k = sem("a_k")

        def chunk_rows(v):
            return v.rearrange("p (j f) -> p j f", j=J)

        def wait_all(eng, pairs):
            for s, n in pairs:
                eng.wait_ge(s, n)

        node_end = [(o_out[k], node_slots(2, k)) for k in range(2)]

        prep_end = [(s_attr, 32), (s_parts, 1), (s_w, 160), (s_chain, 3), (s_p0, 2), (s_scout, 16), (s_mapset, 16)]
        map_end = [(s_attr, 80), (s_ordin, 16)] + [(m_out[k], in_slot(4, k, 1, 64)) for k in range(4)]
        src_end = [(q[k], in_slot(2, k, 1)) for q in S_out for k in range(2)] + [(s_prep, len(FIRSTM_AT))]
        dst_end = [(q[k], in_slot(2, k, 1)) for q in (t_out, f_out) for k in range(2)]

        def nodes_seen(l):
            if l == LAYERS - 1:
                return node_end
            n = A_NODES[l + 1]
            return ([(q, min(n - s, DENSE_TILES)) for q, s in ((xT_r, 0), (x1T_r, 3), (h1T_r, 4), (h2T_r, 5), (oN, 8))]
                    + [(cN, min(n - 1, DENSE_TILES + 6) * KN)])

        def a_end(l):
            return ([(ah_out[k], in_slot(4, k, l + 1)) for k in range(4)]
                    + [(as_out[k], in_slot(2, k, l + 1)) for k in range(2)]
                    + [(a_v[0], 5 * NT * (l + 1))] + nodes_seen(l))

        def b_end(l):
            return ([(b_out[k], in_slot(2, k, l + 1)) for k in range(2)] + [(b_v[1], 4 * NT * (l + 1))]
                    if l < LAYERS - 1 else [])

        def select(t, k, weight, done, chunks=range(J)):
            for j in chunks:
                cols = bass.ds(t * T + j * P, P)
                c = bass.ds(t * J + j, 1)
                if weight is None:
                    op = nc.vector.tensor_scalar(sel[:, k, j, :], ordrow[:, cols], ordcol[:, c], None, ALU.is_equal)
                else:
                    op = nc.vector.tensor_scalar(sel[:, k, j, :], ordrow[:, cols], ordcol[:, c], weight[:, c],
                                                 ALU.is_equal, ALU.mult)
            if j == J - 1:
                op.then_inc(done, 1)

        def carry(dve, t, k, j, ps, chain, at):
            after(dve, chain, at + j)
            before = g1T[:, k, j * P - 1:j * P] if j else g1T[:, 1 - k, T - 1:T]
            if isinstance(t, int) and t == 0 and j == 0:
                before = zcol[:, :]
            nc.vector.scalar_tensor_tensor(g1T[:, k, j * P:(j + 1) * P], firstm[:, bass.ds(t * T + j * P, P)],
                                           before, ps[:, j * P:(j + 1) * P], ALU.mult, ALU.add).then_inc(chain, 1)

        def over_chunks_dve(dve, q, kind, a, b, o):
            rev = kind == "back"
            ops = (ALU.add, ALU.max) if kind == "max" else (ALU.mult, ALU.add)
            first = -BIG if kind == "max" else 0.0
            coef = {"max": nb_row, "add": nostart_row, "back": nolast_row}[kind]

            def within(initial):
                for k in range(2):
                    w = slice(None, None, -1) if rev else slice(None)
                    op = nc.vector.tensor_tensor_scan(o[:, k, w], a[:, k, w], b[:, k, w],
                                                      incol[:, k:k + 1] if initial is None else initial, *ops)
                return op

            within(first).then_inc(s_tail, 1)
            nc.vector.memset(crow[:, NC:NC + 1] if rev else crow[:, 0:1], first).then_inc(s_chain, 1)
            dve.wait_ge(s_row, q + 1)
            ends = bank[6][0:1, 0:NC]
            if rev:
                nc.vector.tensor_tensor_scan(crow[:, NC - 1::-1], coef[:, ::-1], ends[:, ::-1], first, *ops).then_inc(s_crow, 1)
            else:
                nc.vector.tensor_tensor_scan(crow[:, 1:NC + 1], coef[:, :], ends, first, *ops).then_inc(s_crow, 1)
            dve.wait_ge(s_col, q + 1)
            nc.vector.tensor_copy(incol[:, :], bank[7][0:HC, 0:2]).then_inc(s_chain, 1)
            dve.wait_ge(s_chain, 3 * q + 2)
            within(None).then_inc(s_chain, 1)
            dve.wait_ge(s_chain, 3 * q + 3)

        def over_chunks_pe(pe, q, kind, o):
            rev = kind == "back"
            pe.wait_ge(s_tail, q + 1)
            if q:
                pe.wait_ge(s_crow, q)
            e = 0 if rev else P - 1
            for k in range(2):
                mm = nc.tensor.matmul(bank[6][0:1, k * HC:(k + 1) * HC], o[:, k, e:e + 1], ident[0:HC, 0:HC],
                                      start=True, stop=True)
            mm.then_inc(s_row, 1)
            pe.wait_ge(s_crow, q + 1)
            pe.wait_ge(s_chain, 3 * q + 1)
            f = 1 if rev else 0
            for k in range(2):
                mm = nc.tensor.matmul(bank[7][0:HC, k:k + 1], crow[0:1, f + k * HC:f + (k + 1) * HC], one[0:1, 0:1],
                                      start=True, stop=True)
            mm.then_inc(s_col, 1)

        def ends_view(shift):
            return bass.AP(dst_pad.tensor, shift, [[P, HC], [HC * P, 2], [1, P]])

        bias_raw = sel.rearrange("p a j e -> p (a j e)")[0:SPLIT, 0:NBIAS]
        bias_rest = rr.rearrange("p a j e -> p (a j e)")[0:SPLIT, 0:NBIAS]
        bq_wide = x1[:, 0].rearrange("p j f -> p (j f)")[:, 0:LAYERS * SPLIT]

        w1b_rows = x1[0:TERMS, 1, 0, :]
        w1b_rest = x1[0:TERMS, 1, 1, :]
        w1b_part = x1[0:TERMS, 1, 2, :]
        attr_raw = zb.rearrange("p a j f -> p (a j f)")[:, 0:ATTRS * NS // P]
        attr_rest = ey.rearrange("p a j f -> p (a j f)")[:, 0:ATTRS * NS // P]

        @block.sync
        def _(sp):
            for a, b in ((w1a_s, w1a), (w1b_rows, w1b), (w2a_s, w2a), (w2b_s, w2b)):
                sp.dma_start(a[:, :], b).then_inc(s_w, 16)
            for a, b in ((ws_s, ws), (wv_s, wv), (wqT_s, wqT), (wkT_s, wkT)):
                sp.dma_start(a[:, :, :], b).then_inc(s_w, 16)
            sp.dma_start(bq_s[:, :], bq).then_inc(s_w, 16)
            sp.dma_start(bscol_s[:, :], bs_col).then_inc(s_w, 16)
            sp.dma_start(attr_raw, wT.rearrange("a (q n) -> (a q) n", q=P // ATTRS)).then_inc(s_attr, 16)
            sp.dma_start(which[:, :], which_part).then_inc(s_attr, 16)
            for a, shift in ((dp, 0), (di, 1), (dn, 2)):
                sp.dma_start(a[:, :, :], ends_view(shift)).then_inc(s_seg, 16)
            sp.dma_start(slot_all[:, :].rearrange("p (t j) -> p t j", j=J),
                         slot_ids.rearrange("t p j -> p t j")).then_inc(s_seg, 16)
            sp.dma_start(bias_raw[:, SKIP_AT:LAST_AT], bass.AP(bs.tensor, 0, [[0, SPLIT], [1, LAYERS * D]])).then_inc(s_b, 16)
            sp.dma_start(bias_rest[:, 0:LAYERS * D], bass.AP(bv.tensor, 0, [[0, SPLIT], [1, LAYERS * D]])).then_inc(s_b, 16)
            sp.wait_ge(s_p0, 1)
            sp.dma_start(map_d.rearrange("(p n) o -> p (n o)", p=125), minus[0:125, :]).then_inc(s_mapset, 16)
            sp.wait_ge(s_p1, 1)
            sp.dma_start(bass.AP(ord_d.tensor, 0, [[P, HC], [HC * P, 2], [1, P]]), ordb[:, :, :]).then_inc(s_ordout, 16)
            sp.wait_ge(s_ordout, 16)
            sp.dma_start(ordrow[:, :], bass.AP(ord_d.tensor, 0, [[0, P], [1, NS]])).then_inc(s_ordin, 16)
            sp.wait_ge(s_p2, 1)
            sp.dma_start(scat_d.rearrange("t p j -> p t j"),
                         idx_all[:, :].rearrange("p (t j) -> p t j", j=J)).then_inc(s_scout, 16)
            sp.wait_ge(s_scout, 16)

            def map_step(i, u, on, node):
                node_load(sp, *node)
                if on(-2):
                    t, k = i + 2, (u + 2) % 4
                    if not isinstance(t, int) or t >= 4:
                        sp.wait_ge(m_out[k], slot_count(0, t - 4, k, 4, 64))
                        settle(sp)
                    sp.dma_start(gi[:, k, :], scat_d[bass.ds(t, 1)].rearrange("o p j -> p (o j)")).then_inc(i_in[k], 16)
                    sp.dma_start(slotv[:, k, :], slot_ids[bass.ds(t, 1)].rearrange("o p j -> p (o j)")).then_inc(i_in[k], 16)
                node_store(sp, *node)
            pipeline(sp, map_step, MAP_LAST, MAP_NODES)
            wait_all(sp, map_end)

            def src_step(i, u, on, node):
                node_load(sp, *node)
                if on(-2):
                    t, k = i + 2, (u + 2) % 4
                    if not isinstance(t, int) or t >= 4:
                        sp.wait_ge(g_in[k], slot_count(0, t - 4, k, 4, 64))
                        settle(sp)
                    sp.dma_start(gi[:, k, :], xsrc_idx[bass.ds(t, 1)].rearrange("o p j -> p (o j)")).then_inc(
                        i_in[k], 16)
                if on(0):
                    t, k = i, u % 2
                    if on(2):
                        sp.wait_ge(s_e[1], count(0, t - 2))
                        settle(sp)
                    for n in range(3):
                        sp.dma_start(wt[n * 3 * ATTRS:(n + 1) * 3 * ATTRS, k, :], attr_d[:, bass.ds(t * T, T)]).then_inc(
                            w_in[k], 16)
                if on(2):
                    t, k = i - 2, u % 2
                    sp.wait_ge(s_a[1], count(0, t))
                    settle(sp)
                    sp.dma_start(edge_rows(msg_d, t), mrow[:, k]).then_inc(S_out[0][k], 16)
                if on(3):
                    t, k = i - 3, (u - 3) % 2
                    sp.wait_ge(s_v[0], (i - 2) * 5 + 4)
                    settle(sp)
                    sp.dma_start(edge_rows(U[0], t, NS), e1[:, k]).then_inc(S_out[1][k], 16)
                if on(6):
                    t, k = i - 6, u % 2
                    sp.wait_ge(s_a[4], count(0, t))
                    settle(sp)
                    sp.dma_start(edge_rows(U[1], t, NS), r1[:, k]).then_inc(S_out[2][k], 16)
                if on(7):
                    t, k = i - 7, (u - 7) % 2
                    sp.wait_ge(s_a[6], count(0, t))
                    settle(sp)
                    sp.dma_start(edge_rows(U[2], t, NS), r2[:, k]).then_inc(S_out[3][k], 16)
                node_store(sp, *node)
            pipeline(sp, src_step, SRC_LAST, SRC_NODES)
            wait_all(sp, src_end)

            def dst_step(i, u, on, node):
                node_load(sp, *node)
                if on(-2):
                    t, k = i + 2, (u + 2) % 4
                    if not isinstance(t, int) or t >= 4:
                        sp.wait_ge(tg_in[k], slot_count(0, t - 4, k, 4, 128))
                        settle(sp)
                    sp.dma_start(gi[:, k, :], xdst_idx[bass.ds(t, 1)].rearrange("o p j -> p (o j)")).then_inc(
                        ti_in[k], 16)
                    sp.dma_start(gm[:, k, :], xsrc_idx[bass.ds(t, 1)].rearrange("o p j -> p (o j)")).then_inc(
                        ti_in[k], 16)
                    if not isinstance(t, int) or t >= 4:
                        sp.wait_ge(t_e[1], count(0, t - 4))
                        settle(sp)
                    sp.dma_start(rr[:, k], edge_rows(msg_d, t)).then_inc(rows_in[k], 16)
                if on(2):
                    t, k, k4 = i - 2, u % 2, (u - 2) % 4
                    sp.wait_ge(tg_in[k4], slot_count(0, t, k4, 4, 128))
                    settle(sp)
                    sp.dma_start(found_d[bass.ds(t, 1)].rearrange("o p j -> p (o j)"), found[:, k, :]).then_inc(
                        f_out[k], 16)
                if on(7):
                    t, k = i - 7, (u - 7) % 2
                    sp.wait_ge(e_o, count(0, t))
                    settle(sp)
                    sp.dma_start(edge_rows(U[0], t), e1[:, k]).then_inc(t_out[k], 16)
                node_store(sp, *node)
            pipeline(sp, dst_step, DST_LAST, DST_NODES, nodes_until=DST_NODES_UNTIL)
            wait_all(sp, dst_end)
            sp.dma_start(logit_c[:, :].rearrange("p (t j) -> p t j", j=J), found_d.rearrange("t p j -> p t j")).then_inc(s_fd, 16)
            sp.wait_ge(s_fc, 3)
            sp.dma_start(srcslot_d.rearrange("t p j -> p t j"),
                         idx_all[:, :].rearrange("p (t j) -> p t j", j=J)).then_inc(s_fo, 16)
            sp.wait_ge(s_fo, 16)

            def fix(l):
                sp.wait_ge(s_fixg, 32 * (l + 1))
                for k in range(2):
                    sp.dma_start(bass.AP(U[l].tensor, (k * HC * P + P - 1) * D, [[P * D, HC], [1, D]]),
                                 fixrow[:, k, :]).then_inc(s_fixw, 16)
                sp.wait_ge(s_fixw, 32 * (l + 1))

            for l in range(LAYERS):
                fix(l)

                def a_step(i, u, on, node, l=l):
                    b0 = l * NT
                    node_load(sp, *node)
                    if on(-2):
                        t, k = i + 2, (u + 2) % 4
                        if not isinstance(t, int) or t >= 4:
                            sp.wait_ge(ag_in[k], slot_count(in_slot(4, k, l, 64), t - 4, k, 4, 64))
                            settle(sp)
                        sp.dma_start(gi[:, k, :], srcslot_d[bass.ds(t, 1)].rearrange("o p j -> p (o j)")).then_inc(
                            ai_in[k], 16)
                        if not isinstance(t, int) or t >= 4:
                            sp.wait_ge(a_e[0], count(b0, t - 4))
                            settle(sp)
                        sp.dma_start(rr[:, k], edge_rows(U[l], t)).then_inc(rows_in[k], 16)
                    if l == LAYERS - 1 and on(0):
                        t, k = i, u % 4
                        if not isinstance(t, int) or t >= 4:
                            sp.wait_ge(a_k, count(b0, t - 4))
                            settle(sp)
                        sp.dma_start(ey[:, k], edge_rows(U[0], t)).then_inc(skip_in[k], 16)
                    if on(2):
                        t, k = i - 2, (u - 2) % 4
                        sp.wait_ge(ag_in[k], slot_count(in_slot(4, k, l, 64), t, k, 4, 64))
                        settle(sp)
                        sp.dma_start(edge_rows(hs_d, t), er[:, k, :, 0:D]).then_inc(ah_out[k], 16)
                    if on(4):
                        t, k = i - 4, u % 2
                        sp.wait_ge(a_k, count(b0, t))
                        settle(sp)
                        sp.dma_start(edge_rows(skip_d, t), mrow[:, k]).then_inc(as_out[k], 16)
                    node_store(sp, *node)
                pipeline(sp, a_step, A_LAST, A_NODES[l], A_EVERY, back=6)
                wait_all(sp, a_end(l))

                def b_step(i, u, on, node, l=l):
                    b0 = l * NT
                    tail = l == LAYERS - 1
                    if on(-2):
                        t, k = i + 2, (u + 2) % 4
                        if not isinstance(t, int) or t >= 4:
                            sp.wait_ge(b_e[0], count(b0, t - 4))
                            settle(sp)
                        sp.dma_start(er[:, k, :, 0:D], edge_rows(hs_d, t)).then_inc(rows_in[k], 16)
                    if on(0):
                        t, k = i, u % 4
                        if not isinstance(t, int) or t >= 4:
                            sp.wait_ge(b_e[1], count(b0, t - 4))
                            settle(sp)
                        sp.dma_start(rr[:, k], edge_rows(skip_d, t)).then_inc(skip_in[k], 16)
                    if not tail and on(5):
                        t, k = i - 5, (u - 5) % 2
                        sp.wait_ge(b_a, count(b0, t))
                        settle(sp)
                        sp.dma_start(edge_rows(U[l + 1], t), e1[:, k]).then_inc(b_out[k], 16)
                pipeline(sp, b_step, B_LAST)
                wait_all(sp, b_end(l))
            wait_all(sp, [(s_fin[k], in_slot(2, k, 1, 64)) for k in range(2)])

        @block.gpsimd
        def _(gp):
            gp.memset(ident[:, :], 0.0).then_inc(s_id, 1)
            gp.wait_ge(s_id, 1)
            gp.affine_select(out=ident[:, :], in_=ident[:, :], compare_op=ALU.not_equal, fill=1.0, base=0,
                             pattern=[[-1, P]], channel_multiplier=1).then_inc(s_id, 1)
            gp.memset(one[:, :], 1.0).then_inc(s_id, 1)
            gp.memset(zcol[:, :], 0.0).then_inc(s_id, 1)
            gp.memset(er[:, :, :, :], 1.0).then_inc(s_id, 1)
            gp.iota(slot_i[:, :, :], pattern=[[HC * P, 2], [1, P]], base=0, channel_multiplier=P).then_inc(s_iota, 1)
            gp.wait_ge(s_id, 5)
            wait_all(gp, prep_end)

            def map_step(i, u, on, node):
                if on(-1):
                    t, k = i + 1, (u + 1) % 4
                    gp.wait_ge(i_in[k], slot_count(0, t, k, 4, 32))
                    settle(gp)
                    for j in range(J):
                        gp.indirect_dma_start(map_d, bass.IndirectOffsetOnAxis(gi[:, k, j:j + 1], 0), slotv[:, k, j:j + 1],
                                              None, bounds_check=N_NODES - 1, oob_is_err=False).then_inc(m_out[k], 16)
            pipeline(gp, map_step, MAP_LAST, MAP_NODES)
            wait_all(gp, map_end)

            def src_step(i, u, on, node):
                if isinstance(i, int) and i in FIRSTM_AT:
                    n = FIRSTM_AT.index(i) * NS // len(FIRSTM_AT)
                    piece = slice(n, n + NS // len(FIRSTM_AT))
                    nc.gpsimd.tensor_scalar(firstm[:, piece], ordrow[:, piece], 0.0, None, ALU.is_equal).then_inc(s_prep, 1)
                if on(-1):
                    t, k = i + 1, (u + 1) % 4
                    gp.wait_ge(i_in[k], slot_count(in_slot(4, k, 1, 32), t, k, 4, 16))
                    if not isinstance(t, int) or t >= 4:
                        gp.wait_ge(s_e[0], count(0, t - 4))
                        gp.wait_ge(s_v[0], (t - 4) * 5 + 1)
                        settle(gp)
                    for j in range(J):
                        gp.indirect_dma_start(er[:, k, j, 0:D], None, x, bass.IndirectOffsetOnAxis(gi[:, k, j:j + 1], 0)
                                              ).then_inc(g_in[k], 16)
            pipeline(gp, src_step, SRC_LAST, SRC_NODES)
            wait_all(gp, src_end)

            def dst_step(i, u, on, node):
                if on(1):
                    t, k = i - 1, (u - 1) % 4
                    k2 = (u - 1) % 2
                    gp.wait_ge(ti_in[k], slot_count(0, t, k, 4, 32))
                    if not isinstance(t, int) or t >= 4:
                        gp.wait_ge(t_e[0], count(0, t - 4))
                        gp.wait_ge(t_v[2], (t - 4) * 5 + 1)
                    if not isinstance(t, int) or t >= 2:
                        gp.wait_ge(f_out[k2], slot_count(0, t - 2, k2, 2))
                        settle(gp)
                    for j in range(J):
                        gp.indirect_dma_start(er[:, k, j, 0:D], None, x, bass.IndirectOffsetOnAxis(gi[:, k, j:j + 1], 0)
                                              ).then_inc(tg_in[k], 16)
                        gp.indirect_dma_start(found[:, k2, j:j + 1], None, map_d,
                                              bass.IndirectOffsetOnAxis(gm[:, k, j:j + 1], 0)).then_inc(tg_in[k], 16)
            pipeline(gp, dst_step, DST_LAST, DST_NODES, nodes_until=DST_NODES_UNTIL)
            wait_all(gp, dst_end)
            gp.wait_ge(s_fo, 16)

            for l in range(LAYERS):
                for k in range(2):
                    gp.indirect_dma_start(fixrow[:, k, :], None, U[l], bass.IndirectOffsetOnAxis(fixidx[:, k:k + 1], 0)
                                          ).then_inc(s_fixg, 16)
                gp.wait_ge(s_fixw, 32 * (l + 1))

                def a_step(i, u, on, node, l=l):
                    if on(0):
                        t, k = i, u % 4
                        gp.wait_ge(ai_in[k], slot_count(in_slot(4, k, l), t, k, 4))
                        if not isinstance(t, int) or t >= 4:
                            gp.wait_ge(a_v[0], count(l * NT * 5, t - 4, 5))
                            gp.wait_ge(ah_out[k], slot_count(in_slot(4, k, l), t - 4, k, 4))
                            settle(gp)
                        for j in range(J):
                            gp.indirect_dma_start(er[:, k, j, 0:D], None, U[l],
                                                  bass.IndirectOffsetOnAxis(gi[:, k, j:j + 1], 0)).then_inc(ag_in[k], 16)
                pipeline(gp, a_step, A_LAST, A_NODES[l], A_EVERY, back=6)
                wait_all(gp, a_end(l))
                if l < LAYERS - 1:
                    wait_all(gp, b_end(l))

            def out_step(i, u, on, node):
                if on(7):
                    t, k = i - 7, (u - 7) % 4
                    k2 = (u - 7) % 2
                    gp.wait_ge(bi_in[k], slot_count(0, t, k, 4))
                    gp.wait_ge(e_o, count(NT, t))
                    settle(gp)
                    for j in range(J):
                        gp.indirect_dma_start(out, bass.IndirectOffsetOnAxis(gi[:, k, j:j + 1], 0), e1[:, k2, j, :],
                                              None, bounds_check=N_NODES - 1, oob_is_err=False).then_inc(s_fin[k2], 16)
            pipeline(gp, out_step, B_LAST)
            wait_all(gp, [(s_fin[k], in_slot(2, k, 1, 64)) for k in range(2)])

        @block.tensor
        def _(pe):
            pe.wait_ge(s_id, 5)
            pe.wait_ge(s_w, 160)
            pe.wait_ge(s_p0, 2)
            for l in range(LAYERS):
                nc.tensor.matmul(bank[l][:, 0:D + 1], wqT_s[:, l, :], wkT_s[:, l, :], start=True, stop=True)
                mm = nc.tensor.matmul(bank[3 + l][0:SPLIT, 0:D + 1], bq_wide[:, l * SPLIT:(l + 1) * SPLIT], wkT_s[:, l, :],
                                      start=True, stop=True)
            mm.then_inc(s_wt, 1)
            pe.wait_ge(s_p1, 1)
            for n in range(4):
                mm = nc.tensor.matmul(bank[6][0:1, n * HC:(n + 1) * HC], ccol[:, n:n + 1], ident[0:HC, 0:HC],
                                      start=True, stop=True)
            pe.wait_ge(s_wt, 2)
            for k in range(2):
                nc.tensor.transpose(bank[0][:, k * HC:(k + 1) * HC], vb[:, k, :], ident[0:HC, 0:HC])
                nc.tensor.transpose(bank[1][:, k * HC:(k + 1) * HC], vc[:, k, :], ident[0:HC, 0:HC])
                mm = nc.tensor.transpose(bank[2][:, k * HC:(k + 1) * HC], vd[:, k, :], ident[0:HC, 0:HC])
            mm.then_inc(s_wt, 1)
            pe.wait_ge(s_fixi, 1)
            over_chunks_pe(pe, 0, "back", va)
            wait_all(pe, prep_end)

            pipeline(pe, lambda i, u, on, node: node_pe(pe, *node, y_bank=7), MAP_LAST, MAP_NODES)
            wait_all(pe, map_end)

            def src_step(i, u, on, node):
                if on(0):
                    k = u % 4
                    pe.wait_ge(g_in[k], slot_count(0, i, k, 4, 64))
                    if on(6):
                        pe.wait_ge(s_a[4], count(0, i - 6))
                    elif on(1):
                        pe.wait_ge(s_a[0], count(0, i - 1))
                    for j in range(J):
                        mm = nc.tensor.transpose(bank[3][:, j * P:(j + 1) * P], er[:, k, j, 0:D], ident[:, :])
                    mm.then_inc(s_e[0], 1)
                node_pe(pe, *node)
                if on(1):
                    t, k = i - 1, (u - 1) % 2
                    pe.wait_ge(s_a[0], count(0, t))
                    pe.wait_ge(w_in[k], slot_count(0, t, k, 2, 48))
                    if on(6):
                        pe.wait_ge(s_a[5], count(0, i - 6))
                    elif on(2):
                        pe.wait_ge(s_a[1], count(0, i - 2))
                    for j in range(J):
                        c = slice(j * P, (j + 1) * P)
                        nc.tensor.matmul(bank[4][:, c], eT[:, k, c], w1a_s[:, :], start=True, stop=False)
                        mm = nc.tensor.matmul(bank[4][:, c], wt[:, k, c], w1b_s[:, :], start=False, stop=True)
                    mm.then_inc(s_e[1], 1)
                    if on(7):
                        pe.wait_ge(s_a[6], count(0, i - 7))
                    elif on(2):
                        pe.wait_ge(s_v[0], (i - 2) * 5 + 1)
                    for j in range(J):
                        c = slice(j * P, (j + 1) * P)
                        mm = nc.tensor.matmul(bank[5][:, c], eT[:, k, c], w2a_s[:, :], start=True, stop=True)
                    mm.then_inc(s_e[2], 1)
                if on(3):
                    t, k = i - 3, (u - 3) % 2
                    pe.wait_ge(s_v[0], (i - 2) * 5 + 4)
                    if on(4):
                        pe.wait_ge(s_a[2], count(0, t - 1))
                    for j in range(J):
                        mm = nc.tensor.transpose(bank[6][:, j * P:(j + 1) * P], e1[:, k, j, :], ident[:, :])
                    mm.then_inc(s_e[3], 1)
                if on(4):
                    t, k = i - 4, u % 2
                    pe.wait_ge(s_a[2], count(0, t))
                    if on(5):
                        pe.wait_ge(s_a[3], count(0, t - 1))
                    nc.tensor.matmul(bank[7][:, :], ws_s[:, 0, :], e1T[:, k, :], start=True, stop=True).then_inc(s_e[4], 1)
                if on(5):
                    t, k = i - 5, (u - 5) % 2
                    pe.wait_ge(s_a[3], count(0, t))
                    pe.wait_ge(s_a[0], count(0, min(i, NT - 1) if isinstance(i, int) else i))
                    if on(6) and not on(0):
                        pe.wait_ge(s_a[4], count(0, t - 1))
                    for j in range(J):
                        mm = nc.tensor.transpose(bank[3][:, j * P:(j + 1) * P], g1T[:, k, j * P:(j + 1) * P], ident[:, :])
                    mm.then_inc(s_e[5], 1)
                    pe.wait_ge(s_a[1], count(0, min(i - 1, NT - 1) if isinstance(i, int) else i - 1))
                    if on(6) and not on(1):
                        pe.wait_ge(s_a[5], count(0, t - 1))
                    nc.tensor.matmul(bank[4][:, :], ws_s[:, 1, :], g1T[:, k, :], start=True, stop=True).then_inc(s_e[6], 1)
                if on(6):
                    t, k = i - 6, u % 2
                    pe.wait_ge(s_a[5], count(0, t))
                    pe.wait_ge(s_v[0], (min(i - 1, NT - 1) if isinstance(i, int) else i - 1) * 5 + 1)
                    if on(7) and not on(1):
                        pe.wait_ge(s_a[6], count(0, t - 1))
                    for j in range(J):
                        mm = nc.tensor.transpose(bank[5][:, j * P:(j + 1) * P], g2T[:, k, j * P:(j + 1) * P], ident[:, :])
                    mm.then_inc(s_e[7], 1)
            pipeline(pe, src_step, SRC_LAST, SRC_NODES)
            wait_all(pe, src_end)

            def dst_step(i, u, on, node):
                if on(2):
                    t, k4 = i - 2, (u - 2) % 4
                    pe.wait_ge(tg_in[k4], slot_count(0, t, k4, 4, 128))
                    if on(3):
                        pe.wait_ge(t_a, count(0, t - 1))
                    for j in range(J):
                        mm = nc.tensor.transpose(bank[3][:, j * P:(j + 1) * P], er[:, k4, j, 0:D], ident[:, :])
                    mm.then_inc(t_e[0], 1)
                node_pe(pe, *node)
                if on(1):
                    t, k, k4 = i - 1, (u - 1) % 2, (u - 1) % 4
                    pe.wait_ge(rows_in[k4], slot_count(0, t, k4, 4))
                    pe.wait_ge(t_v[0], count(0, t))
                    if on(3):
                        pe.wait_ge(t_v[1], count(0, t - 2, 4))
                    for j in range(J):
                        mm = nc.tensor.matmul(bank[4 + 2 * k][:, j * P:(j + 1) * P], rr[:, k4, j, :], sel[:, k, j, :],
                                              start=True, stop=True)
                    mm.then_inc(t_e[1], 1)
                if on(3):
                    t, k = i - 3, (u - 3) % 2
                    pe.wait_ge(t_a, count(0, t))
                    pe.wait_ge(t_v[1], count(0, t, 4))
                    if on(4):
                        pe.wait_ge(t_v[2], (t - 1) * 5 + 1)
                    for j in range(J):
                        c = slice(j * P, (j + 1) * P)
                        nc.tensor.matmul(bank[5][:, c], eT[:, k, c], w2a_s[:, :], start=True, stop=False)
                        mm = nc.tensor.matmul(bank[5][:, c], g1T[:, k, c], w2b_s[:, :], start=False, stop=True)
                    mm.then_inc(t_e[2], 1)
            pipeline(pe, dst_step, DST_LAST, DST_NODES, nodes_until=DST_NODES_UNTIL)
            wait_all(pe, dst_end)

            for l in range(LAYERS):
                b0 = l * NT

                def a_step(i, u, on, node, l=l, b0=b0):
                    node_pe(pe, *node)
                    if on(1):
                        t, k, k4 = i - 1, (u - 1) % 2, (u - 1) % 4
                        pe.wait_ge(rows_in[k4], slot_count(in_slot(4, k4, 1 + 2 * l), t, k4, 4))
                        pe.wait_ge(a_v[1], count(b0, t))
                        if on(2):
                            pe.wait_ge(a_a, count(b0, t - 1))
                        for j in range(J):
                            mm = nc.tensor.matmul(bank[3][:, j * P:(j + 1) * P], rr[:, k4, j, :], sel[:, k, j, :],
                                                  start=True, stop=True)
                        mm.then_inc(a_e[0], 1)
                    if on(2):
                        t, k = i - 2, u % 2
                        pe.wait_ge(a_a, count(b0, t))
                        if on(3):
                            pe.wait_ge(a_v[0], count(b0 * 5, t - 1, 5) - 1)
                        for j in range(J):
                            ps = bank[4 + j // 2][:, 0:2 * (D + 1)].rearrange("p (j f) -> p j f", j=2)
                            if j % 2 == 0:
                                nc.tensor.matmul(ps, parts[:, :], bias_rows(l * (D + 1), D + 1, 2),
                                                 start=True, stop=False)
                            mm = nc.tensor.matmul(ps[:, j % 2, :], eT[:, k, j * P:(j + 1) * P], a_s[:, l, :],
                                                  start=False, stop=j % 2 == 1)
                        mm.then_inc(a_e[1], 1)
                        if on(3):
                            pe.wait_ge(a_k, count(b0, t - 1))
                        nc.tensor.matmul(chunk_rows(bank[6][:, :]), parts[:, :], bias_rows(SKIP_AT + l * D, D, J),
                                         start=True, stop=False)
                        for j in range(J):
                            mm = nc.tensor.matmul(bank[6][:, j * P:(j + 1) * P], eT[:, k, j * P:(j + 1) * P],
                                                  ws_s[:, l, :], start=False, stop=j == J - 1)
                        mm.then_inc(a_e[2], 1)
                pipeline(pe, a_step, A_LAST, A_NODES[l], A_EVERY, back=6)
                wait_all(pe, a_end(l))
                for k in range(2):
                    mm = nc.tensor.transpose(bank[0][0:HC, k * P:(k + 1) * P], logit_c[:, k * HC:(k + 1) * HC], ident[:, :])
                mm.then_inc(s_lt, 1)
                for n, (kind, o) in enumerate((("max", vb), ("back", vd), ("add", vb), ("back", vd))):
                    over_chunks_pe(pe, 1 + 4 * l + n, kind, o)
                pe.wait_ge(s_al, l + 1)
                for k in range(2):
                    mm = nc.tensor.transpose(bank[0][:, k * HC:(k + 1) * HC], va[:, k, :], ident[0:HC, 0:HC])
                mm.then_inc(s_at, 1)

                def b_step(i, u, on, node, l=l, b0=b0):
                    if on(1):
                        t, k, k4 = i - 1, (u - 1) % 2, (u - 1) % 4
                        pe.wait_ge(rows_in[k4], slot_count(in_slot(4, k4, 2 + 2 * l), t, k4, 4))
                        pe.wait_ge(b_v[0], count(b0, t))
                        if on(3):
                            pe.wait_ge(b_v[1], count(b0 * 4, t - 2, 4))
                        for j in range(J):
                            mm = nc.tensor.matmul(bank[k][:, j * P:(j + 1) * P], er[:, k4, j, 0:D], sel[:, k, j, :],
                                                  start=True, stop=True)
                        mm.then_inc(b_e[0], 1)
                    if on(3):
                        t, k, k4 = i - 3, (u - 3) % 2, (u - 3) % 4
                        tail = l == LAYERS - 1
                        before = in_slot(4, k4, l + (1 if tail else 0))
                        pe.wait_ge(skip_in[k4], slot_count(before, t, k4, 4))
                        pe.wait_ge(b_v[1], count(b0 * 4, t, 4))
                        if on(7):
                            if tail:
                                pe.wait_ge(e_o, count(NT, t - 4))
                            else:
                                pe.wait_ge(b_a, count(b0, t - 4))
                        nc.tensor.matmul(bank[2 + k4][:, :], ident[:, :], rr[:, k4].rearrange("p j f -> p (j f)"),
                                         start=True, stop=False)
                        for j in range(J):
                            mm = nc.tensor.matmul(bank[2 + k4][:, j * P:(j + 1) * P], g1T[:, k, j * P:(j + 1) * P],
                                                  wv_s[:, l, :], start=False, stop=j == J - 1)
                        mm.then_inc(b_e[1], 1)
                pipeline(pe, b_step, B_LAST)
                wait_all(pe, b_end(l))

        @block.scalar
        def _(act):
            def edge_out(k, y):
                for j in range(J):
                    op = nc.scalar.activation(e1[:, k, j, :], y[:, j, :], ACT.Identity,
                                              scale=eri[:, k, j:j + 1], bias=ebias[:, k, j:j + 1])
                op.then_inc(e_o, 1)

            act.wait_ge(s_parts, 1)
            for n in range(3):
                act.dma_start(attr_d[n * ATTRS:(n + 1) * ATTRS, :].rearrange("a (q n) -> (a q) n", q=P // ATTRS),
                              attr_parts[:, n, :]).then_inc(s_attr, 16)
            wait_all(act, prep_end)
            def map_step(i, u, on, node):
                node_x(act, *node)
                node_act(act, *node)
            pipeline(act, map_step, MAP_LAST, MAP_NODES)
            wait_all(act, map_end)

            def src_step(i, u, on, node):
                if on(0):
                    act.wait_ge(s_e[0], count(0, i))
                    if on(2):
                        act.wait_ge(s_e[2], count(0, i - 2))
                    nc.scalar.activation(eT[:, u % 2, :], bank[3][:, :], ACT.Copy).then_inc(s_a[0], 1)
                node_x(act, *node)
                node_act(act, *node)
                if on(2):
                    act.wait_ge(s_v[0], (i - 1) * 5)
                    root(emv[:, u % 2, :, 1], ers[:, :], e_sq)
                if on(1):
                    t, k = i - 1, (u - 1) % 2
                    act.wait_ge(s_e[1], count(0, t))
                    if on(3):
                        act.wait_ge(S_out[0][k], slot_count(0, t - 2, k, 2))
                    nc.scalar.activation(mrow[:, k], chunk_rows(bank[4][:, :]), ACT.Relu).then_inc(s_a[1], 1)
                if on(3):
                    t, k = i - 3, (u - 3) % 2
                    act.wait_ge(s_e[3], count(0, t))
                    if on(5):
                        act.wait_ge(s_e[4], count(0, t - 2))
                    nc.scalar.activation(e1T[:, k, :], bank[6][:, :], ACT.Copy).then_inc(s_a[2], 1)
                if on(4):
                    t, k = i - 4, u % 2
                    act.wait_ge(s_e[4], count(0, t))
                    if on(6):
                        act.wait_ge(s_e[6], count(0, t - 2))
                    nc.scalar.activation(g1T[:, k, :], bank[7][:, :], ACT.Relu, bias=bscol_s[:, 0:1]).then_inc(s_a[3], 1)
                if on(5):
                    t, k = i - 5, (u - 5) % 2
                    act.wait_ge(s_e[5], count(0, t))
                    if on(7):
                        act.wait_ge(S_out[2][k], slot_count(0, t - 2, k, 2))
                    nc.scalar.activation(r1[:, k], chunk_rows(bank[3][:, :]), ACT.Copy).then_inc(s_a[4], 1)
                    act.wait_ge(s_e[6], count(0, t))
                    if on(7):
                        act.wait_ge(s_e[7], count(0, t - 2))
                    nc.scalar.activation(g2T[:, k, :], bank[4][:, :], ACT.Relu, bias=bscol_s[:, 1:2]).then_inc(s_a[5], 1)
                if on(6):
                    t, k = i - 6, u % 2
                    act.wait_ge(s_e[7], count(0, t))
                    if on(8):
                        act.wait_ge(S_out[3][k], slot_count(0, t - 2, k, 2))
                    nc.scalar.activation(r2[:, k], chunk_rows(bank[5][:, :]), ACT.Copy).then_inc(s_a[6], 1)
            pipeline(act, src_step, SRC_LAST, SRC_NODES)
            wait_all(act, src_end)

            def dst_step(i, u, on, node):
                if on(2):
                    t, k = i - 2, u % 2
                    act.wait_ge(t_e[0], count(0, t))
                    if on(4):
                        act.wait_ge(t_e[2], count(0, t - 2))
                    nc.scalar.activation(eT[:, k, :], bank[3][:, :], ACT.Copy).then_inc(t_a, 1)
                node_x(act, *node)
                if on(5):
                    act.wait_ge(t_v[2], (i - 4) * 5)
                    root(emv[:, (u - 5) % 2, :, 1], ers[:, :], e_sq)
                node_act(act, *node)
                if on(6):
                    t, k = i - 6, u % 2
                    act.wait_ge(t_v[2], (i - 5) * 5 + 4)
                    if on(8):
                        act.wait_ge(t_out[k], slot_count(0, t - 2, k, 2))
                    edge_out(k, ey[:, (u - 6) % 4])
            pipeline(act, dst_step, DST_LAST, DST_NODES, nodes_until=DST_NODES_UNTIL)
            wait_all(act, dst_end)

            for l in range(LAYERS):
                b0 = l * NT

                def a_step(i, u, on, node, l=l, b0=b0):
                    node_x(act, *node)
                    node_act(act, *node)
                    if on(1):
                        t, k = i - 1, (u - 1) % 2
                        act.wait_ge(a_e[0], count(b0, t))
                        if on(3):
                            act.wait_ge(a_e[2], count(b0, t - 2))
                        nc.scalar.activation(eT[:, k, :], bank[3][:, :], ACT.Copy).then_inc(a_a, 1)
                    if l < LAYERS - 1 and on(2):
                        t, k = i - 2, u % 2
                        act.wait_ge(a_e[2], count(b0, t))
                        if on(4):
                            act.wait_ge(as_out[k], slot_count(in_slot(2, k, l), t - 2, k, 2))
                        nc.scalar.activation(mrow[:, k], chunk_rows(bank[6][:, :]), ACT.Copy).then_inc(a_k, 1)
                pipeline(act, a_step, A_LAST, A_NODES[l], A_EVERY, back=6)
                wait_all(act, a_end(l))
                act.wait_ge(s_arg, l + 1)
                nc.scalar.activation(va[:, :, :], va[:, :, :], ACT.Exp).then_inc(s_exp, 1)

                def b_step(i, u, on, node, l=l, b0=b0):
                    if on(4):
                        t, k = i - 4, u % 2
                        act.wait_ge(b_e[1], count(b0, t))
                        if on(6):
                            act.wait_ge(b_out[k], slot_count(in_slot(2, k, l), t - 2, k, 2))
                        nc.scalar.activation(e1[:, k], chunk_rows(bank[2 + u % 4][:, :]), ACT.Relu).then_inc(b_a, 1)
                if l < LAYERS - 1:
                    pipeline(act, b_step, B_LAST)
                    wait_all(act, b_end(l))

            def out_step(i, u, on, node):
                b0 = (LAYERS - 1) * NT
                if on(4):
                    t, k = i - 4, u % 4
                    if not isinstance(t, int) or t >= 4:
                        act.wait_ge(s_fin[k % 2], slot_count(0, t - 4, k % 2, 2, 64))
                        settle(act)
                    act.dma_start(gi[:, k, :], scat_d[bass.ds(t, 1)].rearrange("o p j -> p (o j)")).then_inc(bi_in[k], 16)
                if on(5):
                    act.wait_ge(b_v[2], (i - 4) * KT)
                    root(emv[:, (u - 5) % 2, :, 1], ers[:, :], e_sq)
                if on(6):
                    t, k = i - 6, u % 2
                    act.wait_ge(b_v[2], (i - 5) * KT + 3)
                    if on(8):
                        act.wait_ge(s_fin[k], slot_count(0, t - 2, k, 2, 64))
                    edge_out(k, chunk_rows(bank[2 + (u - 6) % 4][:, :]))
            pipeline(act, out_step, B_LAST)

        @block.vector
        def _(dve):
            steps = [1]

            def link(op):
                steps[0] += 1
                op.then_inc(s_vl, 1)
                dve.wait_ge(s_vl, steps[0])

            nc.vector.memset(eps_s[:, :], EPS)
            nc.vector.memset(minus[:, :], -1.0).then_inc(s_p0, 1)
            nc.vector.memset(parts[:, :], 0.0).then_inc(s_vl, 1)
            dve.wait_ge(s_vl, 1)
            for k in range(0, SPLIT, 32):
                nc.vector.memset(parts[k:k + 1, :], 1.0)
            dve.wait_ge(s_w, 160)
            dve.wait_ge(s_p0, 1)
            for l in range(LAYERS):
                op = nc.vector.tensor_scalar(bq_wide[:, l * SPLIT:(l + 1) * SPLIT], minus[:, 0:SPLIT], 0.0, bq_s[:, l:l + 1],
                                             ALU.mult, ALU.add)
            op.then_inc(s_p0, 1)
            dve.wait_ge(s_seg, 64)
            link(nc.vector.tensor_tensor(va[:, :, :], di[:, :, :], dp[:, :, :], ALU.not_equal))
            link(nc.vector.tensor_tensor(last[:, :, :], di[:, :, :], dn[:, :, :], ALU.not_equal))
            link(nc.vector.tensor_scalar(notstart[:, :, :], va[:, :, :], -1.0, 1.0, ALU.mult, ALU.add))
            link(nc.vector.tensor_scalar(notlast[:, :, :], last[:, :, :], -1.0, 1.0, ALU.mult, ALU.add))
            link(nc.vector.tensor_scalar(nb[:, :, :], va[:, :, :], -BIG, None, ALU.mult))
            for k in range(2):
                link(nc.vector.tensor_tensor_scan(vb[:, k, :], va[:, k, :], va[:, k, :], 0.0, ALU.add, ALU.max))
            link(nc.vector.tensor_copy(ordb[:, :, :], vb[:, :, :]))
            link(nc.vector.tensor_copy(vc[:, :, :], last[:, :, :]))
            link(nc.vector.memset(vc[:, :, P - 1:P], 1.0))
            link(nc.vector.scalar_tensor_tensor(vd[:, :, :], notlast[:, :, :], SKIP, di[:, :, :], ALU.mult, ALU.add))
            link(nc.vector.tensor_scalar(ccol[:, 0:2], vb[:, :, P - 1], 0.0, None, ALU.is_equal))
            link(nc.vector.reduce_max(ccol[:, 2:4], last[:, :, :], mybir.AxisListType.X))
            link(nc.vector.tensor_scalar(ccol[:, 2:4], ccol[:, 2:4], 0.0, None, ALU.is_equal))
            nc.vector.tensor_copy(va[:, :, :], last[:, :, :]).then_inc(s_p1, 1)
            dve.wait_ge(s_wt, 1)
            for l in range(LAYERS):
                nc.vector.tensor_copy(a_s[:, l, :], bank[l][:, 0:D + 1])
                op = nc.vector.tensor_copy(bias_raw[:, l * (D + 1):(l + 1) * (D + 1)], bank[3 + l][0:SPLIT, 0:D + 1])
            op.then_inc(s_wt, 1)
            dve.wait_ge(s_b, 32)
            link(nc.vector.tensor_copy(bias_raw[:, LAST_AT:], bias_raw[:, LAST_AT - D:LAST_AT]))
            link(nc.vector.tensor_tensor(bias_raw[:, SKIP_AT:LAST_AT], bias_raw[:, SKIP_AT:LAST_AT],
                                         bias_rest[:, 0:LAYERS * D], ALU.add))
            link(nc.vector.tensor_copy(biases[:, :], bias_raw))
            link(nc.vector.tensor_tensor(bias_rest, bias_raw, biases[:, :], ALU.subtract))
            nc.vector.tensor_copy(biases[32:64, :], bias_rest[32:64, :])
            link(nc.vector.tensor_copy(biases[64:96, :], bias_rest[64:96, :]))
            link(nc.vector.tensor_tensor(bias_raw[64:96, :], bias_rest[64:96, :], biases[64:96, :], ALU.subtract))
            link(nc.vector.tensor_copy(biases[64:96, :], bias_raw[64:96, :]))
            dve.wait_ge(s_wt, 3)
            link(nc.vector.tensor_copy(ordcol[:, :], bank[0][:, 0:NC]))
            link(nc.vector.tensor_copy(endcol[:, :], bank[1][:, 0:NC]))
            nc.vector.tensor_copy(idx_all[:, :], bank[2][:, 0:NC]).then_inc(s_p2, 1)
            link(nc.vector.tensor_copy(nostart_row[:, :], bank[6][0:1, 0:NC]))
            link(nc.vector.tensor_copy(nolast_row[:, :], bank[6][0:1, NC:2 * NC]))
            link(nc.vector.tensor_scalar(nb_row[:, :], nostart_row[:, :], -1.0, BIG, ALU.add, ALU.mult))
            dve.wait_ge(s_iota, 1)
            link(nc.vector.tensor_copy(vd[:, :, :], slot_i[:, :, :]))
            nc.vector.tensor_tensor(vc[:, :, :], vd[:, :, :], last[:, :, :], ALU.mult).then_inc(s_fixi, 1)
            dve.wait_ge(s_fixi, 1)
            over_chunks_dve(dve, 0, "back", notlast, vc, va)
            link(nc.vector.tensor_copy(fixidx[:, :], va[:, :, P - 1]))
            dve.wait_ge(s_attr, 32)
            link(nc.vector.tensor_copy(attr_parts[:, 0], attr_raw))
            link(nc.vector.tensor_tensor(attr_rest, attr_raw, attr_parts[:, 0], ALU.subtract))
            link(nc.vector.tensor_copy(attr_parts[:, 1], attr_rest))
            link(nc.vector.tensor_tensor(attr_raw, attr_rest, attr_parts[:, 1], ALU.subtract))
            nc.vector.tensor_copy(attr_parts[:, 2], attr_raw).then_inc(s_parts, 1)
            link(nc.vector.tensor_copy(w1b_s[:, :], w1b_rows))
            link(nc.vector.tensor_scalar(w1b_part, w1b_s[:, :], which[:, 0:1], None, ALU.mult))
            for n in (1, 2):
                link(nc.vector.tensor_tensor(w1b_rest, w1b_rows, w1b_s[:, :], ALU.subtract))
                link(nc.vector.tensor_copy(w1b_rows, w1b_rest))
                link(nc.vector.tensor_copy(w1b_s[:, :], w1b_rows))
                link(nc.vector.scalar_tensor_tensor(w1b_part, w1b_s[:, :], which[:, n:n + 1], w1b_part, ALU.mult, ALU.add))
            link(nc.vector.tensor_copy(w1b_s[:, :], w1b_part))
            wait_all(dve, prep_end)

            def map_step(i, u, on, node):
                node_zy(dve, *node, y_bank=7)
                for part in (node_inv, node_sums, node_norm, node_means):
                    part(dve, *node)
            pipeline(dve, map_step, MAP_LAST, MAP_NODES)
            wait_all(dve, map_end)

            def src_step(i, u, on, node):
                chain, at = s_v[0], (i - 1) * 5
                node_zy(dve, *node)
                if on(1):
                    after(dve, chain, at - 1)
                    dve.wait_ge(s_e[2], count(0, i - 1))
                    nc.vector.scalar_tensor_tensor(ey[:, (u - 1) % 2], chunk_rows(bank[5][:, :]), 0.0,
                                                   er[:, (u - 1) % 4, :, 0:D], ALU.max, ALU.add).then_inc(chain, 1)
                elif on(2):
                    passed(dve, chain, at)
                node_inv(dve, *node)
                edge_inv(dve, 1, 1, i, u, on, chain, at, 0)
                node_sums(dve, *node)
                edge_sums(dve, 1, 1, i, u, on, chain, at, ey[:, (u - 1) % 2])
                node_norm(dve, *node)
                if on(2):
                    t, k = i - 2, u % 2
                    dve.wait_ge(chain, at + 2)
                    if on(4):
                        dve.wait_ge(S_out[1][k], slot_count(0, t - 2, k, 2))
                        dve.wait_ge(s_e[3], count(0, t - 2))
                    for j in range(J):
                        op = nc.vector.tensor_scalar(e1[:, k, j, :], ey[:, k, j, :], emv[:, k, j, 0:1], eri[:, k, j:j + 1],
                                                     ALU.subtract, ALU.mult)
                    op.then_inc(chain, 1)
                elif on(1):
                    passed(dve, chain, at + 3)
                node_means(dve, *node)
                edge_means(dve, 1, 1, i, u, on, chain, at)
            pipeline(dve, src_step, SRC_LAST, SRC_NODES)
            wait_all(dve, src_end)

            def dst_step(i, u, on, node):
                chain, at = t_v[2], (i - 4) * 5

                def add_carry(j):
                    if on(2):
                        carry(dve, i - 2, u % 2, j, bank[4 + 2 * (u % 2)], t_v[1], (i - 2) * 4)
                if on(0):
                    if on(2):
                        dve.wait_ge(t_e[1], count(0, i - 2))
                    select(i, u % 2, None, t_v[0])
                elif on(2):
                    dve.wait_ge(t_e[1], count(0, i - 2))
                if on(4):
                    dve.wait_ge(t_e[2], count(0, i - 4))
                add_carry(0)
                node_zy(dve, *node)
                add_carry(1)
                if on(4):
                    after(dve, chain, at - 1)
                    nc.vector.scalar_tensor_tensor(ey[:, u % 4], chunk_rows(bank[5][:, :]), 0.0, er[:, (u - 4) % 4, :, 0:D],
                                                   ALU.max, ALU.add).then_inc(chain, 1)
                elif on(5):
                    passed(dve, chain, at)
                node_inv(dve, *node)
                if on(7):
                    dve.wait_ge(e_o, count(0, i - 7))
                edge_inv(dve, 4, 1, i, u, on, chain, at, NT)
                add_carry(2)
                node_sums(dve, *node)
                edge_sums(dve, 4, 1, i, u, on, chain, at, ey[:, u % 4])
                add_carry(3)
                node_norm(dve, *node)
                edge_minus_mean(dve, 4, 1, i, u, on, chain, at)
                node_means(dve, *node)
                edge_means(dve, 4, 1, i, u, on, chain, at)
            pipeline(dve, dst_step, DST_LAST, DST_NODES, nodes_until=DST_NODES_UNTIL)
            wait_all(dve, dst_end)
            dve.wait_ge(s_fd, 16)
            nc.vector.tensor_scalar(alpha_c[:, :], slot_all[:, :], float(NS + 1), None, ALU.add).then_inc(s_fc, 1)
            dve.wait_ge(s_fc, 1)
            nc.vector.scalar_tensor_tensor(alpha_c[:, :], logit_c[:, :], 0.0, alpha_c[:, :], ALU.is_lt, ALU.mult).then_inc(s_fc, 1)
            dve.wait_ge(s_fc, 2)
            nc.vector.tensor_tensor(idx_all[:, :], alpha_c[:, :], logit_c[:, :], ALU.add).then_inc(s_fc, 1)
            dve.wait_ge(s_fc, 3)

            for l in range(LAYERS):
                b0 = l * NT

                def a_step(i, u, on, node, l=l, b0=b0):
                    node_zy(dve, *node)
                    if on(3):
                        t, k, k4 = i - 3, (u - 3) % 2, (u - 3) % 4
                        at = t * 5 + b0 * 5
                        dve.wait_ge(ag_in[k4], slot_count(in_slot(4, k4, l, 64), t, k4, 4, 64))
                        dve.wait_ge(a_e[1], count(b0, t))
                        after(dve, a_v[0], at)
                        for j in range(J):
                            nc.vector.tensor_tensor_reduce(
                                out=junk[:, j, :], in0=bank[4 + j // 2][:, (j % 2) * (D + 1):(j % 2 + 1) * (D + 1)],
                                in1=er[:, k4, j, :], scale=float(D) ** -0.5, scalar=0.0, op0=ALU.mult, op1=ALU.add,
                                accum_out=lg[:, k, j:j + 1]).then_inc(a_v[0], 1)
                    node_inv(dve, *node)
                    if on(0):
                        if on(2):
                            dve.wait_ge(a_e[0], count(b0, i - 2))
                        select(i, u % 2, endcol, a_v[1])
                    if on(3):
                        dve.wait_ge(a_v[0], at + 4)
                        nc.vector.tensor_copy(logit_c[:, bass.ds(t * J, J)], lg[:, k, :]).then_inc(a_v[0], 1)
                    node_sums(dve, *node)
                    node_norm(dve, *node)
                    node_means(dve, *node)
                    if l == LAYERS - 1 and on(3):
                        dve.wait_ge(a_e[2], count(b0, t))
                        dve.wait_ge(skip_in[k4], slot_count(in_slot(4, k4, LAYERS - 1), t, k4, 4))
                        if on(5):
                            dve.wait_ge(as_out[k], slot_count(in_slot(2, k, l), t - 2, k, 2))
                        nc.vector.tensor_tensor(mrow[:, k], chunk_rows(bank[6][:, :]), ey[:, k4], ALU.add).then_inc(a_k, 1)
                pipeline(dve, a_step, A_LAST, A_NODES[l], A_EVERY, back=6)
                wait_all(dve, a_end(l))
                dve.wait_ge(s_lt, l + 1)
                q = 1 + 4 * l
                link(nc.vector.tensor_copy(va[:, :, :], bank[0][0:HC, 0:2 * P].rearrange("c (k e) -> c k e", k=2)))
                over_chunks_dve(dve, q, "max", nb, va, vb)
                link(nc.vector.tensor_tensor(vc[:, :, :], vb[:, :, :], last[:, :, :], ALU.mult))
                over_chunks_dve(dve, q + 1, "back", notlast, vc, vd)
                nc.vector.tensor_tensor(va[:, :, :], va[:, :, :], vd[:, :, :], ALU.subtract).then_inc(s_arg, 1)
                dve.wait_ge(s_exp, l + 1)
                over_chunks_dve(dve, q + 2, "add", notstart, va, vb)
                link(nc.vector.tensor_tensor(vc[:, :, :], vb[:, :, :], last[:, :, :], ALU.mult))
                over_chunks_dve(dve, q + 3, "back", notlast, vc, vd)
                link(nc.vector.tensor_scalar(vd[:, :, :], vd[:, :, :], 1e-16, None, ALU.max))
                link(nc.vector.reciprocal(vc[:, :, :], vd[:, :, :]))
                nc.vector.tensor_tensor(va[:, :, :], va[:, :, :], vc[:, :, :], ALU.mult).then_inc(s_al, 1)
                dve.wait_ge(s_at, l + 1)
                link(nc.vector.tensor_copy(alpha_c[:, :], bank[0][:, 0:NC]))

                def b_step(i, u, on, node, l=l, b0=b0):
                    tail = l == LAYERS - 1
                    chain, at = b_v[2], (i - 4) * KT

                    def add_carry(j):
                        if on(2):
                            carry(dve, i - 2, u % 2, j, bank[u % 2], b_v[1], (i - 2) * 4 + b0 * 4)
                    if on(2):
                        dve.wait_ge(b_e[0], count(b0, i - 2))
                    if on(4):
                        dve.wait_ge(b_e[1], count(b0, i - 4))
                    for j in range(J):
                        if on(0):
                            select(i, u % 2, alpha_c, b_v[0], [j])
                        add_carry(j)
                    if tail:
                        if on(7):
                            dve.wait_ge(e_o, count(NT, i - 7))
                        edge_inv(dve, 4, 0, i, u, on, chain, at, 2 * NT)
                        edge_sums(dve, 4, 0, i, u, on, chain, at, chunk_rows(bank[2 + u % 4][:, :]))
                        edge_minus_mean(dve, 4, 0, i, u, on, chain, at)
                        edge_means(dve, 4, 0, i, u, on, chain, at)
                pipeline(dve, b_step, B_LAST)
                wait_all(dve, b_end(l))


def kernel(**inputs):
    import numpy as _np
    import concourse.bacc as _bacc
    from concourse import mybir as _mybir
    from concourse.bass_utils import run_bass_kernel_spmd as _run

    get = {k: _np.ascontiguousarray(v) for k, v in inputs.items()}
    pad = NS - N_EDGES

    def tiles(v):
        return _np.ascontiguousarray(v.reshape(NT, J, P).transpose(0, 2, 1))

    src, dst = get["src"], get["dst"]
    fill = _np.zeros(pad, _np.int32)
    arrays = {
        "x": get["x"],
        "xsrc_idx": tiles(_np.concatenate([src, fill])),
        "xdst_idx": tiles(_np.concatenate([dst, fill])),
        "slot_ids": tiles(_np.arange(NS, dtype=_np.float32)),
        "dst_pad": _np.concatenate([_np.full(1, -1, _np.int32), dst, _np.full(pad, N_NODES, _np.int32),
                                    _np.full(1, -2, _np.int32)]),
        "wT": _np.concatenate([_np.concatenate([get["edge_attr_3"].T, _np.ones((1, N_EDGES), _np.float32)]),
                               _np.zeros((4, pad), _np.float32)], axis=1),
        "w1a": get["L0_gnn_W1"][:, :D].T,
        "w1b": _np.tile(_np.concatenate([get["L0_gnn_W1"][:, D:].T, get["L0_gnn_b1"][None, :]]), (9, 1)),
        "which_part": _np.repeat(_np.eye(3, dtype=_np.float32), 3 * ATTRS, axis=0),
        "w2a": get["L0_gnn_W2"][:, :D].T,
        "w2b": get["L0_gnn_W2"][:, D:].T,
        "wqT": get["L1_gnn_Wq"].transpose(2, 0, 1),
        "wkT": _np.concatenate([get["L1_gnn_Wk"].transpose(2, 0, 1), get["L1_gnn_bk"].T[:, :, None]], axis=2),
        "bq": get["L1_gnn_bq"].T,
        "wv": get["L1_gnn_Wv"].transpose(1, 0, 2),
        "bv": get["L1_gnn_bv"],
        "ws": get["L1_gnn_Ws"].transpose(1, 0, 2),
        "bs": get["L1_gnn_bs"],
        "bs_col": get["L1_gnn_bs"].T,
    }
    nc = _bacc.Bacc("TRN2", target_bir_lowering=False, num_devices=1)
    given, args = {}, {}
    for name, a in arrays.items():
        a = _np.ascontiguousarray(a)
        given[f"in_{name}"] = a
        args[name] = nc.dram_tensor(f"in_{name}", a.shape, _mybir.dt.from_np(a.dtype), kind="ExternalInput").ap()
    args["out"] = nc.dram_tensor("out_rows", (N_NODES, D), _mybir.dt.float32, kind="ExternalOutput").ap()
    gnn_program(nc, **args)
    return _run(nc, [given], core_ids=[0]).results[0]["out_rows"]
```
